# Optimizing a Trainium2 kernel written in Bass

```python
import numpy as np
import jax
import jax.numpy as jnp

def _softmax(x, axis=-1):
    return jax.nn.softmax(x, axis=axis)

def _gelu(x):
    return jax.nn.gelu(x, approximate=True)

def _silu(x):
    return jax.nn.silu(x)

def _sigmoid(x):
    return jax.nn.sigmoid(x)

def _layernorm(x, axis=-1, eps=1e-05):
    m = jnp.mean(x, axis=axis, keepdims=True)
    v = jnp.var(x, axis=axis, keepdims=True)
    return (x - m) / jnp.sqrt(v + eps)

def _scatter_add(tgt, idx, src, axis=0):
    return tgt.at[idx].add(src)

def _segment_sum(src, seg, n):
    return jax.ops.segment_sum(src, seg, n)
kernel_name = 'mk_seq_preln_d2_jaxref_r8_7f65f9'

def setup_inputs(seed: int=0):
    np.random.seed(seed)
    _w = jnp.asarray

    def _L0_attn_setup():
        import jax, jax.numpy as jnp
        import numpy as np
        from jax import lax
        D_MODEL = 128
        B, T = (4, 256)
        LN_EPS = 1e-05

        def _ln(x, w, b):
            mu = jnp.mean(x, axis=-1, keepdims=True)
            var = jnp.mean((x - mu) ** 2, axis=-1, keepdims=True)
            return (x - mu) * lax.rsqrt(var + LN_EPS) * w + b

        def _wkv(u, k, v):
            Bb, Tt, C = k.shape

            def step(carry, kv):
                aa, bb = carry
                kk, vv = kv
                p = jnp.maximum(bb, u + kk)
                e1 = jnp.exp(bb - p)
                e2 = jnp.exp(u + kk - p)
                out = (e1 * aa + e2 * vv) / (e1 + e2)
                p2 = jnp.maximum(bb, kk)
                e1b = jnp.exp(bb - p2)
                e2b = jnp.exp(kk - p2)
                return ((e1b * aa + e2b * vv, p2 + jnp.log(e1b + e2b)), out)
            init = (jnp.zeros((Bb, C), k.dtype), jnp.zeros((Bb, C), k.dtype))
            _, outs = lax.scan(step, init, (jnp.swapaxes(k, 0, 1), jnp.swapaxes(v, 0, 1)))
            return jnp.swapaxes(outs, 0, 1)
        key = jax.random.key(seed)
        ks = jax.random.split(key, 12)
        C = D_MODEL
        s = 0.02
        return {'x': jax.random.normal(ks[0], (B, T, C), jnp.float32), 'time_decay': jax.random.normal(ks[1], (C,), jnp.float32), 'time_first': jax.random.normal(ks[2], (C,), jnp.float32) * 0.5, 'time_shift': jax.random.normal(ks[3], (1, 1, C), jnp.float32) * 0.1, 'Wk': jax.random.normal(ks[4], (C, C), jnp.float32) * s, 'Wv': jax.random.normal(ks[5], (C, C), jnp.float32) * s, 'Wr': jax.random.normal(ks[6], (C, C), jnp.float32) * s, 'Wck': jax.random.normal(ks[7], (4 * C, C), jnp.float32) * s, 'Wcv': jax.random.normal(ks[8], (C, 4 * C), jnp.float32) * s, 'Wcr': jax.random.normal(ks[9], (C, C), jnp.float32) * s, 'ln1_w': jnp.ones((C,), jnp.float32), 'ln1_b': jnp.zeros((C,), jnp.float32), 'ln2_w': jnp.ones((C,), jnp.float32), 'ln2_b': jnp.zeros((C,), jnp.float32)}
    _L0_attn_in = _L0_attn_setup()

    def _L0_ffn_setup():
        import jax, jax.numpy as jnp
        import numpy as np
        E = 8
        TOP_K = 2
        ROUTE_SCALE = 1.0
        ALPHA = 1.702
        LIMIT = 7.0
        D = 128
        F = 128
        B, S = (2, 128)

        def swiglu(h):
            g = jnp.minimum(h[..., ::2], LIMIT)
            l = jnp.clip(h[..., 1::2], -LIMIT, LIMIT)
            return g * jax.nn.sigmoid(ALPHA * g) * (l + 1.0)
        if __name__ == '__main__':
            out = reference(**setup_inputs())
            print(out.shape, out.dtype)
        key = jax.random.key(seed)
        ks = jax.random.split(key, 16)
        sd = 1.0 / np.sqrt(D)
        sf = 1.0 / np.sqrt(F)
        return {'x': jax.random.normal(ks[0], (B, S, D), jnp.float32), 'gate_w': jax.random.normal(ks[1], (E, D), jnp.float32) * sd, 'gate_b': jax.random.normal(ks[2], (E,), jnp.float32) * 0.01, 'w1': jax.random.normal(ks[3], (E, 2 * F, D), jnp.float32) * sd, 'b1': jax.random.normal(ks[4], (E, 2 * F), jnp.float32) * 0.01, 'w3': jax.random.normal(ks[5], (E, 2 * F, D), jnp.float32) * sd, 'b3': jax.random.normal(ks[6], (E, 2 * F), jnp.float32) * 0.01, 'w2': jax.random.normal(ks[7], (E, D, F), jnp.float32) * sf, 'b2': jax.random.normal(ks[8], (E, D), jnp.float32) * 0.01, 'sw1': jax.random.normal(ks[9], (2 * F, D), jnp.float32) * sd, 'sb1': jax.random.normal(ks[10], (2 * F,), jnp.float32) * 0.01, 'sw3': jax.random.normal(ks[11], (2 * F, D), jnp.float32) * sd, 'sb3': jax.random.normal(ks[12], (2 * F,), jnp.float32) * 0.01, 'sw2': jax.random.normal(ks[13], (D, F), jnp.float32) * sf, 'sb2': jax.random.normal(ks[14], (D,), jnp.float32) * 0.01}
    _L0_ffn_in = _L0_ffn_setup()

    def _L1_attn_setup():
        import math
        import jax, jax.numpy as jnp
        import numpy as np
        DIM, NHEAD, TOPK = (128, 16, 64)
        DK = DIM // NHEAD
        HIDDEN = int(DIM * 8.0)
        EPS = 1e-05

        def _layernorm(x, g, b):
            mu = jnp.mean(x, axis=-1, keepdims=True)
            var = jnp.var(x, axis=-1, keepdims=True)
            return (x - mu) * jax.lax.rsqrt(var + EPS) * g + b

        def _adaptive_sparse_attn(xn, w_qkv, alpha_head, w_out):
            B, T, C = xn.shape
            qkv = xn @ w_qkv
            q, k, v = jnp.split(qkv, 3, axis=-1)

            def heads(t):
                return t.reshape(B, T, NHEAD, DK).transpose(0, 2, 1, 3)
            q, k, v = (heads(q), heads(k), heads(v))
            attn = jnp.einsum('bhqd,bhkd->bhqk', q, k) / math.sqrt(DK)
            dense = jnp.einsum('bhqk,bhkd->bhqd', jax.nn.softmax(attn, axis=-1), v)
            _, idx = jax.lax.top_k(attn, TOPK)
            M = B * NHEAD * T
            keep = jnp.zeros((M, T), bool).at[jnp.arange(M)[:, None], idx.reshape(M, TOPK)].set(True)
            keep = keep.reshape(B, NHEAD, T, T)
            attn_sp = jnp.where(keep, attn, jnp.float32(-1000000000.0))
            sparse = jnp.einsum('bhqk,bhkd->bhqd', jax.nn.softmax(attn_sp, axis=-1), v)
            gate = jax.nn.sigmoid(alpha_head)[None, :, None, None]
            out = gate * dense + (1.0 - gate) * sparse
            out = out.transpose(0, 2, 1, 3).reshape(B, T, C)
            return out @ w_out
        key = jax.random.key(seed)
        ks = jax.random.split(key, 12)
        B, T = (2, 256)
        s = 0.02
        return {'x': jax.random.normal(ks[0], (B, T, DIM), jnp.float32), 'ln1_g': jnp.ones((DIM,), jnp.float32), 'ln1_b': jnp.zeros((DIM,), jnp.float32), 'w_qkv': jax.random.normal(ks[1], (DIM, 3 * DIM), jnp.float32) * s, 'alpha_head': jnp.zeros((NHEAD,), jnp.float32), 'w_out': jax.random.normal(ks[2], (DIM, DIM), jnp.float32) * s, 'ln2_g': jnp.ones((DIM,), jnp.float32), 'ln2_b': jnp.zeros((DIM,), jnp.float32), 'w1': jax.random.normal(ks[3], (DIM, HIDDEN), jnp.float32) * s, 'b1': jnp.zeros((HIDDEN,), jnp.float32), 'w2': jax.random.normal(ks[4], (HIDDEN, DIM), jnp.float32) * s, 'b2': jnp.zeros((DIM,), jnp.float32), 'alpha': jnp.float32(0.5)}
    _L1_attn_in = _L1_attn_setup()

    def _L1_ffn_setup():
        import jax, jax.numpy as jnp
        import numpy as np
        DIM = 128
        EXPERT_DIM = 64
        N_EXPERTS = 16
        TOPK = 2
        SHARED_HIDDEN = EXPERT_DIM * TOPK
        B, T = (4, 128)

        def _moe_forward(x, router_w, router_bias, up_proj, gate_proj, down_proj, sh_gate, sh_up, sh_down):
            Bb, Tt, D = x.shape
            flat = x.reshape(Bb * Tt, D)
            N = flat.shape[0]
            logits = flat @ router_w.T
            topk_scores, topk_idx = jax.lax.top_k(logits + router_bias, TOPK)
            topk_scores = jax.nn.softmax(topk_scores, axis=-1)
            combine = jnp.zeros((N, N_EXPERTS), flat.dtype)
            combine = combine.at[jnp.arange(N)[:, None], topk_idx].add(topk_scores)
            up_all = jnp.einsum('nd,kde->nke', flat, up_proj)
            gate_all = jnp.einsum('nd,kde->nke', flat, gate_proj)
            hidden = jax.nn.silu(gate_all) * up_all
            down_all = jnp.einsum('nke,ked->nkd', hidden, down_proj)
            out = jnp.einsum('nk,nkd->nd', combine, down_all)
            sh_hidden = jax.nn.silu(flat @ sh_gate.T) * (flat @ sh_up.T)
            out = out + sh_hidden @ sh_down.T
            return out.reshape(Bb, Tt, D)
        key = jax.random.key(seed)
        ks = jax.random.split(key, 9)
        std = 0.02
        return {'x': jax.random.normal(ks[0], (B, T, DIM), jnp.float32), 'router_w': jax.random.normal(ks[1], (N_EXPERTS, DIM), jnp.float32) * std, 'router_bias': jnp.zeros((N_EXPERTS,), jnp.float32), 'up_proj': jax.random.normal(ks[2], (N_EXPERTS, DIM, EXPERT_DIM), jnp.float32) * std, 'gate_proj': jax.random.normal(ks[3], (N_EXPERTS, DIM, EXPERT_DIM), jnp.float32) * std, 'down_proj': jax.random.normal(ks[4], (N_EXPERTS, EXPERT_DIM, DIM), jnp.float32) * std, 'sh_gate': jax.random.normal(ks[5], (SHARED_HIDDEN, DIM), jnp.float32) * std, 'sh_up': jax.random.normal(ks[6], (SHARED_HIDDEN, DIM), jnp.float32) * std, 'sh_down': jax.random.normal(ks[7], (DIM, SHARED_HIDDEN), jnp.float32) * std}
    _L1_ffn_in = _L1_ffn_setup()
    _d = {'L0_attn_x': _L0_attn_in['x'], 'L0_attn_time_decay': _L0_attn_in['time_decay'], 'L0_attn_time_first': _L0_attn_in['time_first'], 'L0_attn_time_shift': _L0_attn_in['time_shift'], 'L0_attn_Wk': _L0_attn_in['Wk'], 'L0_attn_Wv': _L0_attn_in['Wv'], 'L0_attn_Wr': _L0_attn_in['Wr'], 'L0_attn_Wck': _L0_attn_in['Wck'], 'L0_attn_Wcv': _L0_attn_in['Wcv'], 'L0_attn_Wcr': _L0_attn_in['Wcr'], 'L0_attn_ln1_w': _L0_attn_in['ln1_w'], 'L0_attn_ln1_b': _L0_attn_in['ln1_b'], 'L0_attn_ln2_w': _L0_attn_in['ln2_w'], 'L0_attn_ln2_b': _L0_attn_in['ln2_b'], 'L0_ffn_gate_w': _L0_ffn_in['gate_w'], 'L0_ffn_gate_b': _L0_ffn_in['gate_b'], 'L0_ffn_w1': _L0_ffn_in['w1'], 'L0_ffn_b1': _L0_ffn_in['b1'], 'L0_ffn_w3': _L0_ffn_in['w3'], 'L0_ffn_b3': _L0_ffn_in['b3'], 'L0_ffn_w2': _L0_ffn_in['w2'], 'L0_ffn_b2': _L0_ffn_in['b2'], 'L0_ffn_sw1': _L0_ffn_in['sw1'], 'L0_ffn_sb1': _L0_ffn_in['sb1'], 'L0_ffn_sw3': _L0_ffn_in['sw3'], 'L0_ffn_sb3': _L0_ffn_in['sb3'], 'L0_ffn_sw2': _L0_ffn_in['sw2'], 'L0_ffn_sb2': _L0_ffn_in['sb2'], 'L1_attn_ln1_g': _L1_attn_in['ln1_g'], 'L1_attn_ln1_b': _L1_attn_in['ln1_b'], 'L1_attn_w_qkv': _L1_attn_in['w_qkv'], 'L1_attn_alpha_head': _L1_attn_in['alpha_head'], 'L1_attn_w_out': _L1_attn_in['w_out'], 'L1_attn_ln2_g': _L1_attn_in['ln2_g'], 'L1_attn_ln2_b': _L1_attn_in['ln2_b'], 'L1_attn_w1': _L1_attn_in['w1'], 'L1_attn_b1': _L1_attn_in['b1'], 'L1_attn_w2': _L1_attn_in['w2'], 'L1_attn_b2': _L1_attn_in['b2'], 'L1_attn_alpha': _L1_attn_in['alpha'], 'L1_ffn_router_w': _L1_ffn_in['router_w'], 'L1_ffn_router_bias': _L1_ffn_in['router_bias'], 'L1_ffn_up_proj': _L1_ffn_in['up_proj'], 'L1_ffn_gate_proj': _L1_ffn_in['gate_proj'], 'L1_ffn_down_proj': _L1_ffn_in['down_proj'], 'L1_ffn_sh_gate': _L1_ffn_in['sh_gate'], 'L1_ffn_sh_up': _L1_ffn_in['sh_up'], 'L1_ffn_sh_down': _L1_ffn_in['sh_down']}
    _x0 = _d['L0_attn_x']
    _d['L0_attn_x'] = jax.random.normal(jax.random.fold_in(jax.random.key(seed), 1), (4, 512, 128), dtype=_x0.dtype)
    del _x0
    return _d

def reference(L0_attn_x, L0_attn_time_decay, L0_attn_time_first, L0_attn_time_shift, L0_attn_Wk, L0_attn_Wv, L0_attn_Wr, L0_attn_Wck, L0_attn_Wcv, L0_attn_Wcr, L0_attn_ln1_w, L0_attn_ln1_b, L0_attn_ln2_w, L0_attn_ln2_b, L0_ffn_gate_w, L0_ffn_gate_b, L0_ffn_w1, L0_ffn_b1, L0_ffn_w3, L0_ffn_b3, L0_ffn_w2, L0_ffn_b2, L0_ffn_sw1, L0_ffn_sb1, L0_ffn_sw3, L0_ffn_sb3, L0_ffn_sw2, L0_ffn_sb2, L1_attn_ln1_g, L1_attn_ln1_b, L1_attn_w_qkv, L1_attn_alpha_head, L1_attn_w_out, L1_attn_ln2_g, L1_attn_ln2_b, L1_attn_w1, L1_attn_b1, L1_attn_w2, L1_attn_b2, L1_attn_alpha, L1_ffn_router_w, L1_ffn_router_bias, L1_ffn_up_proj, L1_ffn_gate_proj, L1_ffn_down_proj, L1_ffn_sh_gate, L1_ffn_sh_up, L1_ffn_sh_down):

    def _L0_attn_ref(x, time_decay, time_first, time_shift, Wk, Wv, Wr, Wck, Wcv, Wcr, ln1_w, ln1_b, ln2_w, ln2_b):
        import jax, jax.numpy as jnp
        import numpy as np
        from jax import lax
        D_MODEL = 128
        B, T = (4, 256)
        LN_EPS = 1e-05

        def _ln(x, w, b):
            mu = jnp.mean(x, axis=-1, keepdims=True)
            var = jnp.mean((x - mu) ** 2, axis=-1, keepdims=True)
            return (x - mu) * lax.rsqrt(var + LN_EPS) * w + b

        def _wkv(u, k, v):
            Bb, Tt, C = k.shape

            def step(carry, kv):
                aa, bb = carry
                kk, vv = kv
                p = jnp.maximum(bb, u + kk)
                e1 = jnp.exp(bb - p)
                e2 = jnp.exp(u + kk - p)
                out = (e1 * aa + e2 * vv) / (e1 + e2)
                p2 = jnp.maximum(bb, kk)
                e1b = jnp.exp(bb - p2)
                e2b = jnp.exp(kk - p2)
                return ((e1b * aa + e2b * vv, p2 + jnp.log(e1b + e2b)), out)
            init = (jnp.zeros((Bb, C), k.dtype), jnp.zeros((Bb, C), k.dtype))
            _, outs = lax.scan(step, init, (jnp.swapaxes(k, 0, 1), jnp.swapaxes(v, 0, 1)))
            return jnp.swapaxes(outs, 0, 1)
        Bb, Tt, C = x.shape
        ts = time_shift
        h = _ln(x, ln1_w, ln1_b)
        x_shifted = jnp.concatenate([jnp.broadcast_to(ts, (Bb, 1, C)), h[:, :-1, :]], axis=1)
        xxx = h + (h - x_shifted) * ts
        k = jnp.einsum('btc,oc->bto', xxx, Wk)
        v = jnp.einsum('btc,oc->bto', xxx, Wv)
        r = jax.nn.sigmoid(jnp.einsum('btc,oc->bto', xxx, Wr))
        wkv = _wkv(time_first, k, v)
        x = x + r * wkv
        h2 = _ln(x, ln2_w, ln2_b)
        xx2 = jnp.concatenate([h2[:, -1:, :], h2[:, :-1, :]], axis=1)
        xxx2 = h2 + (xx2 - h2) * ts
        kc = jnp.einsum('btc,oc->bto', xxx2, Wck)
        rc = jax.nn.sigmoid(jnp.einsum('btc,oc->bto', xxx2, Wcr))
        vv = jnp.einsum('bth,ch->btc', jax.nn.relu(kc) ** 2, Wcv)
        return x + rc * vv

    def _L0_ffn_ref(x, gate_w, gate_b, w1, b1, w3, b3, w2, b2, sw1, sb1, sw3, sb3, sw2, sb2):
        import jax, jax.numpy as jnp
        import numpy as np
        E = 8
        TOP_K = 2
        ROUTE_SCALE = 1.0
        ALPHA = 1.702
        LIMIT = 7.0
        D = 128
        F = 128
        B, S = (2, 128)

        def swiglu(h):
            g = jnp.minimum(h[..., ::2], LIMIT)
            l = jnp.clip(h[..., 1::2], -LIMIT, LIMIT)
            return g * jax.nn.sigmoid(ALPHA * g) * (l + 1.0)
        if __name__ == '__main__':
            out = reference(**setup_inputs())
            print(out.shape, out.dtype)
        inp_shape = x.shape
        xt = x.reshape(-1, D)
        logits = xt @ gate_w.T
        scores = jax.nn.softmax(logits.astype(jnp.float32), axis=-1)
        biased = scores + gate_b.astype(jnp.float32)
        idx = jax.lax.top_k(biased, TOP_K)[1]
        weights = (jnp.take_along_axis(scores, idx, axis=-1) * ROUTE_SCALE).astype(x.dtype)
        cw = jnp.sum(jax.nn.one_hot(idx, E, dtype=x.dtype) * weights[..., None], axis=1)
        h1 = jnp.einsum('td,efd->etf', xt, w1) + b1[:, None, :]
        h3 = jnp.einsum('td,efd->etf', xt, w3) + b3[:, None, :]
        a = swiglu(h1 * h3)
        y = jnp.einsum('etf,edf->etd', a, w2) + b2[:, None, :]
        routed = jnp.einsum('te,etd->td', cw, y)
        sh = swiglu((xt @ sw1.T + sb1) * (xt @ sw3.T + sb3))
        shared = sh @ sw2.T + sb2
        return (routed + shared).reshape(inp_shape)

    def _L1_attn_ref(x, ln1_g, ln1_b, w_qkv, alpha_head, w_out, ln2_g, ln2_b, w1, b1, w2, b2, alpha):
        import math
        import jax, jax.numpy as jnp
        import numpy as np
        DIM, NHEAD, TOPK = (128, 16, 64)
        DK = DIM // NHEAD
        HIDDEN = int(DIM * 8.0)
        EPS = 1e-05

        def _layernorm(x, g, b):
            mu = jnp.mean(x, axis=-1, keepdims=True)
            var = jnp.var(x, axis=-1, keepdims=True)
            return (x - mu) * jax.lax.rsqrt(var + EPS) * g + b

        def _adaptive_sparse_attn(xn, w_qkv, alpha_head, w_out):
            B, T, C = xn.shape
            qkv = xn @ w_qkv
            q, k, v = jnp.split(qkv, 3, axis=-1)

            def heads(t):
                return t.reshape(B, T, NHEAD, DK).transpose(0, 2, 1, 3)
            q, k, v = (heads(q), heads(k), heads(v))
            attn = jnp.einsum('bhqd,bhkd->bhqk', q, k) / math.sqrt(DK)
            dense = jnp.einsum('bhqk,bhkd->bhqd', jax.nn.softmax(attn, axis=-1), v)
            _, idx = jax.lax.top_k(attn, TOPK)
            M = B * NHEAD * T
            keep = jnp.zeros((M, T), bool).at[jnp.arange(M)[:, None], idx.reshape(M, TOPK)].set(True)
            keep = keep.reshape(B, NHEAD, T, T)
            attn_sp = jnp.where(keep, attn, jnp.float32(-1000000000.0))
            sparse = jnp.einsum('bhqk,bhkd->bhqd', jax.nn.softmax(attn_sp, axis=-1), v)
            gate = jax.nn.sigmoid(alpha_head)[None, :, None, None]
            out = gate * dense + (1.0 - gate) * sparse
            out = out.transpose(0, 2, 1, 3).reshape(B, T, C)
            return out @ w_out
        x = x + alpha * _adaptive_sparse_attn(_layernorm(x, ln1_g, ln1_b), w_qkv, alpha_head, w_out)
        h = jax.nn.gelu(_layernorm(x, ln2_g, ln2_b) @ w1 + b1, approximate=False)
        x = x + alpha * (h @ w2 + b2)
        return x

    def _L1_ffn_ref(x, router_w, router_bias, up_proj, gate_proj, down_proj, sh_gate, sh_up, sh_down):
        import jax, jax.numpy as jnp
        import numpy as np
        DIM = 128
        EXPERT_DIM = 64
        N_EXPERTS = 16
        TOPK = 2
        SHARED_HIDDEN = EXPERT_DIM * TOPK
        B, T = (4, 128)

        def _moe_forward(x, router_w, router_bias, up_proj, gate_proj, down_proj, sh_gate, sh_up, sh_down):
            Bb, Tt, D = x.shape
            flat = x.reshape(Bb * Tt, D)
            N = flat.shape[0]
            logits = flat @ router_w.T
            topk_scores, topk_idx = jax.lax.top_k(logits + router_bias, TOPK)
            topk_scores = jax.nn.softmax(topk_scores, axis=-1)
            combine = jnp.zeros((N, N_EXPERTS), flat.dtype)
            combine = combine.at[jnp.arange(N)[:, None], topk_idx].add(topk_scores)
            up_all = jnp.einsum('nd,kde->nke', flat, up_proj)
            gate_all = jnp.einsum('nd,kde->nke', flat, gate_proj)
            hidden = jax.nn.silu(gate_all) * up_all
            down_all = jnp.einsum('nke,ked->nkd', hidden, down_proj)
            out = jnp.einsum('nk,nkd->nd', combine, down_all)
            sh_hidden = jax.nn.silu(flat @ sh_gate.T) * (flat @ sh_up.T)
            out = out + sh_hidden @ sh_down.T
            return out.reshape(Bb, Tt, D)
        return _moe_forward(x, router_w, router_bias, up_proj, gate_proj, down_proj, sh_gate, sh_up, sh_down)
    x = L0_attn_x
    x = x + _L0_attn_ref(_layernorm(x, axis=-1), L0_attn_time_decay, L0_attn_time_first, L0_attn_time_shift, L0_attn_Wk, L0_attn_Wv, L0_attn_Wr, L0_attn_Wck, L0_attn_Wcv, L0_attn_Wcr, L0_attn_ln1_w, L0_attn_ln1_b, L0_attn_ln2_w, L0_attn_ln2_b)
    x = x + _L0_ffn_ref(_layernorm(x, axis=-1), L0_ffn_gate_w, L0_ffn_gate_b, L0_ffn_w1, L0_ffn_b1, L0_ffn_w3, L0_ffn_b3, L0_ffn_w2, L0_ffn_b2, L0_ffn_sw1, L0_ffn_sb1, L0_ffn_sw3, L0_ffn_sb3, L0_ffn_sw2, L0_ffn_sb2)
    x = x + _L1_attn_ref(_layernorm(x, axis=-1), L1_attn_ln1_g, L1_attn_ln1_b, L1_attn_w_qkv, L1_attn_alpha_head, L1_attn_w_out, L1_attn_ln2_g, L1_attn_ln2_b, L1_attn_w1, L1_attn_b1, L1_attn_w2, L1_attn_b2, L1_attn_alpha)
    x = x + _L1_ffn_ref(_layernorm(x, axis=-1), L1_ffn_router_w, L1_ffn_router_bias, L1_ffn_up_proj, L1_ffn_gate_proj, L1_ffn_down_proj, L1_ffn_sh_gate, L1_ffn_sh_up, L1_ffn_sh_down)
    return x

_drawn_inputs = setup_inputs


def setup_inputs(seed=0):
    import zlib

    import numpy as np

    out = dict(_drawn_inputs(seed))
    spreads = {'L0_attn_ln1_w': (1.0, 0.6),
     'L0_attn_ln1_b': (0.0, 0.1),
     'L0_attn_ln2_w': (1.0, 0.6),
     'L0_attn_ln2_b': (0.0, 0.8),
     'L1_attn_ln1_g': (1.0, 0.6),
     'L1_attn_ln1_b': (0.0, 0.8),
     'L1_attn_alpha_head': (0.0, 2.0),
     'L1_attn_ln2_g': (1.0, 0.6),
     'L1_attn_ln2_b': (0.0, 0.8),
     'L1_attn_b1': (0.0, 0.8),
     'L1_attn_b2': (0.0, 0.53),
     'L1_ffn_router_bias': (0.0, 0.8)}
    factors = {'L0_attn_time_first': 8.0,
     'L0_attn_time_shift': 6.635,
     'L0_attn_Wr': 3.86,
     'L0_attn_Wck': 4.777,
     'L0_attn_Wcv': 4.71,
     'L0_attn_Wcr': 8.0,
     'L0_ffn_b1': 58.759,
     'L0_ffn_b3': 55.675,
     'L0_ffn_b2': 51.005,
     'L0_ffn_sb1': 28.042,
     'L0_ffn_sb3': 30.221,
     'L0_ffn_sb2': 34.2,
     'L1_attn_w_qkv': 8.0,
     'L1_attn_w_out': 8.0,
     'L1_attn_w1': 4.721,
     'L1_attn_w2': 4.213,
     'L1_ffn_router_w': 8.0,
     'L1_ffn_up_proj': 8.0,
     'L1_ffn_gate_proj': 8.0,
     'L1_ffn_down_proj': 8.0,
     'L1_ffn_sh_gate': 8.0,
     'L1_ffn_sh_up': 8.0,
     'L1_ffn_sh_down': 8.0,
     'L0_ffn_gate_b': 6.304}
    for name, (base, spread) in spreads.items():
        noise = np.random.default_rng([zlib.crc32(name.encode()), seed]).standard_normal(out[name].shape)
        drawn = base * np.exp(spread * noise) if base else spread * noise
        out[name] = jnp.asarray(drawn.astype(out[name].dtype))
    for name, factor in factors.items():
        out[name] = (out[name] * factor).astype(out[name].dtype)
    return out
```

```python
from contextlib import ExitStack

import concourse.bass as bass
from concourse import mybir

F32 = mybir.dt.float32
ACT = mybir.ActivationFunctionType
ALU = mybir.AluOpType
AX = mybir.AxisListType.X

P = 128
B, T = 4, 512
N = B * T
NT = N // P
QT = T // P
EPS = 1e-5
EB, ED = 8, 16
UNITS = 9
RING = 3
HEADS, DK, TOPK = 16, 8, 64
HG = 4
NI = HEADS // HG * B
SCALE = DK ** -0.5
FILL = -3.0e38
HID = 8 * P

COLS = ["ln1w", "ln1b", "ln2w", "ln2b", "ts", "u", "aln1g", "aln1b", "aln2g", "aln2b", "mb2", "alpha"]
C_MB1 = len(COLS)
NCOLS = C_MB1 + HID // P


class Chain:

    def __init__(self, engine, sem):
        self.engine, self.sem, self.base, self.k = engine, sem, 0, 0

    def __call__(self, ins):
        ins.then_inc(self.sem, 1)
        self.k += 1
        self.engine.wait_ge(self.sem, self.base + self.k)

    def enter(self, i, per, before):
        self.base, self.k = i * per + before, 0

    def leave(self, per, total):
        assert self.k == per, self.k
        self.base, self.k = total, 0

    @property
    def total(self):
        return self.base + self.k


def build(nc, x_d, cols_d, rows_d, cst_d, wa_d, wb_d, b2_d, rt_d, wqkv_d, wo_d, wm1_d, wm2_d, wd_d, out_d):
    ctx = ExitStack()
    with ctx:
        def sb(name, shape):
            return ctx.enter_context(nc.sbuf_tensor(name, shape, F32))

        sems = {}

        def S(name):
            if name not in sems:
                sems[name] = ctx.enter_context(nc.semaphore(name))
            return sems[name]

        bank = [ctx.enter_context(nc.psum_tensor(f"bank{i}", [P, 512], F32)) for i in range(8)]
        SLOT = B * (T + 1)
        NSLOT = 17
        arena = sb("arena", [P, NSLOT * SLOT])

        def flat(n, w=N):
            return arena[:, n * SLOT:n * SLOT + w]

        def seq(n):
            return flat(n, SLOT).rearrange("p (b t) -> p b t", b=B)

        def bt(n):
            return flat(n).rearrange("p (b t) -> p b t", b=B)

        cols = sb("cols", [P, NCOLS])
        rows = sb("rows", [P, EB + ED + NI * HG])
        cst = sb("cst", [P, cst_d.shape[1]])
        ident = cst[:, 0:P]
        halfsel = cst[0:ED + 1, P:2 * P]
        rank = cst[:, 2 * P:2 * P + ED]
        ones = cst[0:EB + 1, 2 * P + ED:]
        xres = sb("xres", [P, NT, P])
        ytok = sb("ytok", [P, NT, P])
        feat = sb("feat", [P, N])
        stats = sb("stats", [P, NT, 6])
        mv = sb("mv", [P, NT, 2])
        rstd = sb("rstd", [P, 2, NT])
        shiftc = sb("shiftc", [P, 4])
        small = sb("small", [P, 8, NT])
        rt = sb("rt", [P, EB + ED])
        b2 = sb("b2", [EB + 1, P])

        def col(name):
            n = COLS.index(name)
            return cols[:, n:n + 1]

        WA = 16
        wk, wv, wr, wcr = (flat(WA)[:, n * P:(n + 1) * P] for n in range(4))
        wck = flat(WA)[:, 4 * P:8 * P]
        wcv = flat(WA)[:, 8 * P:12 * P]
        htok = flat(0).rearrange("p (t c) -> p t c", t=NT)
        htok_b = htok_c = flat(12).rearrange("p (t c) -> p t c", t=NT)
        htok_d = flat(3).rearrange("p (t c) -> p t c", t=NT)
        def temp(slot, n):
            return flat(slot)[:, n * T:(n + 1) * T]
        Q_ALL, K_ALL, O_ALL, V_ALL, QK = 0, 4, 8, 12, 13
        q_all = arena[:, Q_ALL * SLOT:Q_ALL * SLOT + 4 * N]
        k_all = arena[:, K_ALL * SLOT:K_ALL * SLOT + 4 * N]
        o_all = arena[:, O_ALL * SLOT:O_ALL * SLOT + 4 * N]
        v_all = flat(V_ALL)
        q_cur, k_cur, v_cur = temp(QK, 0), temp(QK, 1), temp(QK, 2)
        v_curv = v_cur.rearrange("p (k h c) -> p k h c", k=QT, h=HG)
        scores = [temp(QK, 3), temp(QK + 1, 0)]
        probs = [temp(QK + 1, 1), temp(QK + 1, 2)]
        sparse = [temp(QK + 1, 3), temp(QK + 2, 0)]
        mixed = [temp(QK + 2, 1), temp(QK + 2, 2)]
        wqkv = flat(16)[:, 0:9 * P]
        pT = [sb(f"pT{n}", [P, QT, T]) for n in range(2)]
        hi = sb("hi", [P, 2, 8])
        tiny = sb("tiny", [P, 2, 8])
        gates = sb("gates", [P, 2, NI * HG])

        block = ctx.enter_context(nc.Block())

        WU = {"B": (wb_d, 5 * P + 5), "D": (wd_d, 3 * P + 1)}

        @block.sync
        def _(sp):
            sp.dma_start(cst[:, :], cst_d).then_inc(S("ld_const"), 16)
            sp.dma_start(cols[:, :], cols_d).then_inc(S("ld_const"), 16)
            sp.dma_start(rows[:, :], rows_d).then_inc(S("ld_const"), 16)
            for b in range(B):
                sp.dma_start(xres[:, QT * b:QT * (b + 1), :], x_d[b]).then_inc(S(f"ld_x{b}"), 16)
            sp.dma_start(flat(WA)[:, 0:12 * P], wa_d).then_inc(S("ld_wa"), 16)
            sp.dma_start(rt[:, :], rt_d).then_inc(S("ld_b"), 16)
            sp.dma_start(b2[:, :], b2_d).then_inc(S("ld_b"), 16)

            def moe_weights(tag, free):
                src, w = WU[tag]
                for u in range(RING):
                    sp.dma_start(flat(u)[:, 0:w], src[u]).then_inc(S(f"{tag}_w{u}"), 16)
                with sp.Fori(1, UNITS // RING) as i:
                    for u in range(RING):
                        sp.wait_ge(S(f"{tag}_down"), i * (RING * B) - (RING * B) + B * (u + 1))
                        sp.dma_start(flat(u)[:, 0:w],
                                     src[bass.ds(i * RING + u, 1), :, :].rearrange("a p n -> p (a n)")
                                     ).then_inc(S(f"{tag}_w{u}"), 16)

            sp.wait_ge(S("A_out"), B)
            moe_weights("B", None)
            sp.wait_ge(S("B_out"), B)
            sp.dma_start(wqkv, wqkv_d).then_inc(S("ld_qkv"), 16)
            sp.wait_ge(S("C_iter"), NI + 1)
            sp.dma_start(flat(0)[:, 0:4 * P], wo_d).then_inc(S("ld_wo"), 16)
            sp.dma_start(flat(1)[:, 0:HID], wm1_d).then_inc(S("ld_mlp"), 16)
            sp.dma_start(flat(1)[:, HID:2 * HID], wm2_d).then_inc(S("ld_mlp"), 16)
            sp.wait_ge(S("C_out"), B)
            moe_weights("D", None)
            for b in range(B):
                sp.wait_ge(S("D_out"), b + 1)
                sp.dma_start(out_d[b], xres[:, QT * b:QT * (b + 1), :]).then_inc(S("stored"), 16)
            sp.wait_ge(S("stored"), 16 * B)

        @block.gpsimd
        def _(gp):
            def masks(tag, rows_n, at, cwT):
                gp.wait_ge(S(f"{tag}_cwT"), B)

                def unit(i, u, first):
                    gp.wait_ge(S(f"{tag}_w{u}"), i * 16 + 16)
                    gp.sem_inc(S("gp_passed"), 1)
                    for c in range(B):
                        if not (first and u == 0 and c < 2):
                            k = i * (RING * B) + (B * u + c)
                            gp.wait_ge(S(f"{tag}_bc"), k - 1)
                            gp.sem_inc(S("gp_passed"), 1)
                        gp.tensor_scalar(temp(4, c % 2)[0:rows_n, :], cwT[0:rows_n, c * T:(c + 1) * T],
                                         flat(u)[0:rows_n, at:at + 1], None, ALU.mult).then_inc(S(f"{tag}_msk"), 1)

                for u in range(RING):
                    unit(0, u, True)
                with gp.Fori(1, UNITS // RING) as i:
                    for u in range(RING):
                        unit(i, u, False)

            gp.wait_ge(S("ld_const"), 48)
            masks("B", EB + 1, 5 * P + 4, flat(3))
            gp.wait_ge(S("C_qkv"), 1)
            gp.memset(v_cur, 0.0).then_inc(S("gp_self"), 1)
            gp.wait_ge(S("gp_self"), 1)
            with gp.Fori(0, NI) as i:
                gp.wait_ge(S("C_iter"), i + 1)
                gp.sem_inc(S("gp_passed"), 1)
                gp.tensor_copy(q_cur, q_all[:, bass.ds(i * T, T)]).then_inc(S("C_cur"), 1)
                gp.tensor_copy(k_cur, k_all[:, bass.ds(i * T, T)]).then_inc(S("C_cur"), 1)
                gp.tensor_copy(v_cur.rearrange("p (a c) -> p a c", c=32)[:, :, 0:DK],
                               v_all[:, bass.ds(i * P, P)].rearrange("p (a c) -> p a c", c=DK)
                               ).then_inc(S("C_cur"), 1)
            masks("D", ED + 1, 3 * P, flat(3))

        @block.scalar
        def _(act):
            def ln(tag, dst, w=None, b=None):
                act.wait_ge(S(f"{tag}_var"), 1)
                act.activation(rstd[:, :, :], rstd[:, :, :], ACT.Sqrt).then_inc(S(f"{tag}_std"), 1)
                for c in range(B):
                    act.wait_ge(S(f"{tag}_T"), c + 1)
                    if w is None:
                        act.activation(dst[:, c * T:(c + 1) * T], bank[c][:, :], ACT.Copy).then_inc(S(f"{tag}_F"), 1)
                    else:
                        act.activation(dst[:, c * T:(c + 1) * T], bank[c][:, :], ACT.Identity,
                                       bias=b, scale=w).then_inc(S(f"{tag}_F"), 1)

            def chunk(n, c):
                return flat(n)[:, c * T:(c + 1) * T]

            act.wait_ge(S("ld_const"), 48)
            ln("ln1", feat, col("ln1w"), col("ln1b"))
            for c in range(B):
                act.wait_ge(S("A_kv"), c + 1)
                act.activation(chunk(1, c), bank[c][:, :], ACT.Copy).then_inc(S("A_kvs"), 1)
                act.activation(chunk(2, c), bank[4 + c][:, :], ACT.Copy).then_inc(S("A_kvs"), 1)
            for n, s in ((6, "A_gx"), (7, "A_bx"), (8, "A_e1x"), (9, "A_e2x")):
                act.wait_ge(S(s), 1)
                act.activation(bt(n), bt(n), ACT.Exp).then_inc(S("A_exps"), 1)
            for c in range(B):
                act.wait_ge(S("A_r"), c + 1)
                act.activation(chunk(3, c), bank[c][:, :], ACT.Sigmoid).then_inc(S("A_rs"), 1)
            ln("ln2", feat, col("ln2w"), col("ln2b"))
            for c in range(B):
                act.wait_ge(S("A_rc"), c + 1)
                act.activation(chunk(3, c), bank[c][:, :], ACT.Sigmoid).then_inc(S("A_rcs"), 1)
            for s in range(B * 4):
                act.wait_ge(S("A_kc"), s + 1)
                if s >= 4:
                    act.wait_ge(S("A_sq"), s - 3)
                act.activation(temp(4, s % 4), bank[4 + s % 2][:, :], ACT.Relu).then_inc(S("A_rl"), 1)

            def route(tag, ln_tag, ne):
                act.wait_ge(S(f"{tag}_ex"), 1)
                act.activation(flat(5)[:, 0:NT * ne], flat(5)[:, 0:NT * ne], ACT.Exp).then_inc(S(f"{tag}_exp"), 1)
                for c in range(B):
                    act.wait_ge(S(f"{tag}_cwTp"), c + 1)
                    act.activation(flat(3)[0:ne + 1, c * T:(c + 1) * T], bank[4 + c][0:ne + 1, :],
                                   ACT.Copy).then_inc(S(f"{tag}_cwT"), 1)

            def acc_out(tag):
                for c in range(B):
                    act.wait_ge(S(f"{tag}_acc"), 1)
                    act.activation(chunk(8, c), bank[c][:, :], ACT.Copy).then_inc(S(f"{tag}_accs"), 1)

            ln("ln3", feat)
            route("B", "ln3", EB)

            def unit_b(i, u, first):
                for c in range(B):
                    k = i * (RING * B) + (B * u + c)

                    def bias(n):
                        return flat(u)[:, 5 * P + n:5 * P + n + 1]
                    act.wait_ge(S("B_h1e"), k + 1)
                    act.activation(temp(5, c % 2), bank[4 + (5 * c) % 4][:, :], ACT.Identity,
                                   bias=bias(0)).then_inc(S("B_t1"), 1)
                    act.wait_ge(S("B_h1o"), k + 1)
                    act.activation(temp(5, 2 + c % 2), bank[4 + (5 * c + 2) % 4][:, :], ACT.Identity,
                                   bias=bias(1)).then_inc(S("B_t2"), 1)
                    act.wait_ge(S("B_g"), k + 1)
                    act.activation(temp(6, c % 2), temp(6, 2 + c % 2), ACT.Sigmoid,
                                   scale=1.702).then_inc(S("B_sg"), 1)
            for u in range(RING):
                unit_b(0, u, True)
            with act.Fori(1, UNITS // RING) as i:
                for u in range(RING):
                    unit_b(i, u, False)
            acc_out("B")

            act.wait_ge(S("C_gx"), 1)
            act.activation(gates[:, 0, :], rows[:, EB + ED:], ACT.Sigmoid).then_inc(S("C_gate"), 1)
            ln("ln4", feat, col("aln1g"), col("aln1b"))
            for n in range(2 * HG):
                for c in range(B):
                    s = n * B + c
                    act.wait_ge(S("C_pj"), s + 1)
                    dst = (q_all if n < HG else k_all)[:, ((n % HG) * B + c) * T:((n % HG) * B + c + 1) * T]
                    act.activation(dst, bank[4 + s % 4][:, :], ACT.Copy).then_inc(S("C_pjs"), 1)
            va = v_all.rearrange("p (g t c) -> p g t c", g=HG, t=NT)
            for t in range(NT):
                act.wait_ge(S("C_v"), t + 1)
                act.activation(va[:, :, t, :], bank[4 + t % 4][:, 0:P].rearrange("p (g c) -> p g c", g=HG),
                               ACT.Copy).then_inc(S("C_vs"), 1)
            act.sem_inc(S("C_iter"), 1)
            act.wait_ge(S("C_vs"), NT)
            act.sem_inc(S("C_qkv"), 1)
            NTI = HG * QT
            with act.Fori(0, NI) as i:
                def exp(ti):
                    act.wait_ge(S("C_nm"), i * NTI + (ti + 1))
                    if ti >= 2:
                        act.wait_ge(S("C_mix"), i * NTI + (ti - 1))
                    act.activation(probs[ti % 2], scores_p[ti % 2][:, :], ACT.Exp, bias=tiny[:, ti % 2, 0:1],
                                   scale=SCALE, accum_out=tiny[:, ti % 2, 1:2]).then_inc(S("C_exp"), 1)
                scores_p = [bank[0], bank[1]]
                exp(0)
                for ti in range(NTI):
                    if ti + 1 < NTI:
                        exp(ti + 1)
                    act.wait_ge(S("C_pT"), i * NTI + (ti + 1))
                    if ti >= 8 and ti % QT == 0:
                        act.wait_ge(S("C_pv"), i * HG + (ti // QT - 1))
                    q = ti % QT
                    act.activation(pT[ti // QT % 2][:, :, q * P:(q + 1) * P],
                                   bank[2 + ti % 2][:, :].rearrange("p (k q) -> p k q", k=QT),
                                   ACT.Copy).then_inc(S("C_pTs"), 1)
                act.wait_ge(S("C_pv"), i * HG + HG)
                act.sem_inc(S("act_passed"), 1)
                act.activation(o_all[:, bass.ds(i * T, T)], bank[4][:, :], ACT.Copy).then_inc(S("C_iter"), 1)

            for c in range(B):
                act.wait_ge(S("C_ao"), c + 1)
                act.activation(chunk(12, c), bank[c][:, :], ACT.Copy).then_inc(S("C_aos"), 1)
            ln("ln5", feat, col("aln2g"), col("aln2b"))
            for c in range(B):
                for j in range(HID // P):
                    s = c * (HID // P) + j
                    act.wait_ge(S("C_h"), s + 1)
                    if s >= 4:
                        act.wait_ge(S("C_dn"), s - 3)
                    act.activation(temp(2, s % 4), bank[4 + s % 2][:, :], ACT.Gelu,
                                   bias=cols[:, C_MB1 + j:C_MB1 + j + 1]).then_inc(S("C_gl"), 1)
                act.wait_ge(S("C_dn"), (c + 1) * (HID // P))
                act.activation(chunk(12, c), bank[c][:, :], ACT.Identity, bias=col("mb2")).then_inc(S("C_mo"), 1)

            ln("ln6", feat)
            route("D", "ln6", ED)

            def unit_d(i, u, first):
                for c in range(B):
                    k = i * (RING * B) + (B * u + c)
                    act.wait_ge(S("D_g"), k + 1)
                    act.activation(temp(5, c % 2), bank[4 + (3 * c) % 4][:, :], ACT.Silu).then_inc(S("D_sil"), 1)
            for u in range(RING):
                unit_d(0, u, True)
            with act.Fori(1, UNITS // RING) as i:
                for u in range(RING):
                    unit_d(i, u, False)
            acc_out("D")

        @block.vector
        def _(dve):
            link = Chain(dve, S("dve_self"))
            v = nc.vector

            def ln(tag, src, dst, double, dst_y=None):
                for t in range(NT):
                    if tag == "ln1" and t % QT == 0:
                        dve.wait_ge(S(f"ld_x{t // QT}"), 16)
                    ins = v.bn_stats(stats[:, t, :], src[:, t, :])
                link(ins)
                for t in range(NT):
                    ins = v.bn_aggr(mv[:, t, :], stats[:, t, :])
                link(ins)
                v.tensor_scalar(rstd[:, 0, :], mv[:, :, 1], EPS, None, ALU.add)
                v.tensor_scalar(rstd[:, 1, :], mv[:, :, 1], 1.0 + EPS, EPS * EPS, ALU.mult,
                                ALU.add).then_inc(S(f"{tag}_var"), 1)
                dve.wait_ge(S(f"{tag}_std"), 1)
                link(v.reciprocal(rstd[:, :, :], rstd[:, :, :]))
                r = 1 if double else 0
                for t in range(NT):
                    if dst_y is not None:
                        v.tensor_scalar(dst_y[:, t, :], src[:, t, :], mv[:, t, 0:1], rstd[:, 0, t:t + 1],
                                        ALU.subtract, ALU.mult)
                    ins = v.tensor_scalar(dst[:, t, :], src[:, t, :], mv[:, t, 0:1], rstd[:, r, t:t + 1],
                                          ALU.subtract, ALU.mult)
                    if t % QT == QT - 1:
                        ins.then_inc(S(f"{tag}_norm"), 1)

            def tok(x, c):
                return x[:, QT * c:QT * (c + 1), :].rearrange("p t c -> p (t c)")

            def chunk(n, c):
                return flat(n)[:, c * T:(c + 1) * T]

            dve.wait_ge(S("ld_const"), 48)
            ln("ln1", xres, htok, True, ytok)
            ts = col("ts")
            v.tensor_scalar(shiftc[:, 0:1], ts, 1.0, None, ALU.add)
            link(v.tensor_scalar(shiftc[:, 1:2], ts, -1.0, None, ALU.mult))
            v.tensor_tensor(shiftc[:, 2:3], shiftc[:, 1:2], ts, ALU.mult)
            link(v.tensor_scalar(shiftc[:, 3:4], shiftc[:, 1:2], 1.0, None, ALU.add))
            K_, V_, R_, M_, D_, AA = 1, 2, 3, 4, 5, 10
            G_, B_, E1, E2, MX, BE, X_, TMP = 6, 7, 8, 9, 11, 12, 13, 14
            v.memset(seq(M_)[:, :, 0:1], 0.0)
            v.memset(seq(D_)[:, :, 0:1], 1.0)
            v.memset(seq(AA)[:, :, 0:1], 0.0)
            for c in range(B):
                dve.wait_ge(S("ln1_F"), c + 1)
                h = feat[:, c * T:(c + 1) * T]
                link(v.tensor_scalar(chunk(TMP, c), h, shiftc[:, 0:1], None, ALU.mult))
                v.tensor_scalar(chunk(X_, c)[:, 0:1], chunk(TMP, c)[:, 0:1], shiftc[:, 2:3], None, ALU.add)
                v.scalar_tensor_tensor(chunk(X_, c)[:, 1:T], h[:, 0:T - 1], shiftc[:, 1:2],
                                       chunk(TMP, c)[:, 1:T], ALU.mult, ALU.add).then_inc(S("A_xxx"), 1)
            dve.wait_ge(S("A_kvs"), 2 * B)
            for c in range(B):
                ins = v.tensor_tensor_scan(seq(M_)[:, c, 1:], chunk(K_, c), chunk(K_, c), 0.0, ALU.max, ALU.max)
            link(ins)
            mprev, mcur = seq(M_)[:, :, 0:T], seq(M_)[:, :, 1:]
            v.tensor_tensor(bt(G_), mprev, mcur, ALU.subtract).then_inc(S("A_gx"), 1)
            v.tensor_tensor(bt(B_), bt(K_), mcur, ALU.subtract).then_inc(S("A_bx"), 1)
            link(v.scalar_tensor_tensor(bt(MX), bt(K_), col("u"), mprev, ALU.add, ALU.max))
            v.tensor_tensor(bt(E1), mprev, bt(MX), ALU.subtract).then_inc(S("A_e1x"), 1)
            v.scalar_tensor_tensor(bt(E2), bt(K_), col("u"), bt(MX), ALU.add, ALU.subtract).then_inc(S("A_e2x"), 1)
            dve.wait_ge(S("A_exps"), 2)
            for c in range(B):
                ins = v.tensor_tensor_scan(seq(D_)[:, c, 1:], chunk(G_, c), chunk(B_, c), 1.0, ALU.mult, ALU.add)
            link(ins)
            dprev = seq(D_)[:, :, 0:T]
            link(v.tensor_tensor(bt(G_), bt(G_), dprev, ALU.mult))
            link(v.tensor_tensor(bt(MX), bt(G_), bt(B_), ALU.max))
            link(v.reciprocal(bt(MX), bt(MX)))
            v.tensor_tensor(bt(G_), bt(G_), bt(MX), ALU.mult)
            link(v.tensor_tensor(bt(B_), bt(B_), bt(MX), ALU.mult))
            link(v.tensor_tensor(bt(B_), bt(B_), bt(V_), ALU.mult))
            for c in range(B):
                ins = v.tensor_tensor_scan(seq(AA)[:, c, 1:], chunk(G_, c), chunk(B_, c), 0.0, ALU.mult, ALU.add)
            link(ins)
            aprev = seq(AA)[:, :, 0:T]
            dve.wait_ge(S("A_exps"), 4)
            link(v.tensor_tensor(bt(E1), bt(E1), dprev, ALU.mult))
            v.tensor_tensor(bt(MX), bt(E1), bt(E2), ALU.add)
            v.tensor_tensor(bt(E1), bt(E1), aprev, ALU.mult)
            link(v.tensor_tensor(bt(E2), bt(E2), bt(V_), ALU.mult))
            v.reciprocal(bt(MX), bt(MX))
            link(v.tensor_tensor(bt(E1), bt(E1), bt(E2), ALU.add))
            link(v.tensor_tensor(bt(E1), bt(E1), bt(MX), ALU.mult))
            dve.wait_ge(S("A_rs"), B)
            v.tensor_tensor(bt(E1), bt(E1), bt(R_), ALU.mult).then_inc(S("A_z"), 1)
            for c in range(B):
                dve.wait_ge(S("A_zT"), c + 1)
                ins = v.tensor_tensor(tok(ytok, c), tok(ytok, c), bank[c][:, :], ALU.add)
            link(ins)
            link(v.tensor_tensor(xres[:, :, :], xres[:, :, :], ytok[:, :, :], ALU.add))
            ln("ln2", ytok, htok, False)
            for c in range(B):
                dve.wait_ge(S("ln2_F"), c + 1)
                h = feat[:, c * T:(c + 1) * T]
                link(v.tensor_scalar(chunk(TMP, c), h, shiftc[:, 3:4], None, ALU.mult))
                v.scalar_tensor_tensor(chunk(X_, c)[:, 0:1], h[:, T - 1:T], ts,
                                       chunk(TMP, c)[:, 0:1], ALU.mult, ALU.add)
                v.scalar_tensor_tensor(chunk(X_, c)[:, 1:T], h[:, 0:T - 1], ts,
                                       chunk(TMP, c)[:, 1:T], ALU.mult, ALU.add).then_inc(S("A_xx2"), 1)
            dve.wait_ge(S("A_rcs"), B)
            for c in range(B):
                for j in range(4):
                    s = 4 * c + j
                    dve.wait_ge(S("A_rl"), s + 1)
                    if s >= 4:
                        dve.wait_ge(S("A_vv"), s - 3)
                    v.tensor_tensor(temp(5, s % 4), temp(4, s % 4), temp(4, s % 4), ALU.mult).then_inc(S("A_sq"), 1)
                dve.wait_ge(S("A_vv"), 4 * (c + 1))
                v.tensor_tensor(chunk(7, c), chunk(3, c), bank[6 + c % 2][:, :], ALU.mult).then_inc(S("A_vz"), 1)
            for c in range(B):
                dve.wait_ge(S("A_vT"), c + 1)
                ins = v.tensor_tensor(tok(xres, c), tok(xres, c), bank[c][:, :], ALU.add)
                ins.then_inc(S("A_out"), 1)
            dve.wait_ge(S("A_out"), B)

            def route(tag, ne, soft):
                def e3(n):
                    return flat(n)[:, 0:NT * ne].rearrange("p (t e) -> p t e", e=ne)

                def e2(n):
                    return flat(n)[:, 0:NT * ne]

                def wide(a):
                    return a.unsqueeze(2).broadcast_to([P, NT, ne])

                def over(row):
                    return row.unsqueeze(1).broadcast_to([P, NT, ne])
                logits, bias = bank[4][:, 0:NT * ne].rearrange("p (t e) -> p t e", e=ne), \
                    over(rows[:, 0:EB] if tag == "B" else rows[:, EB:EB + ED])
                rk = over(rank[:, ED - ne:])
                EX, BI, EQ, OH, CW = 5, 6, 7, 9, 10
                m, s = small[:, 0, :], small[:, 1, :]
                dve.wait_ge(S(f"{tag}_lg"), 1)
                if soft:
                    link(v.tensor_reduce(m, logits, AX, ALU.max))
                    v.tensor_tensor(e3(EX), logits, wide(m), ALU.subtract).then_inc(S(f"{tag}_ex"), 1)
                    dve.wait_ge(S(f"{tag}_exp"), 1)
                    link(v.tensor_reduce(s, e3(EX), AX, ALU.add))
                    link(v.reciprocal(s, s))
                    link(v.tensor_tensor(e3(EX), e3(EX), wide(s), ALU.mult))
                    link(v.tensor_tensor(e3(BI), e3(EX), bias, ALU.add))
                else:
                    link(v.tensor_tensor(e3(BI), logits, bias, ALU.add))
                for r in range(2):
                    mx = small[:, 2 + r, :]
                    link(v.tensor_reduce(mx, e3(BI), AX, ALU.max))
                    link(v.tensor_tensor(e3(EQ), e3(BI), wide(mx), ALU.is_equal))
                    link(v.tensor_tensor(e3(EQ), e3(EQ), rk, ALU.mult))
                    link(v.tensor_reduce(small[:, 4, :], e3(EQ), AX, ALU.max))
                    link(v.tensor_tensor(e3(OH + 2 * r), rk, wide(small[:, 4, :]), ALU.is_equal))
                    if r == 0:
                        link(v.scalar_tensor_tensor(e2(BI), e2(OH), FILL, e2(BI), ALU.mult, ALU.add))
                cw = flat(CW)[:, 0:NT * (ne + 1)].rearrange("p (t e) -> p t e", e=ne + 1)
                link(v.memset(cw[:, :, ne:], 1.0))
                if soft:
                    link(v.tensor_tensor(e2(OH), e2(OH), e2(OH + 2), ALU.add))
                    v.tensor_tensor(cw[:, :, 0:ne], e3(EX), e3(OH), ALU.mult).then_inc(S(f"{tag}_cw"), 1)
                else:
                    v.tensor_tensor(flat(EX)[:, 0:NT], small[:, 3, :], small[:, 2, :],
                                    ALU.subtract)
                    v.memset(flat(EX)[:, NT:NT * ne], 0.0).then_inc(S(f"{tag}_ex"), 1)
                    dve.wait_ge(S(f"{tag}_exp"), 1)
                    ex = flat(EX)[:, 0:NT]
                    link(v.tensor_scalar(s, ex, 1.0, None, ALU.add))
                    link(v.reciprocal(s, s))
                    link(v.tensor_tensor(m, ex, s, ALU.mult))
                    v.tensor_tensor(e3(OH), e3(OH), wide(s), ALU.mult)
                    link(v.tensor_tensor(e3(OH + 2), e3(OH + 2), wide(m), ALU.mult))
                    v.tensor_tensor(cw[:, :, 0:ne], e3(OH), e3(OH + 2), ALU.add).then_inc(S(f"{tag}_cw"), 1)

            def add_back(tag):
                for c in range(B):
                    dve.wait_ge(S(f"{tag}_oT"), c + 1)
                    v.tensor_tensor(tok(xres, c), tok(xres, c), bank[4 + c][:, :], ALU.add).then_inc(S(f"{tag}_out"), 1)
                dve.wait_ge(S(f"{tag}_out"), B)

            ln("ln3", xres, htok_b, False)
            route("B", EB, True)

            def unit_b(i, u, first):
                for c in range(B):
                    k = i * (RING * B) + (B * u + c)

                    def bias(n):
                        return flat(u)[:, 5 * P + n:5 * P + n + 1]
                    dve.wait_ge(S("B_h3e"), k + 1)
                    dve.wait_ge(S("B_t1"), k + 1)
                    link(v.scalar_tensor_tensor(temp(7, c % 2), bank[4 + (5 * c + 1) % 4][:, :], bias(2),
                                                temp(5, c % 2), ALU.add, ALU.mult))
                    v.tensor_scalar(temp(6, 2 + c % 2), temp(7, c % 2), 7.0, None, ALU.min).then_inc(S("B_g"), 1)
                    dve.wait_ge(S("B_h3o"), k + 1)
                    dve.wait_ge(S("B_t2"), k + 1)
                    v.scalar_tensor_tensor(temp(7, 2 + c % 2), bank[4 + (5 * c + 3) % 4][:, :], bias(3),
                                           temp(5, 2 + c % 2), ALU.add, ALU.mult).then_inc(S("B_po"), 1)
                    dve.wait_ge(S("B_po"), k + 1)
                    link(v.tensor_scalar(temp(7, 2 + c % 2), temp(7, 2 + c % 2), 7.0, -7.0, ALU.min, ALU.max))
                    link(v.scalar_tensor_tensor(temp(9, c % 2), temp(7, 2 + c % 2), 1.0, temp(6, 2 + c % 2),
                                                ALU.add, ALU.mult))
                    dve.wait_ge(S("B_sg"), k + 1)
                    link(v.tensor_tensor(temp(9, c % 2), temp(9, c % 2), temp(6, c % 2), ALU.mult))
                    if not (first and u == 0 and c < 2):
                        dve.wait_ge(S("B_down"), k - 1)
                    dve.wait_ge(S("B_bc"), k + 1)
                    v.tensor_tensor(temp(9, 2 + c % 2), temp(9, c % 2), bank[4 + (5 * c + 4) % 4][:, :],
                                    ALU.mult).then_inc(S("B_a"), 1)
            per = RING * B * 4
            for u in range(RING):
                unit_b(0, u, True)
            before = link.total
            with dve.Fori(1, UNITS // RING) as i:
                link.enter(i, per, before - per)
                for u in range(RING):
                    unit_b(i, u, False)
                link.leave(per, before + per * (UNITS // RING - 1))
            add_back("B")

            dve.sem_inc(S("C_gx"), 1)
            ln("ln4", xres, htok_c, True, ytok)
            dve.wait_ge(S("C_gate"), 1)
            link(v.tensor_scalar(gates[:, 1, :], gates[:, 0, :], -1.0, 1.0, ALU.mult, ALU.add))
            NTI = HG * QT
            outer, link = link, Chain(dve, S("dve_loop"))
            with dve.Fori(0, NI) as i:
                dve.sem_clear(S("dve_loop"))
                link.k = 0

                def take(ti):
                    r = ti % 2
                    dve.wait_ge(S("C_s"), i * NTI + (ti + 1))
                    link(v.tensor_scalar(scores[r], bank[r][:, :], 1.0, None, ALU.mult, ALU.max,
                                         accum_out=tiny[:, r, 2:3]))
                    v.tensor_scalar(tiny[:, r, 0:1], tiny[:, r, 2:3], -SCALE, None, ALU.mult).then_inc(S("C_nm"), 1)
                take(0)
                for ti in range(NTI):
                    r = ti % 2
                    if ti + 1 < NTI:
                        if ti >= 1:
                            dve.wait_ge(S("C_exp"), i * NTI + ti)
                        take(ti + 1)
                    for n in range(TOPK // 8):
                        link(v.max(hi[:, r, :], scores[r]))
                        link(v.match_replace(scores[r], hi[:, r, :], scores[r], FILL))
                    dve.wait_ge(S("C_exp"), i * NTI + (ti + 1))
                    link(v.reciprocal(tiny[:, r, 3:4], tiny[:, r, 1:2]))
                    v.tensor_tensor(tiny[:, r, 4:5], tiny[:, r, 3:4],
                                    gates[:, 0, bass.ds(i * HG + ti // QT, 1)], ALU.mult)
                    link(v.scalar_tensor_tensor(sparse[r], scores[r], FILL, probs[r], ALU.is_equal, ALU.mult,
                                                accum_out=tiny[:, r, 5:6]))
                    if ti >= 2:
                        dve.wait_ge(S("C_pT"), i * NTI + (ti - 1))
                    v.tensor_scalar(mixed[r], probs[r], tiny[:, r, 4:5], None, ALU.mult)
                    link(v.reciprocal(tiny[:, r, 6:7], tiny[:, r, 5:6]))
                    link(v.tensor_tensor(tiny[:, r, 7:8], tiny[:, r, 6:7],
                                         gates[:, 1, bass.ds(i * HG + ti // QT, 1)], ALU.mult))
                    link(v.scalar_tensor_tensor(mixed[r], sparse[r], tiny[:, r, 7:8], mixed[r],
                                                ALU.mult, ALU.add))
                    dve.sem_inc(S("C_mix"), 1)
            link = outer

            def token_add(tag, out_sem):
                for c in range(B):
                    dve.wait_ge(S(tag), c + 1)
                    ins = v.scalar_tensor_tensor(tok(ytok, c), bank[4 + c][:, :], col("alpha"), tok(ytok, c),
                                                 ALU.mult, ALU.add)
                link(ins)
            token_add("C_aT", None)
            ln("ln5", ytok, htok_d, False)
            token_add("C_mT", None)
            for c in range(B):
                v.tensor_tensor(tok(xres, c), tok(xres, c), tok(ytok, c), ALU.add).then_inc(S("C_out"), 1)
            dve.wait_ge(S("C_out"), B)

            ln("ln6", xres, htok_b, False)
            route("D", ED, False)

            def unit_d(i, u, first):
                for c in range(B):
                    k = i * (RING * B) + (B * u + c)
                    dve.wait_ge(S("D_u"), k + 1)
                    dve.wait_ge(S("D_sil"), k + 1)
                    v.tensor_tensor(temp(9, c % 2), temp(5, c % 2), bank[4 + (3 * c + 1) % 4][:, :],
                                    ALU.mult).then_inc(S("D_us"), 1)
                    dve.wait_ge(S("D_us"), k + 1)
                    if not (first and u == 0 and c < 2):
                        dve.wait_ge(S("D_down"), k - 1)
                    dve.wait_ge(S("D_bc"), k + 1)
                    v.tensor_tensor(temp(9, 2 + c % 2), temp(9, c % 2), bank[4 + (3 * c + 2) % 4][:, :],
                                    ALU.mult).then_inc(S("D_a"), 1)
            for u in range(RING):
                unit_d(0, u, True)
            with dve.Fori(1, UNITS // RING) as i:
                for u in range(RING):
                    unit_d(i, u, False)
            add_back("D")

        @block.tensor
        def _(pe):
            mm = nc.tensor.matmul

            def chunk(n, c):
                return flat(n)[:, c * T:(c + 1) * T]

            def ln(tag, src):
                for c in range(B):
                    pe.wait_ge(S(f"{tag}_norm"), c + 1)
                    for t in range(QT):
                        ins = nc.tensor.transpose(bank[c][:, t * P:(t + 1) * P], src[:, QT * c + t, :], ident)
                    ins.then_inc(S(f"{tag}_T"), 1)

            def to_tokens(src, c, dst):
                for t in range(QT):
                    ins = nc.tensor.transpose(dst[:, t * P:(t + 1) * P], src[:, t * P:(t + 1) * P], ident)
                return ins

            pe.wait_ge(S("ld_const"), 48)
            ln("ln1", htok)
            pe.wait_ge(S("ld_wa"), 16)
            for c in range(B):
                pe.wait_ge(S("A_xxx"), c + 1)
                mm(bank[c][:, :], wk, chunk(13, c), start=True, stop=True)
                mm(bank[4 + c][:, :], wv, chunk(13, c), start=True, stop=True).then_inc(S("A_kv"), 1)
            for c in range(B):
                pe.wait_ge(S("A_kvs"), 2 * (c + 1))
                mm(bank[c][:, :], wr, chunk(13, c), start=True, stop=True).then_inc(S("A_r"), 1)
            pe.wait_ge(S("A_z"), 1)
            for c in range(B):
                to_tokens(chunk(8, c), c, bank[c]).then_inc(S("A_zT"), 1)
            ln("ln2", htok)
            for c in range(B):
                pe.wait_ge(S("A_xx2"), c + 1)
                mm(bank[c][:, :], wcr, chunk(13, c), start=True, stop=True).then_inc(S("A_rc"), 1)

            def up(s):
                if s >= 2:
                    pe.wait_ge(S("A_rl"), s - 1)
                mm(bank[4 + s % 2][:, :], wck[:, (s % 4) * P:(s % 4 + 1) * P], chunk(13, s // 4),
                   start=True, stop=True).then_inc(S("A_kc"), 1)
            up(0)
            up(1)
            for s in range(4 * B):
                if s + 2 < 4 * B:
                    up(s + 2)
                if s % 4 == 0 and s >= 8:
                    pe.wait_ge(S("A_vz"), s // 4 - 1)
                pe.wait_ge(S("A_sq"), s + 1)
                mm(bank[6 + s // 4 % 2][:, :], wcv[:, (s % 4) * P:(s % 4 + 1) * P], temp(5, s % 4),
                   start=(s % 4 == 0), stop=(s % 4 == 3)).then_inc(S("A_vv"), 1)
            for c in range(B):
                pe.wait_ge(S("A_vz"), c + 1)
                to_tokens(chunk(7, c), c, bank[c]).then_inc(S("A_vT"), 1)

            def route(tag, ne, w):
                pe.wait_ge(S(f"ln{'3' if tag == 'B' else '6'}_F"), B)
                for t in range(NT):
                    ins = mm(bank[4][:, t * ne:(t + 1) * ne], feat[:, t * P:(t + 1) * P], w, start=True, stop=True)
                ins.then_inc(S(f"{tag}_lg"), 1)
                pe.wait_ge(S(f"{tag}_cw"), 1)
                cw = flat(10)[:, 0:NT * (ne + 1)].rearrange("p (t e) -> p t e", e=ne + 1)
                for c in range(B):
                    for t in range(QT):
                        ins = nc.tensor.transpose(bank[4 + c][0:ne + 1, t * P:(t + 1) * P], cw[:, QT * c + t, :], ident)
                    ins.then_inc(S(f"{tag}_cwTp"), 1)
                pe.wait_ge(S(f"{tag}_cwT"), B)

            def moe(tag, ne, products, sel, tail):
                npr = len(products) + 1

                def step(i, u, c, first):
                    k = i * (RING * B) + (B * u + c)
                    if c == 0:
                        pe.wait_ge(S(f"{tag}_w{u}"), i * 16 + 16)
                    for n, (done, w, reader, lag) in enumerate(products):
                        if not (first and u == 0 and c < lag):
                            pe.wait_ge(S(reader), k - lag + 1)
                        mm(bank[4 + (npr * c + n) % 4][:, :], flat(u)[:, w * P:(w + 1) * P],
                           feat[:, c * T:(c + 1) * T], start=True, stop=True).then_inc(S(done), 1)
                    reader, lag = sel[1], sel[2]
                    if not (first and u == 0 and c < lag):
                        pe.wait_ge(S(reader), k - lag + 1)
                    pe.wait_ge(S(f"{tag}_msk"), k + 1)
                    mm(bank[4 + (npr * c + npr - 1) % 4][:, :], sel[0], temp(4, c % 2)[0:ne + 1, :],
                       start=True, stop=True).then_inc(S(f"{tag}_bc"), 1)

                def down(i, u, c, first):
                    k = i * (RING * B) + (B * u + c)
                    pe.wait_ge(S(f"{tag}_a"), k + 1)
                    mm(bank[c][:, :], flat(u)[:, len(products) * P:(len(products) + 1) * P], temp(9, 2 + c % 2),
                       start=(first and u == 0), stop=False, skip_group_check=True).then_inc(S(f"{tag}_down"), 1)

                def body(i, first):
                    for l in range(RING * B):
                        step(i, l // B, l % B, first)
                        if l:
                            down(i, (l - 1) // B, (l - 1) % B, first)
                    down(i, RING - 1, B - 1, first)
                body(0, True)
                with pe.Fori(1, UNITS // RING) as i:
                    body(i, False)
                tail()

            def finish(tag):
                for c in range(B):
                    pe.wait_ge(S(f"{tag}_accs"), c + 1)
                    to_tokens(chunk(8, c), c, bank[4 + c]).then_inc(S(f"{tag}_oT"), 1)

            pe.wait_ge(S("A_out"), B)
            ln("ln3", htok_b)
            pe.wait_ge(S("ld_b"), 32)
            route("B", EB, rt[:, 0:EB])

            def tail_b():
                for c in range(B):
                    ins = mm(bank[c][:, :], b2[:, :], flat(3)[0:EB + 1, c * T:(c + 1) * T],
                             start=False, stop=True, skip_group_check=True)
                ins.then_inc(S("B_acc"), 1)
            moe("B", EB,
                [("B_h1e", 0, "B_g", 1), ("B_h3e", 2, "B_t2", 1), ("B_h1o", 1, "B_po", 1), ("B_h3o", 3, "B_a", 1)],
                (ones, "B_t1", 0), tail_b)
            finish("B")

            pe.wait_ge(S("B_out"), B)
            ln("ln4", htok_c)
            pe.wait_ge(S("ld_qkv"), 16)
            pe.wait_ge(S("ln4_F"), B)
            for n in range(2 * HG):
                for c in range(B):
                    s = n * B + c
                    if s >= 4:
                        pe.wait_ge(S("C_pjs"), s - 3)
                    mm(bank[4 + s % 4][:, :], wqkv[:, n * P:(n + 1) * P], feat[:, c * T:(c + 1) * T],
                       start=True, stop=True).then_inc(S("C_pj"), 1)
            for t in range(NT):
                if t < 4:
                    pe.wait_ge(S("C_pjs"), 2 * HG * B - 3 + t)
                else:
                    pe.wait_ge(S("C_vs"), t - 3)
                mm(bank[4 + t % 4][:, 0:P], feat[:, t * P:(t + 1) * P], wqkv[:, 2 * HG * P:],
                   start=True, stop=True).then_inc(S("C_v"), 1)
            NTI = HG * QT
            pe.wait_ge(S("C_vs"), NT)
            with pe.Fori(0, NI) as i:
                pe.wait_ge(S("C_cur"), i * 3 + 3)

                def score(ti):
                    h, q = ti // QT, ti % QT
                    if ti >= 2:
                        pe.wait_ge(S("C_exp"), i * NTI + (ti - 1))
                    mm(bank[ti % 2][:, :], q_cur[32 * h:32 * h + 32, q * P:(q + 1) * P],
                       k_cur[32 * h:32 * h + 32, :], start=True, stop=True).then_inc(S("C_s"), 1)
                score(0)
                score(1)
                for ti in range(NTI):
                    h = ti // QT
                    pe.wait_ge(S("C_mix"), i * NTI + (ti + 1))
                    if ti >= 2:
                        pe.wait_ge(S("C_pTs"), i * NTI + (ti - 1))
                    for kc in range(QT):
                        ins = nc.tensor.transpose(bank[2 + ti % 2][:, kc * P:(kc + 1) * P],
                                                  mixed[ti % 2][:, kc * P:(kc + 1) * P], ident)
                    ins.then_inc(S("C_pT"), 1)
                    if ti + 2 < NTI:
                        score(ti + 2)
                    if ti % QT == QT - 1:
                        pe.wait_ge(S("C_pTs"), i * NTI + (ti + 1))
                        for kc in range(QT):
                            ins = mm(bank[4][32 * h:32 * h + 32, :], v_curv[:, kc, h, :], pT[h % 2][:, kc, :],
                                     start=(kc == 0), stop=(kc == QT - 1))
                        ins.then_inc(S("C_pv"), 1)
            pe.wait_ge(S("ld_wo"), 16)
            pe.wait_ge(S("C_iter"), NI + 1)
            for c in range(B):
                for g in range(HG):
                    ins = mm(bank[c][:, :], flat(0)[:, g * P:(g + 1) * P],
                             o_all[:, (g * B + c) * T:(g * B + c + 1) * T], start=(g == 0), stop=(g == HG - 1))
                ins.then_inc(S("C_ao"), 1)
            for c in range(B):
                pe.wait_ge(S("C_aos"), c + 1)
                to_tokens(chunk(12, c), c, bank[4 + c]).then_inc(S("C_aT"), 1)
            ln("ln5", htok_d)
            pe.wait_ge(S("ld_mlp"), 32)
            pe.wait_ge(S("ln5_F"), B)
            NH = HID // P

            def hidden(s):
                if s >= 2:
                    pe.wait_ge(S("C_gl"), s - 1)
                j, c = s % NH, s // NH
                mm(bank[4 + s % 2][:, :], flat(1)[:, j * P:(j + 1) * P], feat[:, c * T:(c + 1) * T],
                   start=True, stop=True).then_inc(S("C_h"), 1)
            hidden(0)
            hidden(1)
            for s in range(NH * B):
                if s + 2 < NH * B:
                    hidden(s + 2)
                j, c = s % NH, s // NH
                pe.wait_ge(S("C_gl"), s + 1)
                mm(bank[c][:, :], flat(1)[:, HID + j * P:HID + (j + 1) * P], temp(2, s % 4),
                   start=(j == 0), stop=(j == NH - 1)).then_inc(S("C_dn"), 1)
            for c in range(B):
                pe.wait_ge(S("C_mo"), c + 1)
                to_tokens(chunk(12, c), c, bank[4 + c]).then_inc(S("C_mT"), 1)

            pe.wait_ge(S("C_out"), B)
            ln("ln6", htok_b)
            route("D", ED, rt[:, EB:])

            def tail_d():
                pe.wait_ge(S("D_down"), UNITS * B)
                pe.sem_inc(S("D_acc"), 1)
            moe("D", ED, [("D_g", 0, "D_a", 2), ("D_u", 1, "D_sil", 1)], (halfsel, "D_us", 1), tail_d)
            finish("D")


_COLS = ["L0_attn_ln1_w", "L0_attn_ln1_b", "L0_attn_ln2_w", "L0_attn_ln2_b", "L0_attn_time_shift",
         "L0_attn_time_first", "L1_attn_ln1_g", "L1_attn_ln1_b", "L1_attn_ln2_g", "L1_attn_ln2_b", "L1_attn_b2"]


def kernel(**inputs):
    import numpy as np
    import concourse.bacc as bacc
    from concourse import mybir as _mybir
    from concourse.bass_utils import run_bass_kernel_spmd as run

    x = {n: np.asarray(a) for n, a in inputs.items()}
    f = np.float32

    cols = [x[n].reshape(P, 1) for n in _COLS] + [np.broadcast_to(x["L1_attn_alpha"].reshape(1, 1), (P, 1))]
    cols.append(x["L1_attn_b1"].reshape(HID // P, P).T)
    cols = np.ascontiguousarray(np.concatenate(cols, axis=1))
    eb = np.concatenate([np.concatenate([x[f"L0_ffn_{n}"], x[f"L0_ffn_s{n}"][None]]).reshape(UNITS, P, 2)
                         for n in ("b1", "b3")] + [np.eye(P, dtype=f)[:UNITS, :, None]], axis=2)
    heads = np.broadcast_to(x["L1_attn_alpha_head"].reshape(HG, 1, HG), (HG, B, HG)).reshape(-1)
    rows = np.concatenate([x["L0_ffn_gate_b"], x["L1_ffn_router_bias"], heads])
    rows = np.ascontiguousarray(np.broadcast_to(rows, (P, rows.size)))
    pairmask = np.zeros((UNITS, P, 1), f)
    cst = np.zeros((P, 2 * P + ED + P), f)
    cst[:, 0:P] = np.eye(P, dtype=f)
    for e in range(ED):
        cst[e, P + 64 * (e % 2):P + 64 * (e % 2) + 64] = 1
        pairmask[e // 2, e] = 1
    cst[ED, P:2 * P] = 1
    pairmask[UNITS - 1, ED] = 1
    cst[:, 2 * P:2 * P + ED] = np.arange(ED, 0, -1, dtype=f)
    cst[:, 2 * P + ED:] = 1
    wcv = x["L0_attn_Wcv"].T.reshape(4, P, P).transpose(1, 0, 2).reshape(P, 4 * P)
    wa = np.concatenate([x["L0_attn_Wk"].T, x["L0_attn_Wv"].T, x["L0_attn_Wr"].T, x["L0_attn_Wcr"].T,
                         x["L0_attn_Wck"].T, wcv], axis=1)

    def split(w):
        return np.concatenate([w[..., 0::2, :], w[..., 1::2, :]], axis=-2).swapaxes(-1, -2)
    routed = np.concatenate([split(x["L0_ffn_w1"]), split(x["L0_ffn_w3"]), x["L0_ffn_w2"].swapaxes(-1, -2)], axis=-1)
    shared = np.concatenate([split(x["L0_ffn_sw1"]), split(x["L0_ffn_sw3"]), x["L0_ffn_sw2"].T], axis=-1)
    wb = np.concatenate([np.concatenate([routed, shared[None]], axis=0), eb], axis=2)
    b2 = np.concatenate([x["L0_ffn_b2"], x["L0_ffn_sb2"][None]], axis=0)
    rt = np.concatenate([x["L0_ffn_gate_w"].T, x["L1_ffn_router_w"].T], axis=1)
    wqkv = x["L1_attn_w_qkv"]
    spread = [np.pad(wqkv[:, n * P:(n + 1) * P].reshape(P, HG, HG, DK), ((0, 0), (0, 0), (0, 0), (0, 32 - DK)))
              .reshape(P, HG * P) for n in range(2)]
    wqkv = np.concatenate(spread + [wqkv[:, 2 * P:]], axis=1)
    wo = np.pad(x["L1_attn_w_out"].reshape(HG, HG, DK, P), ((0, 0), (0, 0), (0, 32 - DK), (0, 0)))
    wo = wo.reshape(HG, P, P).transpose(1, 0, 2).reshape(P, HG * P)
    wm1 = x["L1_attn_w1"]
    wm2 = x["L1_attn_w2"].reshape(HID // P, P, P).transpose(1, 0, 2).reshape(P, HID)

    def pairs(w):
        return w.reshape(8, 2, P, 64).transpose(0, 2, 1, 3).reshape(8, P, P)
    routed = np.concatenate([pairs(x["L1_ffn_gate_proj"]), pairs(x["L1_ffn_up_proj"]),
                             x["L1_ffn_down_proj"].reshape(8, P, P)], axis=-1)
    shared = np.concatenate([x["L1_ffn_sh_gate"].T, x["L1_ffn_sh_up"].T, x["L1_ffn_sh_down"].T], axis=-1)
    wd = np.concatenate([np.concatenate([routed, shared[None]], axis=0), pairmask], axis=2)
    xt = x["L0_attn_x"].reshape(B, QT, P, P).transpose(0, 2, 1, 3)

    nc = bacc.Bacc("TRN2", target_bir_lowering=False, num_devices=1)
    arrays, args = {}, []
    for name, a in (("x", xt), ("cols", cols), ("rows", rows), ("cst", cst), ("wa", wa), ("wb", wb), ("b2", b2),
                    ("rt", rt), ("wqkv", wqkv), ("wo", wo), ("wm1", wm1), ("wm2", wm2), ("wd", wd)):
        a = np.ascontiguousarray(a)
        arrays[f"{name}_dram"] = a
        args.append(nc.dram_tensor(f"{name}_dram", a.shape, _mybir.dt.from_np(a.dtype), kind="ExternalInput").ap())
    args.append(nc.dram_tensor("out_dram", (B, P, QT, P), F32, kind="ExternalOutput").ap())
    build(nc, *args)
    r = run(nc, [arrays], core_ids=[0])
    got = r.results[0]["out_dram"]
    return np.ascontiguousarray(got.transpose(0, 2, 1, 3).reshape(B, T, P))
```

```python
from contextlib import ExitStack

import concourse.bass as bass
from concourse import mybir

F32 = mybir.dt.float32
ACT = mybir.ActivationFunctionType
ALU = mybir.AluOpType
AX = mybir.AxisListType.X

P = 128
B, T = 4, 512
N = B * T
NT = N // P
QT = T // P
EPS = 1e-5
EB, ED = 8, 16
UNITS = 9
RING = 3
HEADS, DK, TOPK = 16, 8, 64
HG = 4
NI = HEADS // HG * B
SCALE = DK ** -0.5
FILL = -3.0e38
G = 8
NG = HEADS * B * QT // G
WIN = 16
AIM = TOPK - WIN / 2 + 0.5
Z0 = 1.225
GAIN = (1 / 115.0, 1 / 140.0)
HID = 8 * P

COLS = ["ln1w", "ln1b", "ln2w", "ln2b", "ts", "u", "aln1g", "aln1b", "aln2g", "aln2b", "mb2", "alpha"]
C_MB1 = len(COLS)
NCOLS = C_MB1 + HID // P


class Marks:

    def __init__(self, engine, sem):
        self.engine, self.sem, self.k = engine, sem, 0

    def clear(self):
        self.engine.sem_clear(self.sem)
        self.k = 0

    def mark(self, ins):
        ins.then_inc(self.sem, 1)
        self.k += 1
        return self.k

    def need(self, k):
        self.engine.wait_ge(self.sem, k)

    def link(self, ins):
        self.need(self.mark(ins))


class Chain:

    def __init__(self, engine, sem):
        self.engine, self.sem, self.base, self.k = engine, sem, 0, 0

    def __call__(self, ins):
        ins.then_inc(self.sem, 1)
        self.k += 1
        self.engine.wait_ge(self.sem, self.base + self.k)

    def enter(self, i, per, before):
        self.base, self.k = i * per + before, 0

    def leave(self, per, total):
        assert self.k == per, self.k
        self.base, self.k = total, 0

    @property
    def total(self):
        return self.base + self.k


def ln_count(tag, c):
    return B * (int(tag[2]) - 1) + c + 1


def build(nc, x_d, cols_d, rows_d, cst_d, cstc_d, wa_d, wb_d, b2_d, rt_d, wqkv_d, wo_d, wm1_d, wm2_d, wd_d, qk_scr, o_scr, out_d):
    ctx = ExitStack()
    with ctx:
        def sb(name, shape):
            return ctx.enter_context(nc.sbuf_tensor(name, shape, F32))

        sems = {}

        def S(name):
            if name not in sems:
                sems[name] = ctx.enter_context(nc.semaphore(name))
            return sems[name]

        bank = [ctx.enter_context(nc.psum_tensor(f"bank{i}", [P, 512], F32)) for i in range(8)]
        SLOT = B * (T + 1)
        NSLOT = 17
        arena = sb("arena", [P, NSLOT * SLOT])

        def flat(n, w=N):
            return arena[:, n * SLOT:n * SLOT + w]

        def seq(n):
            return flat(n, SLOT).rearrange("p (b t) -> p b t", b=B)

        def bt(n):
            return flat(n).rearrange("p (b t) -> p b t", b=B)

        cols = sb("cols", [P, NCOLS])
        rows = sb("rows", [P, EB + ED + NG * 2 * G])
        cst = sb("cst", [P, cst_d.shape[1]])
        ident = cst[:, 0:P]
        halfsel = cst[0:ED + 1, P:2 * P]
        rank = cst[:, 2 * P:2 * P + ED]
        ones = cst[0:EB + 1, 2 * P + ED:]
        xres = sb("xres", [P, NT, P])
        ytok = sb("ytok", [P, NT, P])
        feat = sb("feat", [P, N])
        stats = sb("stats", [P, NT, 6])
        mv = sb("mv", [P, NT, 2])
        rstd = sb("rstd", [P, 2, NT])
        shiftc = sb("shiftc", [P, 4])
        small = sb("small", [P, 8, NT])
        rt = sb("rt", [P, EB + ED])
        b2 = sb("b2", [EB + 1, P])

        def col(name):
            n = COLS.index(name)
            return cols[:, n:n + 1]

        WA = 16
        wk, wv, wr, wcr = (flat(WA)[:, n * P:(n + 1) * P] for n in range(4))
        wck = flat(WA)[:, 4 * P:8 * P]
        wcv = flat(WA)[:, 8 * P:12 * P]
        htok = flat(0).rearrange("p (t c) -> p t c", t=NT)
        htok_b = htok_c = flat(12).rearrange("p (t c) -> p t c", t=NT)
        htok_d = flat(3).rearrange("p (t c) -> p t c", t=NT)
        def temp(slot, n):
            return flat(slot)[:, n * T:(n + 1) * T]
        V_ALL = 12
        qc, kc_, oc = flat(13), flat(14), flat(2)
        v_all = flat(V_ALL)
        q_cur, k_cur, v_cur, o_cur = (temp(15, n) for n in range(4))
        v_curv = v_cur.rearrange("p (k h c) -> p k h c", k=QT, h=HG)
        score = [arena[:, n * G * T:(n + 1) * G * T].rearrange("p (j t) -> p j t", j=G) for n in range(2)]
        prob = [arena[:, n * G * T:(n + 1) * G * T].rearrange("p (j t) -> p j t", j=G) for n in range(2, 4)]
        sparse = arena[:, 4 * G * T:5 * G * T].rearrange("p (j t) -> p j t", j=G)
        assert 5 * G * T <= 11 * SLOT
        work = [temp(13, n) for n in range(4)]
        slow = temp(16, 3)
        junk = [temp(14, n) for n in range(4)]
        cstc = sb("cstc", [P, P + HEADS + WIN + 1])
        blockmask, headsel = cstc[:, 0:P], cstc[:, P:P + HEADS]
        places, onescol = cstc[:, P + HEADS:P + HEADS + WIN], cstc[:, P + HEADS + WIN:]
        wqkv = flat(16)[:, 0:3 * P]
        pT = [sb(f"pT{n}", [P, QT, T]) for n in range(2)]
        hi = sb("hi", [P, 8])
        sig_all = sb("sig_all", [P, NG * G])
        gates = sb("gates", [P, NG * 2 * G])
        ksum = sb("ksum", [P, B])
        rmax = sb("rmax", [P, 2, G])
        nmax = sb("nmax", [P, 2, G])
        nthr = sb("nthr", [P, 2, G])
        cnt = sb("cnt", [P, 2, G])
        zz = sb("zz", [P, 2, 2 * G])
        cc = sb("cc", [P, 2, 2 * G])
        sg = sb("sg", [P, 2, G])
        step_ = sb("step_", [P, G])
        cand = sb("cand", [P, G, WIN + 1])
        hit = sb("hit", [P, 3, G * WIN])
        thr = sb("thr", [P, 4, G])
        flags = sb("flags", [1, G + 1])

        block = ctx.enter_context(nc.Block())

        WU = {"B": (wb_d, 5 * P + 5), "D": (wd_d, 3 * P + 1)}

        @block.sync
        def _(sp):
            sp.dma_start(cst[:, :], cst_d).then_inc(S("ld_const"), 16)
            sp.dma_start(cols[:, :], cols_d).then_inc(S("ld_const"), 16)
            sp.dma_start(rows[:, :], rows_d).then_inc(S("ld_const"), 16)
            for b in range(B):
                sp.dma_start(xres[:, QT * b:QT * (b + 1), :], x_d[b]).then_inc(S(f"ld_x{b}"), 16)
            sp.dma_start(flat(WA)[:, 0:12 * P], wa_d).then_inc(S("ld_wa"), 16)
            sp.dma_start(rt[:, :], rt_d).then_inc(S("ld_b"), 16)
            sp.dma_start(b2[:, :], b2_d).then_inc(S("ld_b"), 16)

            def moe_weights(tag, free):
                src, w = WU[tag]
                for u in range(RING):
                    sp.dma_start(flat(u)[:, 0:w], src[u]).then_inc(S(f"{tag}_w{u}"), 16)
                with sp.Fori(1, UNITS // RING) as i:
                    for u in range(RING):
                        sp.wait_ge(S(f"{tag}_down"), i * (RING * B) - (RING * B) + B * (u + 1))
                        sp.dma_start(flat(u)[:, 0:w],
                                     src[bass.ds(i * RING + u, 1), :, :].rearrange("a p n -> p (a n)")
                                     ).then_inc(S(f"{tag}_w{u}"), 16)

            sp.wait_ge(S("A_out"), B)
            moe_weights("B", None)
            sp.wait_ge(S("B_out"), B)
            sp.dma_start(wqkv, wqkv_d).then_inc(S("ld_qkv"), 16)
            sp.dma_start(cstc[:, :], cstc_d).then_inc(S("ld_qkv"), 16)
            for n, (src, ready) in enumerate(((qc, "C_q"), (kc_, "C_kc"))):
                sp.wait_ge(S(ready), B)
                for g in range(HG):
                    sp.dma_start(qk_scr[n, B * g:B * (g + 1)].rearrange("b r t -> r b t"),
                                 src[32 * g:32 * g + 32, :].rearrange("p (b t) -> p b t", b=B)
                                 ).then_inc(S("C_qkout"), 16)
            sp.wait_ge(S("C_qkout"), 16 * 2 * HG)

            def load_qk(i, dyn):
                for n, dst in enumerate((q_cur, k_cur)):
                    for h in range(HG):
                        if dyn:
                            src = qk_scr[n][bass.ds(i, 1), DK * h:DK * (h + 1), :].rearrange("a r t -> (a r) t")
                        else:
                            src = qk_scr[n, i, DK * h:DK * (h + 1), :]
                        sp.dma_start(dst[32 * h:32 * h + DK, :], src).then_inc(S("C_qk"), 16)

            def store_o(i, dyn):
                sp.wait_ge(S("C_o"), i + 2)
                for h in range(HG):
                    if dyn:
                        dst = o_scr[bass.ds(i, 1), DK * h:DK * (h + 1), :].rearrange("a r t -> (a r) t")
                    else:
                        dst = o_scr[i, DK * h:DK * (h + 1), :]
                    sp.dma_start(dst, o_cur[32 * h:32 * h + DK, :]).then_inc(S("C_od"), 16)
                sp.wait_ge(S("C_od"), i * 64 + 64)
                sp.sem_inc(S("C_osent"), 1)
            sp.sem_inc(S("C_osent"), 1)
            load_qk(0, False)
            sp.wait_ge(S("C_s"), 2 * G)
            load_qk(1, False)
            with sp.Fori(1, NI - 1) as i:
                sp.wait_ge(S("C_s"), i * (2 * G) + 2 * G)
                load_qk(i + 1, True)
                store_o(i - 1, True)
            store_o(NI - 2, False)
            store_o(NI - 1, False)
            for g in range(HG):
                sp.dma_start(oc[32 * g:32 * g + 32, :].rearrange("p (b t) -> p b t", b=B),
                             o_scr[B * g:B * (g + 1)].rearrange("b r t -> r b t")).then_inc(S("ld_o"), 16)
            sp.dma_start(flat(0)[:, 0:P], wo_d).then_inc(S("ld_wo"), 16)
            sp.dma_start(flat(1)[:, 0:HID], wm1_d).then_inc(S("ld_mlp"), 16)
            sp.dma_start(flat(1)[:, HID:2 * HID], wm2_d).then_inc(S("ld_mlp"), 16)
            sp.wait_ge(S("C_out"), B)
            moe_weights("D", None)
            for b in range(B):
                sp.wait_ge(S("D_out"), b + 1)
                sp.dma_start(out_d[b], xres[:, QT * b:QT * (b + 1), :]).then_inc(S("stored"), 16)
            sp.wait_ge(S("stored"), 16 * B)

        @block.gpsimd
        def _(gp):
            def masks(tag, rows_n, at, cwT):
                gp.wait_ge(S(f"{tag}_cwT"), B)

                def unit(i, u, first):
                    gp.wait_ge(S(f"{tag}_w{u}"), i * 16 + 16)
                    gp.sem_inc(S("gp_passed"), 1)
                    for c in range(B):
                        if not (first and u == 0 and c < 2):
                            k = i * (RING * B) + (B * u + c)
                            gp.wait_ge(S(f"{tag}_bc"), k - 1)
                            gp.sem_inc(S("gp_passed"), 1)
                        gp.tensor_scalar(temp(4, c % 2)[0:rows_n, :], cwT[0:rows_n, c * T:(c + 1) * T],
                                         flat(u)[0:rows_n, at:at + 1], None, ALU.mult).then_inc(S(f"{tag}_msk"), 1)

                for u in range(RING):
                    unit(0, u, True)
                with gp.Fori(1, UNITS // RING) as i:
                    for u in range(RING):
                        unit(i, u, False)

            gp.wait_ge(S("ld_const"), 48)
            masks("B", EB + 1, 5 * P + 4, flat(3))
            gp.wait_ge(S("C_qkv"), 1)
            gp.memset(v_cur, 0.0).then_inc(S("gp_self"), 1)
            gp.wait_ge(S("gp_self"), 1)
            me = Marks(gp, S("gp_loop"))

            def value(i):
                gp.wait_ge(S("C_pv"), i * HG + 2)
                gp.sem_inc(S("gp_passed"), 1)
                src = v_all[:, i * P:(i + 1) * P] if isinstance(i, int) else v_all[:, bass.ds(i * P, P)]
                gp.tensor_copy(v_cur.rearrange("p (a c) -> p a c", c=32)[:, :, 0:DK],
                               src.rearrange("p (a c) -> p a c", c=DK)).then_inc(S("C_v"), 1)

            def mix(n, s):
                gp.wait_ge(S("C_cc"), n + 1)
                gp.sem_inc(S("gp_passed"), 1)
                last = None
                for j in range(G + 1):
                    if j < G:
                        gp.tensor_scalar(prob[s][:, j, :], prob[s][:, j, :], cc[:, s, j:j + 1], 1.0, ALU.mult, ALU.mult)
                        new = me.mark(gp.tensor_scalar(sparse[:, j, :], sparse[:, j, :], cc[:, s, G + j:G + j + 1],
                                                       1.0, ALU.mult, ALU.mult))
                    if j:
                        me.need(last)
                        gp.tensor_tensor(sparse[:, j - 1, :], sparse[:, j - 1, :], prob[s][:, j - 1, :],
                                         ALU.add).then_inc(S("C_mix"), 1)
                    last = new

            def body(i):
                me.clear()
                mix(2 * (i - 1) + 0 if isinstance(i, int) else (i - 1) * 2, 0)
                value(i - 1)
                mix(2 * (i - 1) + 1 if isinstance(i, int) else (i - 1) * 2 + 1, 1)
            with gp.Fori(1, NI) as i:
                body(i)
            body(NI)
            masks("D", ED + 1, 3 * P, flat(3))

        @block.scalar
        def _(act):
            def ln(tag, dst, w=None, b=None):
                act.wait_ge(S("ln_var"), int(tag[2]))
                act.activation(rstd[:, :, :], rstd[:, :, :], ACT.Sqrt).then_inc(S("ln_std"), 1)
                for c in range(B):
                    act.wait_ge(S("ln_T"), ln_count(tag, c))
                    if w is None:
                        act.activation(dst[:, c * T:(c + 1) * T], bank[c][:, :], ACT.Copy).then_inc(S("ln_F"), 1)
                    else:
                        act.activation(dst[:, c * T:(c + 1) * T], bank[c][:, :], ACT.Identity,
                                       bias=b, scale=w).then_inc(S("ln_F"), 1)

            def chunk(n, c):
                return flat(n)[:, c * T:(c + 1) * T]

            act.wait_ge(S("ld_const"), 48)
            ln("ln1", feat, col("ln1w"), col("ln1b"))
            for c in range(B):
                act.wait_ge(S("A_kv"), c + 1)
                act.activation(chunk(1, c), bank[c][:, :], ACT.Copy).then_inc(S("A_kvs"), 1)
                act.activation(chunk(2, c), bank[4 + c][:, :], ACT.Copy).then_inc(S("A_kvs"), 1)
            for n, s in ((6, "A_gx"), (7, "A_bx"), (8, "A_e1x"), (9, "A_e2x")):
                act.wait_ge(S(s), 1)
                act.activation(bt(n), bt(n), ACT.Exp).then_inc(S("A_exps"), 1)
            for c in range(B):
                act.wait_ge(S("A_r"), c + 1)
                act.activation(chunk(3, c), bank[c][:, :], ACT.Sigmoid).then_inc(S("A_rs"), 1)
            ln("ln2", feat, col("ln2w"), col("ln2b"))
            for c in range(B):
                act.wait_ge(S("A_rc"), c + 1)
                act.activation(chunk(3, c), bank[c][:, :], ACT.Sigmoid).then_inc(S("A_rcs"), 1)
            for s in range(B * 4):
                act.wait_ge(S("A_kc"), s + 1)
                if s >= 4:
                    act.wait_ge(S("A_sq"), s - 3)
                act.activation(temp(4, s % 4), bank[4 + s % 2][:, :], ACT.Relu).then_inc(S("A_rl"), 1)

            def route(tag, ln_tag, ne):
                act.wait_ge(S(f"{tag}_ex"), 1)
                act.activation(flat(5)[:, 0:NT * ne], flat(5)[:, 0:NT * ne], ACT.Exp).then_inc(S(f"{tag}_exp"), 1)
                for c in range(B):
                    act.wait_ge(S(f"{tag}_cwTp"), c + 1)
                    act.activation(flat(3)[0:ne + 1, c * T:(c + 1) * T], bank[4 + c][0:ne + 1, :],
                                   ACT.Copy).then_inc(S(f"{tag}_cwT"), 1)

            def acc_out(tag):
                for c in range(B):
                    act.wait_ge(S(f"{tag}_acc"), 1)
                    act.activation(chunk(8, c), bank[c][:, :], ACT.Copy).then_inc(S(f"{tag}_accs"), 1)

            ln("ln3", feat)
            route("B", "ln3", EB)

            def unit_b(i, u, first):
                for c in range(B):
                    k = i * (RING * B) + (B * u + c)

                    def bias(n):
                        return flat(u)[:, 5 * P + n:5 * P + n + 1]
                    act.wait_ge(S("B_h1e"), k + 1)
                    act.activation(temp(5, c % 2), bank[4 + (5 * c) % 4][:, :], ACT.Identity,
                                   bias=bias(0)).then_inc(S("B_t1"), 1)
                    act.wait_ge(S("B_h1o"), k + 1)
                    act.activation(temp(5, 2 + c % 2), bank[4 + (5 * c + 2) % 4][:, :], ACT.Identity,
                                   bias=bias(1)).then_inc(S("B_t2"), 1)
                    act.wait_ge(S("B_g"), k + 1)
                    act.activation(temp(6, c % 2), temp(6, 2 + c % 2), ACT.Sigmoid,
                                   scale=1.702).then_inc(S("B_sg"), 1)
            for u in range(RING):
                unit_b(0, u, True)
            with act.Fori(1, UNITS // RING) as i:
                for u in range(RING):
                    unit_b(i, u, False)
            acc_out("B")

            act.activation(gates[:, :], rows[:, EB + ED:], ACT.Sigmoid).then_inc(S("C_gate"), 1)
            ln("ln4", feat, col("aln1g"), col("aln1b"))
            for c in range(B):
                act.wait_ge(S("C_pq"), c + 1)
                act.activation(chunk(13, c), bank[4 + c][:, :], ACT.Copy).then_inc(S("C_q"), 1)
            for c in range(B):
                act.wait_ge(S("C_pk"), c + 1)
                act.activation(chunk(14, c), bank[c][:, :], ACT.Identity,
                               accum_out=ksum[:, c:c + 1]).then_inc(S("C_k"), 1)
            va = v_all.rearrange("p (g t c) -> p g t c", g=HG, t=NT)
            for t in range(NT):
                act.wait_ge(S("C_v"), t + 1)
                act.activation(va[:, :, t, :], bank[4 + t % 4][:, 0:P].rearrange("p (g c) -> p g c", g=HG),
                               ACT.Copy).then_inc(S("C_vs"), 1)
            for c in range(B):
                act.wait_ge(S("C_kT"), c + 1)
                act.activation(chunk(0, c), bank[c][:, :], ACT.Copy).then_inc(S("C_ktok"), 1)
            act.wait_ge(S("C_var"), 1)
            sv = sig_all[:, :].rearrange("p (g b h q) -> p g b h q", g=HG, b=B, h=HG)
            for c in range(B):
                for q in range(QT):
                    src = bank[6][:, (c * QT + q) * HEADS:(c * QT + q + 1) * HEADS]
                    ins = act.activation(sv[:, :, c, :, q], src.rearrange("p (g h) -> p g h", g=HG), ACT.Sqrt)
            ins.then_inc(S("C_sig"), 1)
            act.wait_ge(S("C_vs"), NT)
            act.wait_ge(S("C_q"), B)
            act.sem_inc(S("C_qkv"), 1)
            act.sem_inc(S("C_o"), 1)
            act.sem_inc(S("C_pTs"), 2)

            def count(n, s, j, done, first=False):
                if j >= 4:
                    act.wait_ge(S(done), n * G + j - 3)
                elif done == "C_c1" and not first:
                    act.wait_ge(S("C_c3"), n * G + j - 3)
                act.activation(junk[j % 4], score[s][:, j, :], ACT.Sign, bias=nthr[:, s, j:j + 1],
                               accum_out=cnt[:, s, j:j + 1]).then_inc(S(done), 1)

            def exp(n, s, j):
                if j == 0:
                    act.wait_ge(S("C_nm"), n + 1)
                act.activation(prob[s][:, j, :], score[s][:, j, :], ACT.Exp, bias=nmax[:, s, j:j + 1],
                               scale=SCALE, accum_out=zz[:, s, j:j + 1]).then_inc(S("C_exp"), 1)

            def pt_out(n, j):
                act.wait_ge(S("C_pT"), n * G + j + 1)
                if j % QT == 0:
                    act.wait_ge(S("C_pv"), n * 2 + j // QT + 1)
                q = j % QT
                act.activation(pT[j // QT][:, :, q * P:(q + 1) * P],
                               bank[5 + j % 2][:, :].rearrange("p (k q) -> p k q", k=QT),
                               ACT.Copy).then_inc(S("C_pTs"), 1)

            def step(i, s, cur, prev, old):
                n = 2 * i + s if isinstance(i, int) else i * 2 + s
                for j in range(G):
                    if cur:
                        act.wait_ge(S("C_take"), n * G + j + 1)
                        count(n, s, j, "C_c1", first=isinstance(n, int) and n == 0)
                for j in range(G):
                    if prev:
                        exp(n - 1, 1 - s, j)
                    if old and j in (2, 4, 6):
                        pt_out(n - 2, j // 2 - 1)
                if cur:
                    act.wait_ge(S("C_n1"), n + 1)
                for j in range(G):
                    if cur:
                        count(n, s, j, "C_c2")
                    if old and j in (1, 4, 7):
                        pt_out(n - 2, 3 + j // 3)
                if cur:
                    act.wait_ge(S("C_n2"), n + 1)
                for j in range(G):
                    if old and j in (0, 3):
                        pt_out(n - 2, 6 + j // 3)
                    if cur:
                        count(n, s, j, "C_c3")

            def out_done(i):
                act.wait_ge(S("C_pv"), i * HG + HG + 2)
                act.wait_ge(S("C_osent"), i + 1)
                act.activation(o_cur, bank[4][:, :], ACT.Copy).then_inc(S("C_o"), 1)
            step(0, 0, True, False, False)
            step(0, 1, True, True, False)
            with act.Fori(1, NI) as i:
                step(i, 0, True, True, True)
                step(i, 1, True, True, True)
                out_done(i - 1)
            step(NI, 0, False, True, True)
            step(NI, 1, False, False, True)
            out_done(NI - 1)

            for c in range(B):
                act.wait_ge(S("C_ao"), c + 1)
                act.activation(chunk(12, c), bank[c][:, :], ACT.Copy).then_inc(S("C_aos"), 1)
            ln("ln5", feat, col("aln2g"), col("aln2b"))
            for c in range(B):
                for j in range(HID // P):
                    s = c * (HID // P) + j
                    act.wait_ge(S("C_h"), s + 1)
                    if s >= 4:
                        act.wait_ge(S("C_dn"), s - 3)
                    act.activation(temp(2, s % 4), bank[4 + s % 2][:, :], ACT.Gelu,
                                   bias=cols[:, C_MB1 + j:C_MB1 + j + 1]).then_inc(S("C_gl"), 1)
                act.wait_ge(S("C_dn"), (c + 1) * (HID // P))
                act.activation(chunk(12, c), bank[c][:, :], ACT.Identity, bias=col("mb2")).then_inc(S("C_mo"), 1)

            ln("ln6", feat)
            route("D", "ln6", ED)

            def unit_d(i, u, first):
                for c in range(B):
                    k = i * (RING * B) + (B * u + c)
                    act.wait_ge(S("D_g"), k + 1)
                    act.activation(temp(5, c % 2), bank[4 + (3 * c) % 4][:, :], ACT.Silu).then_inc(S("D_sil"), 1)
            for u in range(RING):
                unit_d(0, u, True)
            with act.Fori(1, UNITS // RING) as i:
                for u in range(RING):
                    unit_d(i, u, False)
            acc_out("D")

        @block.vector
        def _(dve):
            link = Chain(dve, S("dve_self"))
            v = nc.vector

            def ln(tag, src, dst, double, dst_y=None):
                for t in range(NT):
                    if tag == "ln1" and t % QT == 0:
                        dve.wait_ge(S(f"ld_x{t // QT}"), 16)
                    ins = v.bn_stats(stats[:, t, :], src[:, t, :])
                link(ins)
                for t in range(NT):
                    ins = v.bn_aggr(mv[:, t, :], stats[:, t, :])
                link(ins)
                v.tensor_scalar(rstd[:, 0, :], mv[:, :, 1], EPS, None, ALU.add)
                v.tensor_scalar(rstd[:, 1, :], mv[:, :, 1], 1.0 + EPS, EPS * EPS, ALU.mult,
                                ALU.add).then_inc(S("ln_var"), 1)
                dve.wait_ge(S("ln_std"), int(tag[2]))
                link(v.reciprocal(rstd[:, :, :], rstd[:, :, :]))
                r = 1 if double else 0
                for t in range(NT):
                    if dst_y is not None:
                        v.tensor_scalar(dst_y[:, t, :], src[:, t, :], mv[:, t, 0:1], rstd[:, 0, t:t + 1],
                                        ALU.subtract, ALU.mult)
                    ins = v.tensor_scalar(dst[:, t, :], src[:, t, :], mv[:, t, 0:1], rstd[:, r, t:t + 1],
                                          ALU.subtract, ALU.mult)
                    if t % QT == QT - 1:
                        ins.then_inc(S("ln_norm"), 1)

            def tok(x, c):
                return x[:, QT * c:QT * (c + 1), :].rearrange("p t c -> p (t c)")

            def chunk(n, c):
                return flat(n)[:, c * T:(c + 1) * T]

            dve.wait_ge(S("ld_const"), 48)
            ln("ln1", xres, htok, True, ytok)
            ts = col("ts")
            v.tensor_scalar(shiftc[:, 0:1], ts, 1.0, None, ALU.add)
            link(v.tensor_scalar(shiftc[:, 1:2], ts, -1.0, None, ALU.mult))
            v.tensor_tensor(shiftc[:, 2:3], shiftc[:, 1:2], ts, ALU.mult)
            link(v.tensor_scalar(shiftc[:, 3:4], shiftc[:, 1:2], 1.0, None, ALU.add))
            K_, V_, R_, M_, D_, AA = 1, 2, 3, 4, 5, 10
            G_, B_, E1, E2, MX, BE, X_, TMP = 6, 7, 8, 9, 11, 12, 13, 14
            v.memset(seq(M_)[:, :, 0:1], 0.0)
            v.memset(seq(D_)[:, :, 0:1], 1.0)
            v.memset(seq(AA)[:, :, 0:1], 0.0)
            for c in range(B):
                dve.wait_ge(S("ln_F"), ln_count("ln1", c))
                h = feat[:, c * T:(c + 1) * T]
                link(v.tensor_scalar(chunk(TMP, c), h, shiftc[:, 0:1], None, ALU.mult))
                v.tensor_scalar(chunk(X_, c)[:, 0:1], chunk(TMP, c)[:, 0:1], shiftc[:, 2:3], None, ALU.add)
                v.scalar_tensor_tensor(chunk(X_, c)[:, 1:T], h[:, 0:T - 1], shiftc[:, 1:2],
                                       chunk(TMP, c)[:, 1:T], ALU.mult, ALU.add).then_inc(S("A_xxx"), 1)
            dve.wait_ge(S("A_kvs"), 2 * B)
            for c in range(B):
                ins = v.tensor_tensor_scan(seq(M_)[:, c, 1:], chunk(K_, c), chunk(K_, c), 0.0, ALU.max, ALU.max)
            link(ins)
            mprev, mcur = seq(M_)[:, :, 0:T], seq(M_)[:, :, 1:]
            v.tensor_tensor(bt(G_), mprev, mcur, ALU.subtract).then_inc(S("A_gx"), 1)
            v.tensor_tensor(bt(B_), bt(K_), mcur, ALU.subtract).then_inc(S("A_bx"), 1)
            link(v.scalar_tensor_tensor(bt(MX), bt(K_), col("u"), mprev, ALU.add, ALU.max))
            v.tensor_tensor(bt(E1), mprev, bt(MX), ALU.subtract).then_inc(S("A_e1x"), 1)
            v.scalar_tensor_tensor(bt(E2), bt(K_), col("u"), bt(MX), ALU.add, ALU.subtract).then_inc(S("A_e2x"), 1)
            dve.wait_ge(S("A_exps"), 2)
            for c in range(B):
                ins = v.tensor_tensor_scan(seq(D_)[:, c, 1:], chunk(G_, c), chunk(B_, c), 1.0, ALU.mult, ALU.add)
            link(ins)
            dprev = seq(D_)[:, :, 0:T]
            link(v.tensor_tensor(bt(G_), bt(G_), dprev, ALU.mult))
            link(v.tensor_tensor(bt(MX), bt(G_), bt(B_), ALU.max))
            link(v.reciprocal(bt(MX), bt(MX)))
            v.tensor_tensor(bt(G_), bt(G_), bt(MX), ALU.mult)
            link(v.tensor_tensor(bt(B_), bt(B_), bt(MX), ALU.mult))
            link(v.tensor_tensor(bt(B_), bt(B_), bt(V_), ALU.mult))
            for c in range(B):
                ins = v.tensor_tensor_scan(seq(AA)[:, c, 1:], chunk(G_, c), chunk(B_, c), 0.0, ALU.mult, ALU.add)
            link(ins)
            aprev = seq(AA)[:, :, 0:T]
            dve.wait_ge(S("A_exps"), 4)
            link(v.tensor_tensor(bt(E1), bt(E1), dprev, ALU.mult))
            v.tensor_tensor(bt(MX), bt(E1), bt(E2), ALU.add)
            v.tensor_tensor(bt(E1), bt(E1), aprev, ALU.mult)
            link(v.tensor_tensor(bt(E2), bt(E2), bt(V_), ALU.mult))
            v.reciprocal(bt(MX), bt(MX))
            link(v.tensor_tensor(bt(E1), bt(E1), bt(E2), ALU.add))
            link(v.tensor_tensor(bt(E1), bt(E1), bt(MX), ALU.mult))
            dve.wait_ge(S("A_rs"), B)
            v.tensor_tensor(bt(E1), bt(E1), bt(R_), ALU.mult).then_inc(S("A_z"), 1)
            for c in range(B):
                dve.wait_ge(S("A_zT"), c + 1)
                ins = v.tensor_tensor(tok(ytok, c), tok(ytok, c), bank[c][:, :], ALU.add)
            link(ins)
            link(v.tensor_tensor(xres[:, :, :], xres[:, :, :], ytok[:, :, :], ALU.add))
            ln("ln2", ytok, htok, False)
            for c in range(B):
                dve.wait_ge(S("ln_F"), ln_count("ln2", c))
                h = feat[:, c * T:(c + 1) * T]
                link(v.tensor_scalar(chunk(TMP, c), h, shiftc[:, 3:4], None, ALU.mult))
                v.scalar_tensor_tensor(chunk(X_, c)[:, 0:1], h[:, T - 1:T], ts,
                                       chunk(TMP, c)[:, 0:1], ALU.mult, ALU.add)
                v.scalar_tensor_tensor(chunk(X_, c)[:, 1:T], h[:, 0:T - 1], ts,
                                       chunk(TMP, c)[:, 1:T], ALU.mult, ALU.add).then_inc(S("A_xx2"), 1)
            dve.wait_ge(S("A_rcs"), B)
            for c in range(B):
                for j in range(4):
                    s = 4 * c + j
                    dve.wait_ge(S("A_rl"), s + 1)
                    if s >= 4:
                        dve.wait_ge(S("A_vv"), s - 3)
                    v.tensor_tensor(temp(5, s % 4), temp(4, s % 4), temp(4, s % 4), ALU.mult).then_inc(S("A_sq"), 1)
                dve.wait_ge(S("A_vv"), 4 * (c + 1))
                v.tensor_tensor(chunk(7, c), chunk(3, c), bank[6 + c % 2][:, :], ALU.mult).then_inc(S("A_vz"), 1)
            for c in range(B):
                dve.wait_ge(S("A_vT"), c + 1)
                ins = v.tensor_tensor(tok(xres, c), tok(xres, c), bank[c][:, :], ALU.add)
                ins.then_inc(S("A_out"), 1)
            dve.wait_ge(S("A_out"), B)

            def route(tag, ne, soft):
                def e3(n):
                    return flat(n)[:, 0:NT * ne].rearrange("p (t e) -> p t e", e=ne)

                def e2(n):
                    return flat(n)[:, 0:NT * ne]

                def wide(a):
                    return a.unsqueeze(2).broadcast_to([P, NT, ne])

                def over(row):
                    return row.unsqueeze(1).broadcast_to([P, NT, ne])
                logits, bias = bank[4][:, 0:NT * ne].rearrange("p (t e) -> p t e", e=ne), \
                    over(rows[:, 0:EB] if tag == "B" else rows[:, EB:EB + ED])
                rk = over(rank[:, ED - ne:])
                EX, BI, EQ, OH, CW = 5, 6, 7, 9, 10
                m, s = small[:, 0, :], small[:, 1, :]
                dve.wait_ge(S(f"{tag}_lg"), 1)
                if soft:
                    link(v.tensor_reduce(m, logits, AX, ALU.max))
                    v.tensor_tensor(e3(EX), logits, wide(m), ALU.subtract).then_inc(S(f"{tag}_ex"), 1)
                    dve.wait_ge(S(f"{tag}_exp"), 1)
                    link(v.tensor_reduce(s, e3(EX), AX, ALU.add))
                    link(v.reciprocal(s, s))
                    link(v.tensor_tensor(e3(EX), e3(EX), wide(s), ALU.mult))
                    link(v.tensor_tensor(e3(BI), e3(EX), bias, ALU.add))
                else:
                    link(v.tensor_tensor(e3(BI), logits, bias, ALU.add))
                for r in range(2):
                    mx = small[:, 2 + r, :]
                    link(v.tensor_reduce(mx, e3(BI), AX, ALU.max))
                    link(v.tensor_tensor(e3(EQ), e3(BI), wide(mx), ALU.is_equal))
                    link(v.tensor_tensor(e3(EQ), e3(EQ), rk, ALU.mult))
                    link(v.tensor_reduce(small[:, 4, :], e3(EQ), AX, ALU.max))
                    link(v.tensor_tensor(e3(OH + 2 * r), rk, wide(small[:, 4, :]), ALU.is_equal))
                    if r == 0:
                        link(v.scalar_tensor_tensor(e2(BI), e2(OH), FILL, e2(BI), ALU.mult, ALU.add))
                cw = flat(CW)[:, 0:NT * (ne + 1)].rearrange("p (t e) -> p t e", e=ne + 1)
                link(v.memset(cw[:, :, ne:], 1.0))
                if soft:
                    link(v.tensor_tensor(e2(OH), e2(OH), e2(OH + 2), ALU.add))
                    v.tensor_tensor(cw[:, :, 0:ne], e3(EX), e3(OH), ALU.mult).then_inc(S(f"{tag}_cw"), 1)
                else:
                    v.tensor_tensor(flat(EX)[:, 0:NT], small[:, 3, :], small[:, 2, :],
                                    ALU.subtract)
                    v.memset(flat(EX)[:, NT:NT * ne], 0.0).then_inc(S(f"{tag}_ex"), 1)
                    dve.wait_ge(S(f"{tag}_exp"), 1)
                    ex = flat(EX)[:, 0:NT]
                    link(v.tensor_scalar(s, ex, 1.0, None, ALU.add))
                    link(v.reciprocal(s, s))
                    link(v.tensor_tensor(m, ex, s, ALU.mult))
                    v.tensor_tensor(e3(OH), e3(OH), wide(s), ALU.mult)
                    link(v.tensor_tensor(e3(OH + 2), e3(OH + 2), wide(m), ALU.mult))
                    v.tensor_tensor(cw[:, :, 0:ne], e3(OH), e3(OH + 2), ALU.add).then_inc(S(f"{tag}_cw"), 1)

            def add_back(tag):
                for c in range(B):
                    dve.wait_ge(S(f"{tag}_oT"), c + 1)
                    v.tensor_tensor(tok(xres, c), tok(xres, c), bank[4 + c][:, :], ALU.add).then_inc(S(f"{tag}_out"), 1)
                dve.wait_ge(S(f"{tag}_out"), B)

            ln("ln3", xres, htok_b, False)
            route("B", EB, True)

            def unit_b(i, u, first):
                for c in range(B):
                    k = i * (RING * B) + (B * u + c)

                    def bias(n):
                        return flat(u)[:, 5 * P + n:5 * P + n + 1]
                    dve.wait_ge(S("B_h3e"), k + 1)
                    dve.wait_ge(S("B_t1"), k + 1)
                    link(v.scalar_tensor_tensor(temp(7, c % 2), bank[4 + (5 * c + 1) % 4][:, :], bias(2),
                                                temp(5, c % 2), ALU.add, ALU.mult))
                    v.tensor_scalar(temp(6, 2 + c % 2), temp(7, c % 2), 7.0, None, ALU.min).then_inc(S("B_g"), 1)
                    dve.wait_ge(S("B_h3o"), k + 1)
                    dve.wait_ge(S("B_t2"), k + 1)
                    v.scalar_tensor_tensor(temp(7, 2 + c % 2), bank[4 + (5 * c + 3) % 4][:, :], bias(3),
                                           temp(5, 2 + c % 2), ALU.add, ALU.mult).then_inc(S("B_po"), 1)
                    dve.wait_ge(S("B_po"), k + 1)
                    link(v.tensor_scalar(temp(7, 2 + c % 2), temp(7, 2 + c % 2), 7.0, -7.0, ALU.min, ALU.max))
                    link(v.scalar_tensor_tensor(temp(9, c % 2), temp(7, 2 + c % 2), 1.0, temp(6, 2 + c % 2),
                                                ALU.add, ALU.mult))
                    dve.wait_ge(S("B_sg"), k + 1)
                    link(v.tensor_tensor(temp(9, c % 2), temp(9, c % 2), temp(6, c % 2), ALU.mult))
                    if not (first and u == 0 and c < 2):
                        dve.wait_ge(S("B_down"), k - 1)
                    dve.wait_ge(S("B_bc"), k + 1)
                    v.tensor_tensor(temp(9, 2 + c % 2), temp(9, c % 2), bank[4 + (5 * c + 4) % 4][:, :],
                                    ALU.mult).then_inc(S("B_a"), 1)
            per = RING * B * 4
            for u in range(RING):
                unit_b(0, u, True)
            before = link.total
            with dve.Fori(1, UNITS // RING) as i:
                link.enter(i, per, before - per)
                for u in range(RING):
                    unit_b(i, u, False)
                link.leave(per, before + per * (UNITS // RING - 1))
            add_back("B")

            ln("ln4", xres, htok_c, True, ytok)
            dve.wait_ge(S("C_gate"), 1)
            gv = gates[:, :].rearrange("p (n k) -> p n k", k=2 * G)[:, :, G:]
            v.tensor_scalar(gv, gv, -1.0, 1.0, ALU.mult, ALU.add)
            dve.wait_ge(S("C_k"), B)
            link(v.tensor_scalar(ksum[:, :], ksum[:, :], 1.0 / T, None, ALU.mult))
            for c in range(B):
                v.tensor_scalar(chunk(14, c), chunk(14, c), ksum[:, c:c + 1], None,
                                ALU.subtract).then_inc(S("C_kc"), 1)
            dve.wait_ge(S("ld_qkv"), 32)
            for c in range(B):
                dve.wait_ge(S("C_gram"), c + 1)
                v.tensor_tensor(temp(1, c)[:, 0:P], bank[4 + c][:, 0:P], blockmask, ALU.mult).then_inc(S("C_gm"), 1)
            for c in range(B):
                dve.wait_ge(S("C_gq"), c + 1)
                v.tensor_tensor(chunk(2, c), chunk(13, c), bank[c][:, :], ALU.mult).then_inc(S("C_qgq"), 1)
            dve.wait_ge(S("C_sig"), 1)
            dve.wait_ge(S("C_qkout"), 16 * 2 * HG)
            me = Marks(dve, S("dve_loop"))
            any_bad, bad = dve.alloc_register("any_bad"), dve.alloc_register("bad")

            def step(i, s, cur, prev):
                static = isinstance(i, int)
                n = 2 * i + s if static else i * 2 + s
                o = 1 - s

                def take():
                    at = n * G
                    sig = sig_all[:, at:at + G] if static else sig_all[:, bass.ds(at, G)]
                    v.tensor_copy(sg[:, s, :], sig)
                    v.tensor_scalar(nthr[:, s, :], sig, -Z0, None, ALU.mult)
                    for j in range(G):
                        dve.wait_ge(S("C_s"), n * G + j + 1)
                        ins = v.tensor_scalar(score[s][:, j, :], bank[j % 4][:, :], 1.0, None, ALU.mult, ALU.max,
                                              accum_out=rmax[:, s, j:j + 1])
                        ins.then_inc(S("C_take"), 1)

                def newton(k, counted, done):
                    dve.wait_ge(S(counted), n * G + G)
                    me.link(v.scalar_tensor_tensor(step_[:, :], cnt[:, s, :], T - 2 * AIM, sg[:, s, :],
                                                   ALU.add, ALU.mult))
                    v.scalar_tensor_tensor(nthr[:, s, :], step_[:, :], -GAIN[k] / 2, nthr[:, s, :],
                                           ALU.mult, ALU.add).then_inc(S(done), 1)

                def window(j):
                    buf = work[j % 4:j % 4 + 2]
                    a = [me.mark(v.scalar_tensor_tensor(buf[k], score[o][:, j + k, :], cand[:, j + k, 0:1],
                                                        score[o][:, j + k, :], ALU.is_lt, ALU.mult)) for k in (0, 1)]
                    b = []
                    for k in (0, 1):
                        me.need(a[k])
                        b.append(me.mark(v.max(cand[:, j + k, 1:9], buf[k])))
                    c = []
                    for k in (0, 1):
                        me.need(b[k])
                        c.append(me.mark(v.match_replace(buf[k], cand[:, j + k, 1:9], buf[k], FILL)))
                    for k in (0, 1):
                        me.need(c[k])
                        last = me.mark(v.max(cand[:, j + k, 9:17], buf[k]))
                    return last

                def wide(x):
                    return x.unsqueeze(2).broadcast_to([P, G, WIN])

                def fix():
                    dve.reg_load(any_bad, flags[0:1, G:G + 1].bitcast(mybir.dt.uint32))
                    with dve.If_ne(any_bad, 0):
                        with dve.Fori(0, G) as t:
                            dve.reg_load(bad, flags[0:1, bass.ds(t, 1)].bitcast(mybir.dt.uint32))
                            with dve.If_ne(bad, 0):
                                here = Marks(dve, S("dve_slow"))
                                here.clear()
                                here.link(v.tensor_copy(slow, score[o].rearrange("p j t -> p (j t)")[:, bass.ds(t * T, T)]))
                                for _ in range(TOPK // 8):
                                    here.link(v.max(hi[:, :], slow))
                                    here.link(v.match_replace(slow, hi[:, :], slow, FILL))
                                here.link(v.scalar_tensor_tensor(
                                    sparse.rearrange("p j t -> p (j t)")[:, bass.ds(t * T, T)], slow, FILL,
                                    prob[o].rearrange("p j t -> p (j t)")[:, bass.ds(t * T, T)],
                                    ALU.is_equal, ALU.mult, accum_out=zz[:, o, bass.ds(t + G, 1)]))
                            dve.nop()
                        dve.nop()

                if cur:
                    take()
                if prev:
                    dve.wait_ge(S("C_c3"), n * G)
                    first = me.mark(v.tensor_scalar(cand[:, :, 0], nthr[:, o, :], -1.0, None, ALU.mult))
                    if cur:
                        dve.wait_ge(S("C_take"), n * G + G)
                        v.tensor_scalar(nmax[:, s, :], rmax[:, s, :], -SCALE, None, ALU.mult).then_inc(S("C_nm"), 1)
                    me.need(first)
                    for j in range(0, G, 2):
                        last = window(j)
                        if cur and j == 2:
                            newton(0, "C_c1", "C_n1")
                    r, good = thr[:, 0, :], thr[:, 3, :]
                    me.link(v.tensor_scalar(r, cnt[:, o, :], -0.5, TOPK - T / 2, ALU.mult, ALU.add))
                    h3 = [hit[:, k, :].rearrange("p (j w) -> p j w", j=G) for k in range(3)]
                    me.link(v.tensor_tensor(h3[0], places.unsqueeze(1).broadcast_to([P, G, WIN]), wide(r),
                                            ALU.is_equal))
                    v.tensor_tensor(h3[1], h3[0], cand[:, :, 0:WIN], ALU.mult)
                    me.link(v.tensor_tensor(h3[2], h3[0], cand[:, :, 1:], ALU.mult))
                    me.link(v.tensor_reduce(thr[:, 1:3, :].rearrange("p k j -> p (k j)"),
                                            hit[:, 1:3, :].rearrange("p k (j w) -> p (k j) w", j=G), AX, ALU.add))
                    me.link(v.scalar_tensor_tensor(good, thr[:, 2, :], 0.0, thr[:, 1, :], ALU.max, ALU.is_lt))
                    dve.sem_inc(S("C_good"), 1)
                    if cur:
                        newton(1, "C_c2", "C_n2")
                    for j in range(G):
                        dve.wait_ge(S("C_exp"), (n - 1) * G + j + 1)
                        if not (static and n < 2):
                            dve.wait_ge(S("C_pT"), (n - 2) * G + j + 1)
                        me.mark(v.scalar_tensor_tensor(sparse[:, j, :], score[o][:, j, :], thr[:, 1, j:j + 1],
                                                       prob[o][:, j, :], ALU.is_ge, ALU.mult,
                                                       accum_out=zz[:, o, G + j:G + j + 1]))
                    me.need(me.k)
                    dve.wait_ge(S("C_flag"), n)
                    me.link(v.tensor_scalar(flags[:, 0:G], bank[7][0:1, 0:G], P - 0.5, None, ALU.is_lt))
                    me.link(v.tensor_reduce(flags[:, G:G + 1], flags[:, 0:G], AX, ALU.max))
                    fix()
                    me.link(v.reciprocal(zz[:, o, :], zz[:, o, :]))
                    at = (n - 1) * 2 * G
                    gt = gates[:, at:at + 2 * G] if static else gates[:, bass.ds(at, 2 * G)]
                    v.tensor_tensor(cc[:, o, :], zz[:, o, :], gt, ALU.mult).then_inc(S("C_cc"), 1)
                else:
                    dve.wait_ge(S("C_take"), G)
                    v.tensor_scalar(nmax[:, s, :], rmax[:, s, :], -SCALE, None, ALU.mult).then_inc(S("C_nm"), 1)
                    newton(0, "C_c1", "C_n1")
                    newton(1, "C_c2", "C_n2")
            me.clear()
            step(0, 0, True, False)
            step(0, 1, True, True)
            with dve.Fori(1, NI) as i:
                me.clear()
                step(i, 0, True, True)
                step(i, 1, True, True)
            me.clear()
            step(NI, 0, False, True)

            def token_add(tag, out_sem):
                for c in range(B):
                    dve.wait_ge(S(tag), c + 1)
                    ins = v.scalar_tensor_tensor(tok(ytok, c), bank[4 + c][:, :], col("alpha"), tok(ytok, c),
                                                 ALU.mult, ALU.add)
                link(ins)
            token_add("C_aT", None)
            ln("ln5", ytok, htok_d, False)
            token_add("C_mT", None)
            for c in range(B):
                v.tensor_tensor(tok(xres, c), tok(xres, c), tok(ytok, c), ALU.add).then_inc(S("C_out"), 1)
            dve.wait_ge(S("C_out"), B)

            ln("ln6", xres, htok_b, False)
            route("D", ED, False)

            def unit_d(i, u, first):
                for c in range(B):
                    k = i * (RING * B) + (B * u + c)
                    dve.wait_ge(S("D_u"), k + 1)
                    dve.wait_ge(S("D_sil"), k + 1)
                    v.tensor_tensor(temp(9, c % 2), temp(5, c % 2), bank[4 + (3 * c + 1) % 4][:, :],
                                    ALU.mult).then_inc(S("D_us"), 1)
                    dve.wait_ge(S("D_us"), k + 1)
                    if not (first and u == 0 and c < 2):
                        dve.wait_ge(S("D_down"), k - 1)
                    dve.wait_ge(S("D_bc"), k + 1)
                    v.tensor_tensor(temp(9, 2 + c % 2), temp(9, c % 2), bank[4 + (3 * c + 2) % 4][:, :],
                                    ALU.mult).then_inc(S("D_a"), 1)
            for u in range(RING):
                unit_d(0, u, True)
            with dve.Fori(1, UNITS // RING) as i:
                for u in range(RING):
                    unit_d(i, u, False)
            add_back("D")

        @block.tensor
        def _(pe):
            mm = nc.tensor.matmul

            def chunk(n, c):
                return flat(n)[:, c * T:(c + 1) * T]

            def ln(tag, src):
                for c in range(B):
                    pe.wait_ge(S("ln_norm"), ln_count(tag, c))
                    for t in range(QT):
                        ins = nc.tensor.transpose(bank[c][:, t * P:(t + 1) * P], src[:, QT * c + t, :], ident)
                    ins.then_inc(S("ln_T"), 1)

            def to_tokens(src, c, dst):
                for t in range(QT):
                    ins = nc.tensor.transpose(dst[:, t * P:(t + 1) * P], src[:, t * P:(t + 1) * P], ident)
                return ins

            pe.wait_ge(S("ld_const"), 48)
            ln("ln1", htok)
            pe.wait_ge(S("ld_wa"), 16)
            for c in range(B):
                pe.wait_ge(S("A_xxx"), c + 1)
                mm(bank[c][:, :], wk, chunk(13, c), start=True, stop=True)
                mm(bank[4 + c][:, :], wv, chunk(13, c), start=True, stop=True).then_inc(S("A_kv"), 1)
            for c in range(B):
                pe.wait_ge(S("A_kvs"), 2 * (c + 1))
                mm(bank[c][:, :], wr, chunk(13, c), start=True, stop=True).then_inc(S("A_r"), 1)
            pe.wait_ge(S("A_z"), 1)
            for c in range(B):
                to_tokens(chunk(8, c), c, bank[c]).then_inc(S("A_zT"), 1)
            ln("ln2", htok)
            for c in range(B):
                pe.wait_ge(S("A_xx2"), c + 1)
                mm(bank[c][:, :], wcr, chunk(13, c), start=True, stop=True).then_inc(S("A_rc"), 1)

            def up(s):
                if s >= 2:
                    pe.wait_ge(S("A_rl"), s - 1)
                mm(bank[4 + s % 2][:, :], wck[:, (s % 4) * P:(s % 4 + 1) * P], chunk(13, s // 4),
                   start=True, stop=True).then_inc(S("A_kc"), 1)
            up(0)
            up(1)
            for s in range(4 * B):
                if s + 2 < 4 * B:
                    up(s + 2)
                if s % 4 == 0 and s >= 8:
                    pe.wait_ge(S("A_vz"), s // 4 - 1)
                pe.wait_ge(S("A_sq"), s + 1)
                mm(bank[6 + s // 4 % 2][:, :], wcv[:, (s % 4) * P:(s % 4 + 1) * P], temp(5, s % 4),
                   start=(s % 4 == 0), stop=(s % 4 == 3)).then_inc(S("A_vv"), 1)
            for c in range(B):
                pe.wait_ge(S("A_vz"), c + 1)
                to_tokens(chunk(7, c), c, bank[c]).then_inc(S("A_vT"), 1)

            def route(tag, ne, w):
                pe.wait_ge(S("ln_F"), ln_count("ln3" if tag == "B" else "ln6", B - 1))
                for t in range(NT):
                    ins = mm(bank[4][:, t * ne:(t + 1) * ne], feat[:, t * P:(t + 1) * P], w, start=True, stop=True)
                ins.then_inc(S(f"{tag}_lg"), 1)
                pe.wait_ge(S(f"{tag}_cw"), 1)
                cw = flat(10)[:, 0:NT * (ne + 1)].rearrange("p (t e) -> p t e", e=ne + 1)
                for c in range(B):
                    for t in range(QT):
                        ins = nc.tensor.transpose(bank[4 + c][0:ne + 1, t * P:(t + 1) * P], cw[:, QT * c + t, :], ident)
                    ins.then_inc(S(f"{tag}_cwTp"), 1)
                pe.wait_ge(S(f"{tag}_cwT"), B)

            def moe(tag, ne, products, sel, tail):
                npr = len(products) + 1

                def step(i, u, c, first):
                    k = i * (RING * B) + (B * u + c)
                    if c == 0:
                        pe.wait_ge(S(f"{tag}_w{u}"), i * 16 + 16)
                    for n, (done, w, reader, lag) in enumerate(products):
                        if not (first and u == 0 and c < lag):
                            pe.wait_ge(S(reader), k - lag + 1)
                        mm(bank[4 + (npr * c + n) % 4][:, :], flat(u)[:, w * P:(w + 1) * P],
                           feat[:, c * T:(c + 1) * T], start=True, stop=True).then_inc(S(done), 1)
                    reader, lag = sel[1], sel[2]
                    if not (first and u == 0 and c < lag):
                        pe.wait_ge(S(reader), k - lag + 1)
                    pe.wait_ge(S(f"{tag}_msk"), k + 1)
                    mm(bank[4 + (npr * c + npr - 1) % 4][:, :], sel[0], temp(4, c % 2)[0:ne + 1, :],
                       start=True, stop=True).then_inc(S(f"{tag}_bc"), 1)

                def down(i, u, c, first):
                    k = i * (RING * B) + (B * u + c)
                    pe.wait_ge(S(f"{tag}_a"), k + 1)
                    mm(bank[c][:, :], flat(u)[:, len(products) * P:(len(products) + 1) * P], temp(9, 2 + c % 2),
                       start=(first and u == 0), stop=False, skip_group_check=True).then_inc(S(f"{tag}_down"), 1)

                def body(i, first):
                    for l in range(RING * B):
                        step(i, l // B, l % B, first)
                        if l:
                            down(i, (l - 1) // B, (l - 1) % B, first)
                    down(i, RING - 1, B - 1, first)
                body(0, True)
                with pe.Fori(1, UNITS // RING) as i:
                    body(i, False)
                tail()

            def finish(tag):
                for c in range(B):
                    pe.wait_ge(S(f"{tag}_accs"), c + 1)
                    to_tokens(chunk(8, c), c, bank[4 + c]).then_inc(S(f"{tag}_oT"), 1)

            pe.wait_ge(S("A_out"), B)
            ln("ln3", htok_b)
            pe.wait_ge(S("ld_b"), 32)
            route("B", EB, rt[:, 0:EB])

            def tail_b():
                for c in range(B):
                    ins = mm(bank[c][:, :], b2[:, :], flat(3)[0:EB + 1, c * T:(c + 1) * T],
                             start=False, stop=True, skip_group_check=True)
                ins.then_inc(S("B_acc"), 1)
            moe("B", EB,
                [("B_h1e", 0, "B_g", 1), ("B_h3e", 2, "B_t2", 1), ("B_h1o", 1, "B_po", 1), ("B_h3o", 3, "B_a", 1)],
                (ones, "B_t1", 0), tail_b)
            finish("B")

            pe.wait_ge(S("B_out"), B)
            ln("ln4", htok_c)
            pe.wait_ge(S("ld_qkv"), 32)
            pe.wait_ge(S("ln_F"), ln_count("ln4", B - 1))
            for c in range(B):
                mm(bank[4 + c][:, :], wqkv[:, 0:P], feat[:, c * T:(c + 1) * T],
                   start=True, stop=True).then_inc(S("C_pq"), 1)
            for c in range(B):
                mm(bank[c][:, :], wqkv[:, P:2 * P], feat[:, c * T:(c + 1) * T],
                   start=True, stop=True).then_inc(S("C_pk"), 1)
            for t in range(NT):
                if t < 4:
                    pe.wait_ge(S("C_q"), t + 1)
                else:
                    pe.wait_ge(S("C_vs"), t - 3)
                mm(bank[4 + t % 4][:, 0:P], feat[:, t * P:(t + 1) * P], wqkv[:, 2 * P:],
                   start=True, stop=True).then_inc(S("C_v"), 1)
            pe.wait_ge(S("ld_qkv"), 32)
            for c in range(B):
                pe.wait_ge(S("C_kc"), c + 1)
                to_tokens(chunk(14, c), c, bank[c]).then_inc(S("C_kT"), 1)
            pe.wait_ge(S("C_vs"), NT)
            for c in range(B):
                pe.wait_ge(S("C_ktok"), c + 1)
                for t in range(QT):
                    kt = chunk(0, c)[:, t * P:(t + 1) * P]
                    ins = mm(bank[4 + c][:, 0:P], kt, kt, start=(t == 0), stop=(t == QT - 1))
                ins.then_inc(S("C_gram"), 1)
            for c in range(B):
                pe.wait_ge(S("C_gm"), c + 1)
                mm(bank[c][:, :], temp(1, c)[:, 0:P], chunk(13, c), start=True, stop=True).then_inc(S("C_gq"), 1)
            for c in range(B):
                pe.wait_ge(S("C_qgq"), c + 1)
                for q in range(QT):
                    ins = mm(bank[6][:, (c * QT + q) * HEADS:(c * QT + q + 1) * HEADS],
                             chunk(2, c)[:, q * P:(q + 1) * P], headsel, start=True, stop=True)
            ins.then_inc(S("C_var"), 1)
            pe.wait_ge(S("C_sig"), 1)
            pe.sem_inc(S("C_pv"), 2)

            def scores(i, s, j, wait_free):
                n = 2 * i + s if isinstance(i, int) else i * 2 + s
                h, q = 2 * s + j // QT, j % QT
                if wait_free:
                    pe.wait_ge(S("C_take"), n * G + j - 3)
                mm(bank[j % 4][:, :], q_cur[32 * h:32 * h + DK, q * P:(q + 1) * P],
                   k_cur[32 * h:32 * h + DK, :], start=True, stop=True).then_inc(S("C_s"), 1)

            def pv(n, i, s, h):
                pe.wait_ge(S("C_pTs"), n * G + QT * (h + 1) + 2)
                if s == 0 and h == 0:
                    pe.wait_ge(S("C_o"), i + 1)
                    pe.wait_ge(S("C_v"), NT + 1 + i)
                at = 32 * (2 * s + h)
                for kc in range(QT):
                    ins = mm(bank[4][at:at + 32, :], v_curv[:, kc, 2 * s + h, :], pT[h][:, kc, :],
                             start=(kc == 0), stop=(kc == QT - 1))
                ins.then_inc(S("C_pv"), 1)

            def step(i, s, cur, ahead, prev, old):
                n = 2 * i + s if isinstance(i, int) else i * 2 + s
                if cur:
                    for j in range(4, G):
                        scores(i, s, j, True)
                for half in range(2):
                    if old:
                        for j in range(QT * half, QT * half + QT):
                            pe.wait_ge(S("C_mix"), (n - 2) * G + j + 1)
                            pe.wait_ge(S("C_pTs"), (n - 2) * G + j + 1)
                            for kc in range(QT):
                                ins = nc.tensor.transpose(bank[5 + j % 2][:, kc * P:(kc + 1) * P],
                                                          sparse[:, j, kc * P:(kc + 1) * P], ident)
                            ins.then_inc(S("C_pT"), 1)
                    if half == 0 and ahead:
                        if s == 1:
                            pe.wait_ge(S("C_qk"), (i + 2) * (16 * 2 * HG))
                        for j in range(4):
                            scores(i + s, 1 - s, j, True)
                    if half == 1 and prev:
                        pe.wait_ge(S("C_good"), n)
                        mm(bank[7][0:1, 0:G], onescol, thr[:, 3, :], start=True, stop=True).then_inc(S("C_flag"), 1)
                    if old:
                        pv(n - 2, i - 1, s, half)

            pe.wait_ge(S("C_qk"), 16 * 2 * HG)
            for j in range(4):
                scores(0, 0, j, False)
            step(0, 0, True, True, False, False)
            step(0, 1, True, True, True, False)
            with pe.Fori(1, NI - 1) as i:
                step(i, 0, True, True, True, True)
                step(i, 1, True, True, True, True)
            step(NI - 1, 0, True, True, True, True)
            step(NI - 1, 1, True, False, True, True)
            step(NI, 0, False, False, True, True)
            step(NI, 1, False, False, False, True)
            pe.wait_ge(S("ld_wo"), 16)
            pe.wait_ge(S("ld_o"), 16 * HG)
            for c in range(B):
                mm(bank[c][:, :], flat(0)[:, 0:P], chunk(2, c), start=True, stop=True).then_inc(S("C_ao"), 1)
            for c in range(B):
                pe.wait_ge(S("C_aos"), c + 1)
                to_tokens(chunk(12, c), c, bank[4 + c]).then_inc(S("C_aT"), 1)
            ln("ln5", htok_d)
            pe.wait_ge(S("ld_mlp"), 32)
            pe.wait_ge(S("ln_F"), ln_count("ln5", B - 1))
            NH = HID // P

            def hidden(s):
                if s >= 2:
                    pe.wait_ge(S("C_gl"), s - 1)
                j, c = s % NH, s // NH
                mm(bank[4 + s % 2][:, :], flat(1)[:, j * P:(j + 1) * P], feat[:, c * T:(c + 1) * T],
                   start=True, stop=True).then_inc(S("C_h"), 1)
            hidden(0)
            hidden(1)
            for s in range(NH * B):
                if s + 2 < NH * B:
                    hidden(s + 2)
                j, c = s % NH, s // NH
                pe.wait_ge(S("C_gl"), s + 1)
                mm(bank[c][:, :], flat(1)[:, HID + j * P:HID + (j + 1) * P], temp(2, s % 4),
                   start=(j == 0), stop=(j == NH - 1)).then_inc(S("C_dn"), 1)
            for c in range(B):
                pe.wait_ge(S("C_mo"), c + 1)
                to_tokens(chunk(12, c), c, bank[4 + c]).then_inc(S("C_mT"), 1)

            pe.wait_ge(S("C_out"), B)
            ln("ln6", htok_b)
            route("D", ED, rt[:, EB:])

            def tail_d():
                pe.wait_ge(S("D_down"), UNITS * B)
                pe.sem_inc(S("D_acc"), 1)
            moe("D", ED, [("D_g", 0, "D_a", 2), ("D_u", 1, "D_sil", 1)], (halfsel, "D_us", 1), tail_d)
            finish("D")


_COLS = ["L0_attn_ln1_w", "L0_attn_ln1_b", "L0_attn_ln2_w", "L0_attn_ln2_b", "L0_attn_time_shift",
         "L0_attn_time_first", "L1_attn_ln1_g", "L1_attn_ln1_b", "L1_attn_ln2_g", "L1_attn_ln2_b", "L1_attn_b2"]


def kernel(**inputs):
    import numpy as np
    import concourse.bacc as bacc
    from concourse import mybir as _mybir
    from concourse.bass_utils import run_bass_kernel_spmd as run

    x = {n: np.asarray(a) for n, a in inputs.items()}
    f = np.float32

    cols = [x[n].reshape(P, 1) for n in _COLS] + [np.broadcast_to(x["L1_attn_alpha"].reshape(1, 1), (P, 1))]
    cols.append(x["L1_attn_b1"].reshape(HID // P, P).T)
    cols = np.ascontiguousarray(np.concatenate(cols, axis=1))
    eb = np.concatenate([np.concatenate([x[f"L0_ffn_{n}"], x[f"L0_ffn_s{n}"][None]]).reshape(UNITS, P, 2)
                         for n in ("b1", "b3")] + [np.eye(P, dtype=f)[:UNITS, :, None]], axis=2)
    heads = np.broadcast_to(x["L1_attn_alpha_head"].reshape(HG, 1, 2, 1, 2, 1), (HG, B, 2, 2, 2, QT)).reshape(-1)
    rows = np.concatenate([x["L0_ffn_gate_b"], x["L1_ffn_router_bias"], heads])
    rows = np.ascontiguousarray(np.broadcast_to(rows, (P, rows.size)))
    pairmask = np.zeros((UNITS, P, 1), f)
    cst = np.zeros((P, 2 * P + ED + P), f)
    cst[:, 0:P] = np.eye(P, dtype=f)
    for e in range(ED):
        cst[e, P + 64 * (e % 2):P + 64 * (e % 2) + 64] = 1
        pairmask[e // 2, e] = 1
    cst[ED, P:2 * P] = 1
    pairmask[UNITS - 1, ED] = 1
    cst[:, 2 * P:2 * P + ED] = np.arange(ED, 0, -1, dtype=f)
    cst[:, 2 * P + ED:] = 1
    wcv = x["L0_attn_Wcv"].T.reshape(4, P, P).transpose(1, 0, 2).reshape(P, 4 * P)
    wa = np.concatenate([x["L0_attn_Wk"].T, x["L0_attn_Wv"].T, x["L0_attn_Wr"].T, x["L0_attn_Wcr"].T,
                         x["L0_attn_Wck"].T, wcv], axis=1)

    def split(w):
        return np.concatenate([w[..., 0::2, :], w[..., 1::2, :]], axis=-2).swapaxes(-1, -2)
    routed = np.concatenate([split(x["L0_ffn_w1"]), split(x["L0_ffn_w3"]), x["L0_ffn_w2"].swapaxes(-1, -2)], axis=-1)
    shared = np.concatenate([split(x["L0_ffn_sw1"]), split(x["L0_ffn_sw3"]), x["L0_ffn_sw2"].T], axis=-1)
    wb = np.concatenate([np.concatenate([routed, shared[None]], axis=0), eb], axis=2)
    b2 = np.concatenate([x["L0_ffn_b2"], x["L0_ffn_sb2"][None]], axis=0)
    rt = np.concatenate([x["L0_ffn_gate_w"].T, x["L1_ffn_router_w"].T], axis=1)
    wqkv = x["L1_attn_w_qkv"]
    wo = x["L1_attn_w_out"]
    cstc = np.zeros((P, P + HEADS + WIN + 1), f)
    for h in range(HEADS):
        cstc[DK * h:DK * h + DK, DK * h:DK * h + DK] = 1 / T
        cstc[DK * h:DK * h + DK, P + h] = 1
    cstc[:, P + HEADS:P + HEADS + WIN] = np.arange(WIN, dtype=f)
    cstc[:, P + HEADS + WIN] = 1
    wm1 = x["L1_attn_w1"]
    wm2 = x["L1_attn_w2"].reshape(HID // P, P, P).transpose(1, 0, 2).reshape(P, HID)

    def pairs(w):
        return w.reshape(8, 2, P, 64).transpose(0, 2, 1, 3).reshape(8, P, P)
    routed = np.concatenate([pairs(x["L1_ffn_gate_proj"]), pairs(x["L1_ffn_up_proj"]),
                             x["L1_ffn_down_proj"].reshape(8, P, P)], axis=-1)
    shared = np.concatenate([x["L1_ffn_sh_gate"].T, x["L1_ffn_sh_up"].T, x["L1_ffn_sh_down"].T], axis=-1)
    wd = np.concatenate([np.concatenate([routed, shared[None]], axis=0), pairmask], axis=2)
    xt = x["L0_attn_x"].reshape(B, QT, P, P).transpose(0, 2, 1, 3)

    nc = bacc.Bacc("TRN2", target_bir_lowering=False, num_devices=1)
    arrays, args = {}, []
    for name, a in (("x", xt), ("cols", cols), ("rows", rows), ("cst", cst), ("cstc", cstc),
                    ("wa", wa), ("wb", wb), ("b2", b2),
                    ("rt", rt), ("wqkv", wqkv), ("wo", wo), ("wm1", wm1), ("wm2", wm2), ("wd", wd)):
        a = np.ascontiguousarray(a)
        arrays[f"{name}_dram"] = a
        args.append(nc.dram_tensor(f"{name}_dram", a.shape, _mybir.dt.from_np(a.dtype), kind="ExternalInput").ap())
    args.append(nc.dram_tensor("qk_scratch", (2, NI, HG * DK, T), F32, kind="Internal").ap())
    args.append(nc.dram_tensor("o_scratch", (NI, HG * DK, T), F32, kind="Internal").ap())
    args.append(nc.dram_tensor("out_dram", (B, P, QT, P), F32, kind="ExternalOutput").ap())
    build(nc, *args)
    r = run(nc, [arrays], core_ids=[0])
    got = r.results[0]["out_dram"]
    return np.ascontiguousarray(got.transpose(0, 2, 1, 3).reshape(B, T, P))
```

```python
from contextlib import ExitStack

import concourse.bass as bass
from concourse import mybir

F32 = mybir.dt.float32
BF16 = mybir.dt.bfloat16
ACT = mybir.ActivationFunctionType
ALU = mybir.AluOpType
AX = mybir.AxisListType.X

P = 128
B, T = 4, 512
N = B * T
NT = N // P
QT = T // P
EPS = 1e-5
EB, ED = 8, 16
UNITS = 9
BY_DVE = 3
RING = 3
HEADS, DK, TOPK = 16, 8, 64
HG = 4
NI = HEADS // HG * B
SCALE = DK ** -0.5
PARTS = 3
SPLIT_ROWS = PARTS * 32
QK_ROWS = PARTS * PARTS * DK
FILL = -3.0e38
G = 8
NG = HEADS * B * QT // G
ONE_BITS, ALL_BITS = 0x3F800000, 0x43000000
LAST_BY_DVE = 5
BY_ACT = 3
WIN = 8
AIM = TOPK - WIN / 2 + 0.5
Z0 = 1.185
GAIN = 1 / 120.0
TURN = 0.45
HID = 8 * P

COLS = ["ln1w", "ln1b", "ln2w", "ln2b", "ts", "u", "aln1g", "aln1b", "aln2g", "aln2b", "mb2", "alpha"]
C_MB1 = len(COLS)
NCOLS = C_MB1 + HID // P


class Marks:

    def __init__(self, engine, sem):
        self.engine, self.sem, self.k = engine, sem, 0

    def clear(self):
        self.engine.sem_clear(self.sem)
        self.k = 0

    def mark(self, ins):
        ins.then_inc(self.sem, 1)
        self.k += 1
        return self.k

    def need(self, k):
        self.engine.wait_ge(self.sem, k)

    def link(self, ins):
        self.need(self.mark(ins))


class Chain:

    def __init__(self, engine, sem):
        self.engine, self.sem, self.k = engine, sem, 0

    def __call__(self, ins):
        ins.then_inc(self.sem, 1)
        self.k += 1
        self.engine.wait_ge(self.sem, self.k)


def ln_count(tag, c):
    return B * (int(tag[2]) - 1) + c + 1


def norm_count(tag, c):
    mine = BY_DVE if c < BY_DVE else B - BY_DVE
    return mine * (int(tag[2]) - 1) + (c if c < BY_DVE else c - BY_DVE) + 1


def build(nc, x_d, cols_d, rows_d, cst_d, cstc_d, wa_d, wb_d, b2_d, rt_d, wqkv_d, wo_d, wm1_d, wm2_d, wd_d, qk_scr, out_d):
    ctx = ExitStack()
    with ctx:
        def sb(name, shape):
            return ctx.enter_context(nc.sbuf_tensor(name, shape, F32))

        sems = {}

        def S(name):
            if name not in sems:
                sems[name] = ctx.enter_context(nc.semaphore(name))
            return sems[name]

        bank = [ctx.enter_context(nc.psum_tensor(f"bank{i}", [P, 512], F32)) for i in range(8)]
        SLOT = B * (T + 1)
        NSLOT = 17
        arena = sb("arena", [P, NSLOT * SLOT])

        def flat(n, w=N):
            return arena[:, n * SLOT:n * SLOT + w]

        def seq(n):
            return flat(n, SLOT).rearrange("p (b t) -> p b t", b=B)

        def bt(n):
            return flat(n).rearrange("p (b t) -> p b t", b=B)

        cols = sb("cols", [P, NCOLS])
        rows = sb("rows", [P, EB + ED + NG * 2 * G])
        cst = sb("cst", [P, cst_d.shape[1]])
        ident = cst[:, 0:P]
        halfsel = cst[0:SPLIT_ROWS, P:2 * P]
        rank = cst[:, 2 * P:2 * P + ED]
        xres = sb("xres", [P, NT, P])
        ytok = sb("ytok", [P, NT, P])
        feat = sb("feat", [P, N])
        stats = sb("stats", [P, NT, 6])
        mv = sb("mv", [P, NT, 2])
        rstd = sb("rstd", [P, 2, NT])
        shiftc = sb("shiftc", [P, 5])
        small = sb("small", [P, 8, NT])
        rt = sb("rt", [P, EB + ED])
        b2 = sb("b2", [EB + 1, P])

        def col(name):
            n = COLS.index(name)
            return cols[:, n:n + 1]

        WA = 16
        wk, wv, wr, wcr = (flat(WA)[:, n * P:(n + 1) * P] for n in range(4))
        wck = flat(WA)[:, 4 * P:8 * P]
        wcv = flat(WA)[:, 8 * P:12 * P]
        htok = flat(0).rearrange("p (t c) -> p t c", t=NT)
        htok_b = htok_c = flat(12).rearrange("p (t c) -> p t c", t=NT)
        htok_d = flat(3).rearrange("p (t c) -> p t c", t=NT)
        def temp(slot, n):
            return flat(slot)[:, n * T:(n + 1) * T]
        cw_all = flat(10)[:, 0:NT * UNITS].rearrange("p (t e) -> p t e", e=UNITS)
        cw_unit = [flat(4)[:, u * NT:(u + 1) * NT] for u in range(RING)]
        LOOP = RING * B

        def up_bank(l, n):
            return bank[(4 * l + n) % 6]
        V_ALL = 12
        qc, kc_ = flat(13), flat(14)
        v_all = flat(V_ALL)
        def halves(n):
            return flat(n).bitcast(BF16).rearrange("p (a n) -> p a n", a=2)

        cw_parts = flat(10)[:, 0:NT * SPLIT_ROWS].rearrange("p (t r) -> p t r", r=SPLIT_ROWS)
        cw_full = flat(15)[:, 0:NT * (ED + 1)].rearrange("p (t e) -> p t e", e=ED + 1)
        cw_bf = halves(13)[:, 0, 0:NT * (ED + 1)].rearrange("p (t e) -> p t e", e=ED + 1)
        cw_rows = halves(3)[0:SPLIT_ROWS, 0, :]
        cw_masked = [halves(4)[0:SPLIT_ROWS, 0, n * T:(n + 1) * T] for n in range(2)]
        halfsel_bf = halves(14)[0:SPLIT_ROWS, 0, 0:P]
        split = [[halves(5 + (PARTS * w + a) // 2)[:, (PARTS * w + a) % 2, :] for a in range(PARTS)] for w in range(2)]
        qk_rows = [[halves(15)[0:QK_ROWS, s, w * 2 * T:(w + 1) * 2 * T].rearrange("p (h t) -> p h t", h=2)
                    for w in range(2)] for s in range(2)]
        o_tok = flat(3).rearrange("p (t c) -> p t c", t=NT)
        score = [arena[:, n * G * T:(n + 1) * G * T].rearrange("p (j t) -> p j t", j=G) for n in range(2)]
        prob = [arena[:, n * G * T:(n + 1) * G * T].rearrange("p (j t) -> p j t", j=G) for n in range(2, 4)]
        sparse = arena[:, 4 * G * T:5 * G * T].rearrange("p (j t) -> p j t", j=G)
        assert 5 * G * T <= 11 * SLOT
        work = [temp(13, n) for n in range(4)]
        slow = temp(16, 3)
        marks_of = work + [temp(16, 0)]
        junk = [temp(14, n) for n in range(4)]
        cstc = sb("cstc", [P, P + HEADS + WIN + 1])
        blockmask, headsel = cstc[:, 0:P], cstc[:, P:P + HEADS]
        places, onescol = cstc[:, P + HEADS:P + HEADS + WIN], cstc[:, P + HEADS + WIN:]
        wqkv = flat(16)[:, 0:3 * P]
        pT = [sb(f"pT{n}", [P, QT, P]) for n in range(4)]
        o_all = sb("o_all", [P, NG * G * DK])
        hi = sb("hi", [P, 8])
        sig_all = sb("sig_all", [P, NG * G])
        gates = sb("gates", [P, NG * 2 * G])
        ksum = sb("ksum", [P, B])
        rmax = sb("rmax", [P, 2, G])
        nmax = sb("nmax", [P, 2, G])
        nthr = sb("nthr", [P, 2, G])
        cnt = sb("cnt", [P, 2, G])
        zz = sb("zz", [P, 2, 2 * G])
        cc = sb("cc", [P, 2, 2 * G])
        gain = sb("gain", [P, 2, G])
        firstthr = sb("firstthr", [P, G])
        above = sb("above", [P, G])
        exc = sb("exc", [P, 2, G])
        move = sb("move", [P, 3, G])
        cand = sb("cand", [P, G, WIN + 1])
        hit = sb("hit", [P, 3, G * WIN])
        thr = sb("thr", [P, 4, G])
        flags = sb("flags", [1, 2 * G + 3])
        last_bad = ctx.enter_context(nc.sbuf_tensor("last_bad", [1, 1], mybir.dt.uint32))

        block = ctx.enter_context(nc.Block())

        WU = {"B": (wb_d, 5 * P + 4), "D": (wd_d, 3 * P + 1)}

        @block.sync
        def _(sp):
            sp.dma_start(cst[:, :], cst_d).then_inc(S("ld_const"), 16)
            sp.dma_start(cols[:, :], cols_d).then_inc(S("ld_const"), 16)
            sp.dma_start(rows[:, :], rows_d).then_inc(S("ld_const"), 16)
            for b in range(B):
                sp.dma_start(xres[:, QT * b:QT * (b + 1), :], x_d[b]).then_inc(S(f"ld_x{b}"), 16)
            sp.dma_start(flat(WA)[:, 0:12 * P], wa_d).then_inc(S("ld_wa"), 16)
            sp.dma_start(rt[:, :], rt_d).then_inc(S("ld_b"), 16)
            sp.dma_start(b2[:, :], b2_d).then_inc(S("ld_b"), 16)

            def moe_weights(tag):
                src, w = WU[tag]
                for u in range(RING):
                    sp.dma_start(flat(u)[:, 0:w], src[u]).then_inc(S(f"{tag}_w{u}"), 16)
                with sp.Fori(1, UNITS // RING) as i:
                    for u in range(RING):
                        sp.wait_ge(S(f"{tag}_down"), i * (RING * B) - (RING * B) + B * (u + 1))
                        sp.dma_start(flat(u)[:, 0:w],
                                     src[bass.ds(i * RING + u, 1), :, :].rearrange("a p n -> p (a n)")
                                     ).then_inc(S(f"{tag}_w{u}"), 16)

            sp.wait_ge(S("A_out"), B)
            moe_weights("B")
            sp.wait_ge(S("B_out"), B)
            sp.dma_start(wqkv, wqkv_d).then_inc(S("ld_qkv"), 16)
            sp.dma_start(cstc[:, :], cstc_d).then_inc(S("ld_qkv"), 16)
            for w in (1, 0):
                sp.wait_ge(S(("C_qsplit", "C_ksplit")[w]), B)
                for a in range(PARTS):
                    sp.dma_start(qk_scr[w, a], split[w][a]).then_inc(S("C_qkout"), 16)
            sp.wait_ge(S("C_qkout"), 16 * 2 * PARTS)

            def load_qk(g, b, s):
                at = g * (HG * DK) + 2 * DK * s
                rows_at = slice(at, at + 2 * DK) if isinstance(at, int) else bass.ds(at, 2 * DK)
                for w in range(2):
                    src = qk_scr[w, :, rows_at, b * T:(b + 1) * T].rearrange("c (h d) t -> c h d t", h=2)
                    for h in range(2):
                        for a in range(PARTS):
                            dst = qk_rows[s][w][PARTS * DK * a:PARTS * DK * (a + 1), h, :]
                            if w == 0:
                                same = src[a:a + 1, h].broadcast_to([PARTS, DK, T])
                                sp.dma_start(dst, same).then_inc(S(f"C_qk{s}"), 16)
                            else:
                                sp.dma_start(dst, src[:, h]).then_inc(S(f"C_qk{s}"), 16)

            def load_next(g, b):
                for s in range(2):
                    sp.wait_ge(S("C_s"), g * (B * 2 * G) + (b * 2 * G + (s + 1) * G - 2 * G))
                    load_qk(g, b, s)
            load_qk(0, 0, 0)
            load_qk(0, 0, 1)
            for b in range(1, B):
                load_next(0, b)
            with sp.Fori(1, HG) as g:
                for b in range(B):
                    load_next(g, b)
            sp.wait_ge(S("C_pv"), NG * G + 2 * G)
            sp.dma_start(flat(0)[:, 0:P], wo_d).then_inc(S("ld_wo"), 16)
            sp.dma_start(flat(1)[:, 0:HID], wm1_d).then_inc(S("ld_mlp"), 16)
            sp.dma_start(flat(1)[:, HID:2 * HID], wm2_d).then_inc(S("ld_mlp"), 16)
            sp.wait_ge(S("C_out"), B)
            moe_weights("D")
            for b in range(B):
                sp.wait_ge(S("D_out"), b + 1)
                sp.dma_start(out_d[b], xres[:, QT * b:QT * (b + 1), :]).then_inc(S("stored"), 16)
            sp.wait_ge(S("stored"), 16 * B)

        @block.gpsimd
        def _(gp):
            def masks(tag, at):
                gp.wait_ge(S(f"{tag}_cwT"), B)

                def unit(i, u, first):
                    gp.wait_ge(S(f"{tag}_w{u}"), i * 16 + 16)
                    gp.sem_inc(S("gp_passed"), 1)
                    for c in range(B):
                        if not (first and u == 0 and c < 2):
                            k = i * (RING * B) + (B * u + c)
                            gp.wait_ge(S(f"{tag}_bc"), k - 1)
                            gp.sem_inc(S("gp_passed"), 1)
                        gp.tensor_scalar(cw_masked[c % 2], cw_rows[:, c * T:(c + 1) * T],
                                         flat(u)[0:SPLIT_ROWS, at:at + 1], None, ALU.mult).then_inc(S(f"{tag}_msk"), 1)

                for u in range(RING):
                    unit(0, u, True)
                with gp.Fori(1, UNITS // RING) as i:
                    for u in range(RING):
                        unit(i, u, False)

            def ln(tag, src, dst, double):
                gp.wait_ge(S("ln_rstd"), int(tag[2]))
                r = 1 if double else 0
                for t in range(BY_DVE * QT, NT):
                    ins = gp.tensor_scalar(dst[:, t, :], src[:, t, :], mv[:, t, 0:1], rstd[:, r, t:t + 1],
                                           ALU.subtract, ALU.mult)
                    if t % QT == QT - 1:
                        ins.then_inc(S("ln_norm_gp"), 1)

            gp.wait_ge(S("ld_const"), 48)
            ln("ln1", xres, htok, True)
            for c in range(B):
                gp.wait_ge(S("A_s"), 2 * c + 2)
                new, val = flat(7)[:, c * T:(c + 1) * T], flat(2)[:, c * T:(c + 1) * T]
                gp.tensor_tensor(new, new, val, ALU.mult).then_inc(S("A_sv"), 1)
            ln("ln2", ytok, htok, False)
            ln("ln3", xres, htok_b, False)
            def unit_b(i, u, first):
                if first and u == 0:
                    gp.wait_ge(S("B_cw"), 1)
                if not first:
                    gp.wait_ge(S("B_y"), i * LOOP + (B * u + B - LOOP))
                    gp.sem_inc(S("gp_passed"), 1)
                e = i * RING + u
                src = cw_all[:, :, e:e + 1] if isinstance(e, int) else cw_all[:, :, bass.ds(e, 1)]
                gp.tensor_copy(cw_unit[u].unsqueeze(2), src).then_inc(S("B_cwu"), 1)
                for c in range(B):
                    k = i * LOOP + (B * u + c)
                    gp.wait_ge(S("B_l"), k + 1)
                    gp.wait_ge(S("B_sg"), k + 1)
                    if not (first and u == 0):
                        gp.wait_ge(S("B_down"), k - 3)
                    gp.sem_inc(S("gp_passed"), 1)
                    gp.tensor_tensor(temp(9, c), temp(8, c % 2), temp(6, c % 2), ALU.mult).then_inc(S("B_a"), 1)

            for u in range(RING):
                unit_b(0, u, True)
            with gp.Fori(1, UNITS // RING) as i:
                for u in range(RING):
                    unit_b(i, u, False)
            def chunk(x, c):
                return x[:, c * T:(c + 1) * T]

            ln("ln4", xres, htok_c, True)
            for c in range(B):
                gp.wait_ge(S("C_q1"), c + 1)
                gp.tensor_tensor(chunk(flat(8), c), chunk(qc, c), chunk(split[0][0], c), ALU.subtract).then_inc(S("C_qr"), 1)
            me = Marks(gp, S("gp_loop"))

            def mix(n, s, first=0):
                gp.wait_ge(S("C_cc"), n + 1)
                gp.sem_inc(S("gp_passed"), 1)
                last = None
                for j in range(first, G + 1):
                    if j < G:
                        gp.tensor_scalar(prob[s][:, j, :], prob[s][:, j, :], cc[:, s, j:j + 1], 1.0, ALU.mult, ALU.mult)
                        new = me.mark(gp.tensor_scalar(sparse[:, j, :], sparse[:, j, :], cc[:, s, G + j:G + j + 1],
                                                       1.0, ALU.mult, ALU.mult))
                    if j > first:
                        me.need(last)
                        gp.tensor_tensor(sparse[:, j - 1, :], sparse[:, j - 1, :], prob[s][:, j - 1, :],
                                         ALU.add).then_inc(S("C_mix"), 1)
                    last = new

            def body(i):
                me.clear()
                mix(2 * (i - 1) + 0 if isinstance(i, int) else (i - 1) * 2, 0)
                if isinstance(i, int):
                    mix(2 * (i - 1) + 1, 1, LAST_BY_DVE)
                else:
                    mix((i - 1) * 2 + 1, 1)
            with gp.Fori(1, NI) as i:
                body(i)
            body(NI)
            ln("ln5", ytok, htok_d, False)
            ln("ln6", xres, htok_b, False)
            masks("D", 3 * P)

        @block.scalar
        def _(act):
            def ln(tag, dst, w=None, b=None):
                act.wait_ge(S("ln_var"), int(tag[2]))
                act.activation(rstd[:, :, :], rstd[:, :, :], ACT.Sqrt).then_inc(S("ln_std"), 1)
                for c in range(B):
                    act.wait_ge(S("ln_T"), ln_count(tag, c))
                    if w is None:
                        act.activation(dst[:, c * T:(c + 1) * T], bank[c][:, :], ACT.Copy).then_inc(S("ln_F"), 1)
                    else:
                        act.activation(dst[:, c * T:(c + 1) * T], bank[c][:, :], ACT.Identity,
                                       bias=b, scale=w).then_inc(S("ln_F"), 1)

            def chunk(n, c):
                return flat(n)[:, c * T:(c + 1) * T]

            act.wait_ge(S("ld_const"), 48)
            ln("ln1", feat, col("ln1w"), col("ln1b"))
            for c in range(B):
                act.wait_ge(S("A_kv"), c + 1)
                act.activation(chunk(1, c), bank[c][:, :], ACT.Copy).then_inc(S("A_kvs"), 1)
                act.activation(chunk(2, c), bank[4 + c][:, :], ACT.Copy).then_inc(S("A_kvs"), 1)
            for c in range(B):
                for n, ready in ((6, "A_gx"), (7, "A_bx")):
                    act.wait_ge(S(ready), c + 1)
                    act.activation(chunk(n, c), chunk(n, c), ACT.Exp).then_inc(S("A_exps"), 1)
            for c in range(B):
                act.wait_ge(S("A_D"), c + 1)
                act.activation(chunk(11, c), seq(5)[:, c, 0:T], ACT.Ln).then_inc(S("A_ln"), 1)
            for c in range(B):
                for n in (8, 9):
                    act.wait_ge(S("A_x"), c + 1)
                    act.activation(chunk(n, c), chunk(n, c), ACT.Exp).then_inc(S("A_e"), 1)
            for c in range(B):
                act.wait_ge(S("A_r"), c + 1)
                act.activation(chunk(3, c), bank[c][:, :], ACT.Sigmoid).then_inc(S("A_rs"), 1)
                act.wait_ge(S("A_d"), c + 1)
                act.activation(chunk(6, c), chunk(11, c), ACT.Sigmoid, bias=shiftc[:, 4:5]).then_inc(S("A_s"), 1)
                act.activation(chunk(7, c), chunk(11, c), ACT.Sigmoid, bias=col("u"), scale=-1.0).then_inc(S("A_s"), 1)
            ln("ln2", feat, col("ln2w"), col("ln2b"))
            for c in range(B):
                act.wait_ge(S("A_rc"), c + 1)
                act.activation(chunk(3, c), bank[c][:, :], ACT.Sigmoid).then_inc(S("A_rcs"), 1)
            for s in range(B * 4):
                act.wait_ge(S("A_kc"), s + 1)
                if s >= 4:
                    act.wait_ge(S("A_sq"), s - 3)
                act.activation(temp(4, s % 4), bank[4 + s % 2][:, :], ACT.Relu).then_inc(S("A_rl"), 1)

            def route(tag, ln_tag, ne):
                act.wait_ge(S(f"{tag}_ex"), 1)
                act.activation(flat(5)[:, 0:NT * ne], flat(5)[:, 0:NT * ne], ACT.Exp).then_inc(S(f"{tag}_exp"), 1)
                for c in range(B):
                    act.wait_ge(S(f"{tag}_cwTp"), c + 1)
                    rows_n = ne + 1 if tag == "B" else SPLIT_ROWS
                    dst = flat(3)[0:rows_n, :] if tag == "B" else cw_rows
                    act.activation(dst[:, c * T:(c + 1) * T], bank[4 + c][0:rows_n, :],
                                   ACT.Copy).then_inc(S(f"{tag}_cwT"), 1)

            def acc_out(tag):
                for c in range(B):
                    act.wait_ge(S(f"{tag}_acc"), 1)
                    act.activation(chunk(8, c), bank[c][:, :], ACT.Copy).then_inc(S(f"{tag}_accs"), 1)

            ln("ln3", feat)
            route("B", "ln3", EB)

            def unit_b(i, u, first):
                for c in range(B):
                    k = i * (RING * B) + (B * u + c)

                    def bias(n):
                        return flat(u)[:, 5 * P + n:5 * P + n + 1]
                    l = B * u + c
                    act.wait_ge(S("B_h1e"), k + 1)
                    act.activation(temp(5, c % 2), up_bank(l, 0)[:, :], ACT.Identity, bias=bias(0)).then_inc(S("B_t1"), 1)
                    act.wait_ge(S("B_h1o"), k + 1)
                    act.activation(temp(5, 2 + c % 2), up_bank(l, 2)[:, :], ACT.Identity,
                                   bias=bias(1)).then_inc(S("B_t2"), 1)
                    act.wait_ge(S("B_g"), k + 1)
                    if not (first and u == 0 and c < 2):
                        act.wait_ge(S("B_a"), k - 1)
                    act.activation(temp(6, c % 2), temp(6, 2 + c % 2), ACT.Sigmoid,
                                   scale=1.702).then_inc(S("B_sg"), 1)
            for u in range(RING):
                unit_b(0, u, True)
            with act.Fori(1, UNITS // RING) as i:
                for u in range(RING):
                    unit_b(i, u, False)

            def part(w, a, c):
                return split[w][a][:, c * T:(c + 1) * T]

            act.activation(gates[:, :], rows[:, EB + ED:], ACT.Sigmoid).then_inc(S("C_gate"), 1)
            ln("ln4", feat, col("aln1g"), col("aln1b"))
            for c in range(B):
                act.wait_ge(S("C_pk"), c + 1)
                act.activation(chunk(14, c), bank[c][:, :], ACT.Identity,
                               accum_out=ksum[:, c:c + 1]).then_inc(S("C_k"), 1)
            for c in range(B):
                act.wait_ge(S("C_pq"), c + 1)
                act.activation(chunk(13, c), bank[4 + c][:, :], ACT.Copy).then_inc(S("C_q"), 1)
                act.wait_ge(S("C_q"), c + 1)
                act.activation(part(0, 0, c), chunk(13, c), ACT.Copy).then_inc(S("C_q1"), 1)
            for c in range(B):
                act.wait_ge(S("C_kT"), c + 1)
                act.activation(chunk(0, c), bank[c][:, :], ACT.Copy).then_inc(S("C_ktok"), 1)
                act.wait_ge(S("C_qr"), c + 1)
                act.activation(part(0, 1, c), chunk(8, c), ACT.Copy).then_inc(S("C_q2"), 1)
            act.wait_ge(S("C_var"), 1)
            sv = sig_all[:, :].rearrange("p (g b h q) -> p g b h q", g=HG, b=B, h=HG)
            for c in range(B):
                for q in range(QT):
                    src = bank[6][:, (c * QT + q) * HEADS:(c * QT + q + 1) * HEADS]
                    ins = act.activation(sv[:, :, c, :, q], src.rearrange("p (g h) -> p g h", g=HG), ACT.Sqrt)
            ins.then_inc(S("C_sig"), 1)
            va = v_all.rearrange("p (g t c) -> p g t c", g=HG, t=NT)
            for t in range(NT):
                act.wait_ge(S("C_v"), t + 1)
                act.activation(va[:, :, t, :], bank[4 + t % 2][:, 0:P].rearrange("p (g c) -> p g c", g=HG),
                               ACT.Copy).then_inc(S("C_vs"), 1)
            act.sem_inc(S("C_o"), 1)
            act.sem_inc(S("C_pTs"), 2)

            def count(n, s, k, tiles, first=False):
                done = S(f"C_c{k}")
                for j in tiles:
                    if k == 1:
                        act.wait_ge(S("C_take"), n * G + j + 1)
                    elif j == 0:
                        act.wait_ge(S(f"C_n{k - 1}"), n + 1)
                    if j >= 4:
                        act.wait_ge(done, n * (G if k > 1 else BY_ACT) + j - 3)
                    elif k == 1 and not first:
                        act.wait_ge(S("C_c4"), n * G + j - 3)
                    act.activation(junk[j % 4], score[s][:, j, :], ACT.Sign, bias=nthr[:, s, j:j + 1],
                                   accum_out=cnt[:, s, j:j + 1]).then_inc(done, 1)

            def exp(n, s, j):
                if j == 0:
                    act.wait_ge(S("C_nm"), n + 1)
                act.activation(prob[s][:, j, :], score[s][:, j, :], ACT.Exp, bias=nmax[:, s, j:j + 1],
                               scale=SCALE, accum_out=zz[:, s, j:j + 1]).then_inc(S("C_exp"), 1)

            def pt_out(n, j):
                act.wait_ge(S("C_pT"), n * G + j + 1)
                act.wait_ge(S("C_pv"), n * G + j + 1 + (2 * G - 4))
                act.activation(pT[j % 4][:, :, :],
                               bank[5 + j % 2][:, :].rearrange("p (k q) -> p k q", k=QT),
                               ACT.Copy).then_inc(S("C_pTs"), 1)

            def step(i, s, cur, prev, old):
                n = 2 * i + s if isinstance(i, int) else i * 2 + s

                def counts(k, tiles=range(G)):
                    if cur:
                        count(n, s, k, tiles, first=isinstance(n, int) and n == 0)

                def pt(*tiles):
                    for j in tiles:
                        if old:
                            pt_out(n - 2, j)
                counts(1, range(BY_ACT))
                for j in range(G):
                    if prev:
                        exp(n - 1, 1 - s, j)
                pt(0)
                pt(1)
                counts(2, range(4))
                pt(2)
                counts(2, range(4, G))
                pt(3)
                pt(4)
                counts(3, range(4))
                counts(3, range(4, G))
                pt(5)
                pt(6)
                counts(4, range(4))
                pt(7)
                counts(4, range(4, G))

            step(0, 0, True, False, False)
            step(0, 1, True, True, False)
            with act.Fori(1, NI) as i:
                step(i, 0, True, True, True)
                step(i, 1, True, True, True)
            step(NI, 0, False, True, True)
            step(NI, 1, False, False, True)
            for c in range(B):
                act.wait_ge(S("C_oT"), c + 1)
                act.activation(chunk(2, c), bank[4 + c][:, :], ACT.Copy).then_inc(S("C_oTs"), 1)
            for c in range(B):
                act.wait_ge(S("C_ao"), c + 1)
                act.activation(chunk(12, c), bank[c][:, :], ACT.Copy).then_inc(S("C_aos"), 1)
            ln("ln5", feat, col("aln2g"), col("aln2b"))
            NH = HID // P

            def mlp_out(c):
                act.wait_ge(S("C_dn"), (c + 1) * NH)
                act.activation(chunk(12, c), bank[c][:, :], ACT.Identity, bias=col("mb2")).then_inc(S("C_mo"), 1)
            for s in range(B * NH):
                act.wait_ge(S("C_h"), s + 1)
                if s >= 4:
                    act.wait_ge(S("C_dn"), s - 3)
                act.activation(temp(2, s % 4), bank[4 + s % 2][:, :], ACT.Gelu,
                               bias=cols[:, C_MB1 + s % NH:C_MB1 + s % NH + 1]).then_inc(S("C_gl"), 1)
                if s % NH == 2 and s > NH:
                    mlp_out(s // NH - 1)
            mlp_out(B - 1)

            ln("ln6", feat)
            route("D", "ln6", ED)

            def unit_d(i, u, first):
                for c in range(B):
                    k = i * (RING * B) + (B * u + c)
                    act.wait_ge(S("D_g"), k + 1)
                    act.activation(temp(5, c % 2), bank[4 + (3 * c) % 4][:, :], ACT.Silu).then_inc(S("D_sil"), 1)
            for u in range(RING):
                unit_d(0, u, True)
            with act.Fori(1, UNITS // RING) as i:
                for u in range(RING):
                    unit_d(i, u, False)
            acc_out("D")

        @block.vector
        def _(dve):
            link = Chain(dve, S("dve_self"))
            v = nc.vector

            def ln(tag, src, dst, double, dst_y=None):
                for t in range(NT):
                    if tag == "ln1" and t % QT == 0:
                        dve.wait_ge(S(f"ld_x{t // QT}"), 16)
                    ins = v.bn_stats(stats[:, t, :], src[:, t, :])
                link(ins)
                for t in range(NT):
                    ins = v.bn_aggr(mv[:, t, :], stats[:, t, :])
                link(ins)
                v.tensor_scalar(rstd[:, 0, :], mv[:, :, 1], EPS, None, ALU.add)
                v.tensor_scalar(rstd[:, 1, :], mv[:, :, 1], 1.0 + EPS, EPS * EPS, ALU.mult,
                                ALU.add).then_inc(S("ln_var"), 1)
                dve.wait_ge(S("ln_std"), int(tag[2]))
                v.reciprocal(rstd[:, :, :], rstd[:, :, :]).then_inc(S("ln_rstd"), 1)
                dve.wait_ge(S("ln_rstd"), int(tag[2]))
                r = 1 if double else 0
                for t in range(BY_DVE * QT):
                    ins = v.tensor_scalar(dst[:, t, :], src[:, t, :], mv[:, t, 0:1], rstd[:, r, t:t + 1],
                                          ALU.subtract, ALU.mult)
                    if t % QT == QT - 1:
                        ins.then_inc(S("ln_norm"), 1)
                if dst_y is not None:
                    for t in range(NT):
                        ins = v.tensor_scalar(dst_y[:, t, :], src[:, t, :], mv[:, t, 0:1], rstd[:, 0, t:t + 1],
                                              ALU.subtract, ALU.mult)
                    link(ins)

            def tok(x, c):
                return x[:, QT * c:QT * (c + 1), :].rearrange("p t c -> p (t c)")

            def chunk(n, c):
                return flat(n)[:, c * T:(c + 1) * T]

            dve.wait_ge(S("ld_const"), 48)
            ln("ln1", xres, htok, True, ytok)
            ts = col("ts")
            v.tensor_scalar(shiftc[:, 0:1], ts, 1.0, None, ALU.add)
            link(v.tensor_scalar(shiftc[:, 1:2], ts, -1.0, None, ALU.mult))
            v.tensor_tensor(shiftc[:, 2:3], shiftc[:, 1:2], ts, ALU.mult)
            link(v.tensor_scalar(shiftc[:, 3:4], shiftc[:, 1:2], 1.0, None, ALU.add))
            link(v.tensor_scalar(shiftc[:, 4:5], col("u"), -1.0, None, ALU.mult))
            K_, V_, R_, M_, D_, AA = 1, 2, 3, 4, 5, 10
            G_, B_, E1, E2, DL, X_, TMP = 6, 7, 8, 9, 11, 13, 14
            v.memset(seq(M_)[:, :, 0:1], 0.0)
            v.memset(seq(D_)[:, :, 0:1], 1.0)
            v.memset(seq(AA)[:, :, 0:1], 0.0)
            for c in range(B):
                dve.wait_ge(S("ln_F"), ln_count("ln1", c))
                h = feat[:, c * T:(c + 1) * T]
                link(v.tensor_scalar(chunk(TMP, c), h, shiftc[:, 0:1], None, ALU.mult))
                v.tensor_scalar(chunk(X_, c)[:, 0:1], chunk(TMP, c)[:, 0:1], shiftc[:, 2:3], None, ALU.add)
                v.scalar_tensor_tensor(chunk(X_, c)[:, 1:T], h[:, 0:T - 1], shiftc[:, 1:2],
                                       chunk(TMP, c)[:, 1:T], ALU.mult, ALU.add).then_inc(S("A_xxx"), 1)
            own = Marks(dve, S("dve_own"))
            maxed, summed, scaled, scanned, shared, mixed = [], [], [], [], [], []

            def before(n, c):
                return seq(n)[:, c, 0:T]
            for c in range(B):
                dve.wait_ge(S("A_kvs"), 2 * c + 1)
                maxed.append(own.mark(v.tensor_tensor_scan(seq(M_)[:, c, 1:], chunk(K_, c), chunk(K_, c), 0.0,
                                                           ALU.max, ALU.max)))
            for c in range(B):
                own.need(maxed[c])
                v.tensor_tensor(chunk(G_, c), before(M_, c), seq(M_)[:, c, 1:], ALU.subtract).then_inc(S("A_gx"), 1)
                v.tensor_tensor(chunk(B_, c), chunk(K_, c), seq(M_)[:, c, 1:], ALU.subtract).then_inc(S("A_bx"), 1)
            for c in range(B):
                dve.wait_ge(S("A_exps"), 2 * c + 2)
                v.tensor_tensor_scan(seq(D_)[:, c, 1:], chunk(G_, c), chunk(B_, c), 1.0, ALU.mult,
                                     ALU.add).then_inc(S("A_D"), 1)
            for c in range(B):
                dve.wait_ge(S("A_ln"), c + 1)
                summed.append(own.mark(v.tensor_tensor(chunk(DL, c), chunk(DL, c), before(M_, c), ALU.add)))
            for c in range(B):
                own.need(summed[c])
                v.tensor_tensor(chunk(DL, c), chunk(DL, c), chunk(K_, c), ALU.subtract).then_inc(S("A_d"), 1)
            for c in range(B):
                dve.wait_ge(S("A_d"), c + 1)
                v.tensor_scalar(chunk(E1, c), chunk(DL, c), 0.0, None, ALU.min)
                v.tensor_scalar(chunk(E2, c), chunk(DL, c), 0.0, -1.0, ALU.max, ALU.mult).then_inc(S("A_x"), 1)
            for c in range(B):
                dve.wait_ge(S("A_e"), 2 * c + 2)
                dve.wait_ge(S("A_kvs"), 2 * c + 2)
                scaled.append(own.mark(v.tensor_tensor(chunk(E2, c), chunk(E2, c), chunk(V_, c), ALU.mult)))
            for c in range(B):
                own.need(scaled[c])
                scanned.append(own.mark(v.tensor_tensor_scan(seq(AA)[:, c, 1:], chunk(E1, c), chunk(E2, c), 0.0,
                                                             ALU.mult, ALU.add)))
            for c in range(B):
                own.need(scanned[c])
                dve.wait_ge(S("A_s"), 2 * c + 2)
                shared.append(own.mark(v.tensor_tensor(chunk(G_, c), chunk(G_, c), before(AA, c), ALU.mult)))
            for c in range(B):
                own.need(shared[c])
                dve.wait_ge(S("A_sv"), c + 1)
                mixed.append(own.mark(v.tensor_tensor(chunk(G_, c), chunk(G_, c), chunk(B_, c), ALU.add)))
            for c in range(B):
                own.need(mixed[c])
                dve.wait_ge(S("A_rs"), c + 1)
                v.tensor_tensor(chunk(E1, c), chunk(G_, c), chunk(R_, c), ALU.mult).then_inc(S("A_z"), 1)
            for c in range(B):
                dve.wait_ge(S("A_zT"), c + 1)
                ins = v.tensor_tensor(tok(ytok, c), tok(ytok, c), bank[c][:, :], ALU.add)
            link(ins)
            link(v.tensor_tensor(xres[:, :, :], xres[:, :, :], ytok[:, :, :], ALU.add))
            ln("ln2", ytok, htok, False)
            for c in range(B):
                dve.wait_ge(S("ln_F"), ln_count("ln2", c))
                h = feat[:, c * T:(c + 1) * T]
                link(v.tensor_scalar(chunk(TMP, c), h, shiftc[:, 3:4], None, ALU.mult))
                v.scalar_tensor_tensor(chunk(X_, c)[:, 0:1], h[:, T - 1:T], ts,
                                       chunk(TMP, c)[:, 0:1], ALU.mult, ALU.add)
                v.scalar_tensor_tensor(chunk(X_, c)[:, 1:T], h[:, 0:T - 1], ts,
                                       chunk(TMP, c)[:, 1:T], ALU.mult, ALU.add).then_inc(S("A_xx2"), 1)
            dve.wait_ge(S("A_rcs"), B)
            for c in range(B):
                for j in range(4):
                    s = 4 * c + j
                    dve.wait_ge(S("A_rl"), s + 1)
                    if s >= 4:
                        dve.wait_ge(S("A_vv"), s - 3)
                    v.tensor_tensor(temp(5, s % 4), temp(4, s % 4), temp(4, s % 4), ALU.mult).then_inc(S("A_sq"), 1)
                dve.wait_ge(S("A_vv"), 4 * (c + 1))
                v.tensor_tensor(chunk(7, c), chunk(3, c), bank[6 + c % 2][:, :], ALU.mult).then_inc(S("A_vz"), 1)
            for c in range(B):
                dve.wait_ge(S("A_vT"), c + 1)
                ins = v.tensor_tensor(tok(xres, c), tok(xres, c), bank[c][:, :], ALU.add)
                ins.then_inc(S("A_out"), 1)
            dve.wait_ge(S("A_out"), B)

            def route(tag, ne, soft):
                def e3(n):
                    return flat(n)[:, 0:NT * ne].rearrange("p (t e) -> p t e", e=ne)

                def e2(n):
                    return flat(n)[:, 0:NT * ne]

                def wide(a):
                    return a.unsqueeze(2).broadcast_to([P, NT, ne])

                def over(row):
                    return row.unsqueeze(1).broadcast_to([P, NT, ne])
                logits, bias = bank[4][:, 0:NT * ne].rearrange("p (t e) -> p t e", e=ne), \
                    over(rows[:, 0:EB] if tag == "B" else rows[:, EB:EB + ED])
                rk = over(rank[:, ED - ne:])
                EX, BI, EQ, OH, CW = 5, 6, 7, 9, 10
                m, s = small[:, 0, :], small[:, 1, :]
                dve.wait_ge(S(f"{tag}_lg"), 1)
                if soft:
                    link(v.tensor_reduce(m, logits, AX, ALU.max))
                    v.tensor_tensor(e3(EX), logits, wide(m), ALU.subtract).then_inc(S(f"{tag}_ex"), 1)
                    dve.wait_ge(S(f"{tag}_exp"), 1)
                    link(v.tensor_reduce(s, e3(EX), AX, ALU.add))
                    link(v.reciprocal(s, s))
                    link(v.tensor_tensor(e3(EX), e3(EX), wide(s), ALU.mult))
                    link(v.tensor_tensor(e3(BI), e3(EX), bias, ALU.add))
                else:
                    link(v.tensor_tensor(e3(BI), logits, bias, ALU.add))
                for r in range(2):
                    mx = small[:, 2 + r, :]
                    link(v.tensor_reduce(mx, e3(BI), AX, ALU.max))
                    link(v.tensor_tensor(e3(EQ), e3(BI), wide(mx), ALU.is_equal))
                    link(v.tensor_tensor(e3(EQ), e3(EQ), rk, ALU.mult))
                    link(v.tensor_reduce(small[:, 4, :], e3(EQ), AX, ALU.max))
                    link(v.tensor_tensor(e3(OH + 2 * r), rk, wide(small[:, 4, :]), ALU.is_equal))
                    if r == 0:
                        link(v.scalar_tensor_tensor(e2(BI), e2(OH), FILL, e2(BI), ALU.mult, ALU.add))
                cw = cw_all if tag == "B" else cw_full
                if tag == "B":
                    link(v.memset(cw[:, :, ne:], 1.0))
                if soft:
                    link(v.tensor_tensor(e2(OH), e2(OH), e2(OH + 2), ALU.add))
                    v.tensor_tensor(cw[:, :, 0:ne], e3(EX), e3(OH), ALU.mult).then_inc(S(f"{tag}_cw"), 1)
                else:
                    v.tensor_tensor(flat(EX)[:, 0:NT], small[:, 3, :], small[:, 2, :],
                                    ALU.subtract)
                    v.memset(flat(EX)[:, NT:NT * ne], 0.0).then_inc(S(f"{tag}_ex"), 1)
                    dve.wait_ge(S(f"{tag}_exp"), 1)
                    ex = flat(EX)[:, 0:NT]
                    link(v.tensor_scalar(s, ex, 1.0, None, ALU.add))
                    link(v.reciprocal(s, s))
                    link(v.tensor_tensor(m, ex, s, ALU.mult))
                    v.tensor_tensor(e3(OH), e3(OH), wide(s), ALU.mult)
                    link(v.tensor_tensor(e3(OH + 2), e3(OH + 2), wide(m), ALU.mult))
                    link(v.tensor_tensor(cw[:, :, 0:ne], e3(OH), e3(OH + 2), ALU.add))
                    for a in range(PARTS):
                        link(v.tensor_copy(cw_bf, cw))
                        ins = v.tensor_copy(cw_parts[:, :, 32 * a:32 * a + ne + 1], cw_bf)
                        if a < PARTS - 1:
                            link(v.tensor_tensor(cw, cw, cw_bf, ALU.subtract))
                    ins.then_inc(S("D_cw"), 1)

            def add_back(tag):
                for c in range(B):
                    dve.wait_ge(S(f"{tag}_oT"), c + 1)
                    v.tensor_tensor(tok(xres, c), tok(xres, c), bank[4 + c][:, :], ALU.add).then_inc(S(f"{tag}_out"), 1)
                dve.wait_ge(S(f"{tag}_out"), B)

            ln("ln3", xres, htok_b, False)
            route("B", EB, True)

            def hidden_b(i, u, c, first):
                k, l = i * LOOP + (B * u + c), B * u + c

                def bias(n):
                    return flat(u)[:, 5 * P + n:5 * P + n + 1]
                even, odd, g = temp(7, c % 2), temp(7, 2 + c % 2), temp(6, 2 + c % 2)
                dve.wait_ge(S("B_h3e"), k + 1)
                dve.wait_ge(S("B_t1"), k + 1)
                v.scalar_tensor_tensor(even, up_bank(l, 1)[:, :], bias(2), temp(5, c % 2),
                                       ALU.add, ALU.mult).then_inc(S("B_pe"), 1)
                dve.wait_ge(S("B_h3o"), k + 1)
                dve.wait_ge(S("B_t2"), k + 1)
                v.scalar_tensor_tensor(odd, up_bank(l, 3)[:, :], bias(3), temp(5, 2 + c % 2),
                                       ALU.add, ALU.mult).then_inc(S("B_po"), 1)
                dve.wait_ge(S("B_pe"), k + 1)
                if not (first and l < 2):
                    dve.wait_ge(S("B_sg"), k - 1)
                v.tensor_scalar(g, even, 7.0, None, ALU.min).then_inc(S("B_g"), 1)
                dve.wait_ge(S("B_po"), k + 1)
                v.tensor_scalar(odd, odd, 7.0, -7.0, ALU.min, ALU.max).then_inc(S("B_lin"), 1)
                dve.wait_ge(S("B_lin"), k + 1)
                dve.wait_ge(S("B_g"), k + 1)
                if not (first and l < 2):
                    dve.wait_ge(S("B_a"), k - 1)
                v.scalar_tensor_tensor(temp(8, c % 2), odd, 1.0, g, ALU.add, ALU.mult).then_inc(S("B_l"), 1)

            def add_b(i, l, first):
                u, c, k = l // B, l % B, i * LOOP + l
                dve.wait_ge(S("B_down"), k + 1)
                dve.wait_ge(S("B_cwu"), i * RING + (u + 1))
                if not (first and l < B):
                    dve.wait_ge(S("B_y"), k - 3)
                for t in range(QT):
                    tile = xres[:, QT * c + t, :]
                    ins = v.scalar_tensor_tensor(tile, bank[6 + l % 2][:, t * P:(t + 1) * P],
                                                 cw_unit[u][:, QT * c + t:QT * c + t + 1], tile, ALU.mult, ALU.add)
                ins.then_inc(S("B_y"), 1)

            def steps_b(i, first):
                for l in range(LOOP):
                    hidden_b(i, l // B, l % B, first)
                    if l >= 2:
                        add_b(i, l - 2, first)
                    elif not first:
                        add_b(i - 1, LOOP + l - 2, False)
            steps_b(0, True)
            with dve.Fori(1, UNITS // RING) as i:
                steps_b(i, False)
            for l in (LOOP - 2, LOOP - 1):
                add_b(UNITS // RING - 1, l, False)
            dve.wait_ge(S("B_y"), UNITS * B)
            for c in range(B):
                dve.wait_ge(S("B_bias"), c + 1)
                v.tensor_tensor(tok(xres, c), tok(xres, c), bank[c][:, :], ALU.add).then_inc(S("B_out"), 1)
            dve.wait_ge(S("B_out"), B)

            ln("ln4", xres, htok_c, True, ytok)
            dve.wait_ge(S("C_gate"), 1)
            gv = gates[:, :].rearrange("p (n k) -> p n k", k=2 * G)[:, :, G:]
            v.tensor_scalar(gv, gv, -1.0, 1.0, ALU.mult, ALU.add)
            for c in range(B):
                dve.wait_ge(S("C_k"), c + 1)
                link(v.tensor_scalar(ksum[:, c:c + 1], ksum[:, c:c + 1], 1.0 / T, None, ALU.mult))
                v.tensor_scalar(chunk(14, c), chunk(14, c), ksum[:, c:c + 1], None,
                                ALU.subtract).then_inc(S("C_kc"), 1)
            def part(w, a, c):
                return split[w][a][:, c * T:(c + 1) * T]
            for c in range(B):
                dve.wait_ge(S("C_kc"), c + 1)
                v.tensor_copy(part(1, 0, c), chunk(14, c)).then_inc(S("C_k1"), 1)
            for c in range(B):
                dve.wait_ge(S("C_k1"), c + 1)
                v.tensor_tensor(chunk(9, c), chunk(14, c), part(1, 0, c), ALU.subtract).then_inc(S("C_kr"), 1)
            for c in range(B):
                dve.wait_ge(S("C_kr"), c + 1)
                v.tensor_copy(part(1, 1, c), chunk(9, c)).then_inc(S("C_k2"), 1)
            for c in range(B):
                dve.wait_ge(S("C_k2"), c + 1)
                v.tensor_tensor(part(1, 2, c), chunk(9, c), part(1, 1, c), ALU.subtract).then_inc(S("C_ksplit"), 1)
            for c in range(B):
                dve.wait_ge(S("C_q2"), c + 1)
                v.tensor_tensor(part(0, 2, c), chunk(8, c), part(0, 1, c), ALU.subtract).then_inc(S("C_qsplit"), 1)
            dve.wait_ge(S("ld_qkv"), 32)
            for c in range(B):
                dve.wait_ge(S("C_gram"), c + 1)
                v.tensor_tensor(temp(1, c)[:, 0:P], bank[4 + c][:, 0:P], blockmask, ALU.mult).then_inc(S("C_gm"), 1)
            for c in range(B):
                dve.wait_ge(S("C_gq"), c + 1)
                v.tensor_tensor(chunk(2, c), chunk(13, c), bank[c][:, :], ALU.mult).then_inc(S("C_qgq"), 1)
            dve.wait_ge(S("C_sig"), 1)
            dve.wait_ge(S("C_qkout"), 16 * 2 * PARTS)
            me = Marks(dve, S("dve_loop"))
            any_bad, bad = dve.alloc_register("any_bad"), dve.alloc_register("bad")

            def step(i, s, cur, prev, old):
                static = isinstance(i, int)
                n = 2 * i + s if static else i * 2 + s
                o = 1 - s

                def take():
                    at = n * G
                    sig = sig_all[:, at:at + G] if static else sig_all[:, bass.ds(at, G)]
                    v.tensor_scalar(gain[:, s, :], sig, -GAIN / 2, None, ALU.mult)
                    v.tensor_scalar(nthr[:, s, :], sig, -Z0, None, ALU.mult)
                    v.tensor_scalar(firstthr[:, :], sig, Z0, None, ALU.mult)
                    for j in range(G):
                        dve.wait_ge(S("C_s"), n * G + j + 1)
                        ins = v.tensor_scalar(score[s][:, j, :], bank[j % 4][:, :], 1.0, None, ALU.mult, ALU.max,
                                              accum_out=rmax[:, s, j:j + 1])
                        ins.then_inc(S("C_take"), 1)

                def first_counts():
                    for j in range(BY_ACT, G):
                        dve.wait_ge(S("C_take"), n * G + j + 1)
                        ins = v.tensor_scalar(marks_of[j - BY_ACT], score[s][:, j, :], firstthr[:, j:j + 1], None,
                                              ALU.is_gt, ALU.add, accum_out=above[:, j:j + 1])
                    return me.mark(ins)

                def update(k):
                    dve.wait_ge(S(f"C_c{k}"), n * BY_ACT + BY_ACT if k == 1 else n * G + G)
                    new, old = exc[:, k % 2, :], exc[:, 1 - k % 2, :]
                    if k > 1:
                        v.scalar_tensor_tensor(move[:, 1, :], cnt[:, s, :], T - 2 * AIM, old, ALU.add, ALU.mult)
                        me.link(v.tensor_scalar(new, cnt[:, s, :], T - 2 * AIM, None, ALU.add))
                        v.tensor_tensor(move[:, 0, :], new, new, ALU.mult)
                        me.link(v.tensor_scalar(move[:, 1, :], move[:, 1, :], 0.0, TURN - 1, ALU.is_lt, ALU.mult))
                        v.scalar_tensor_tensor(gain[:, s, :], move[:, 1, :], 1.0, gain[:, s, :], ALU.add, ALU.mult)
                    else:
                        v.tensor_scalar(new[:, BY_ACT:], above[:, BY_ACT:], 2.0, -2 * AIM, ALU.mult, ALU.add)
                        me.link(v.tensor_scalar(new[:, 0:BY_ACT], cnt[:, s, 0:BY_ACT], T - 2 * AIM, None, ALU.add))
                        me.link(v.tensor_tensor(move[:, 0, :], new, new, ALU.mult))
                    me.link(v.scalar_tensor_tensor(move[:, 2, :], move[:, 0, :], (WIN - 0.5) ** 2, new,
                                                   ALU.is_gt, ALU.mult))
                    me.link(v.tensor_tensor(move[:, 2, :], move[:, 2, :], gain[:, s, :], ALU.mult))
                    v.tensor_tensor(nthr[:, s, :], nthr[:, s, :], move[:, 2, :], ALU.add).then_inc(S(f"C_n{k}"), 1)

                def window(j):
                    buf = work[j % 4:j % 4 + 2]
                    below = [me.mark(v.scalar_tensor_tensor(buf[k], score[o][:, j + k, :], cand[:, j + k, 0:1],
                                                            score[o][:, j + k, :], ALU.is_lt, ALU.mult))
                             for k in (0, 1)]
                    for k in (0, 1):
                        me.need(below[k])
                        last = me.mark(v.max(cand[:, j + k, 1:], buf[k]))
                    return last

                def wide(x):
                    return x.unsqueeze(2).broadcast_to([P, G, WIN])

                def exact(t):
                    here = Marks(dve, S("dve_own"))
                    here.clear()
                    here.link(v.tensor_copy(slow, score[o].rearrange("p j t -> p (j t)")[:, bass.ds(t * T, T)]))
                    for _ in range(TOPK // 8):
                        here.link(v.max(hi[:, :], slow))
                        here.link(v.match_replace(slow, hi[:, :], slow, FILL))
                    here.link(v.scalar_tensor_tensor(
                        sparse.rearrange("p j t -> p (j t)")[:, bass.ds(t * T, T)], slow, FILL,
                        prob[o].rearrange("p j t -> p (j t)")[:, bass.ds(t * T, T)],
                        ALU.is_equal, ALU.mult, accum_out=zz[:, o, bass.ds(t + G, 1)]))

                def fix():
                    u32 = mybir.dt.uint32
                    dve.reg_load(any_bad, flags[0:1, G:G + 1].bitcast(u32))
                    with dve.If_ne(any_bad, ALL_BITS):
                        me.need(me.k)
                        here = Marks(dve, S("dve_own"))
                        here.clear()
                        here.link(v.tensor_scalar(flags[:, 0:G], bank[7][0:1, 0:G], P - 0.5, None, ALU.is_lt))
                        here.link(v.tensor_tensor(flags[:, G + 1:2 * G + 1], flags[:, 0:G], places[0:1, :], ALU.mult))
                        v.tensor_reduce(flags[:, 2 * G + 2:], flags[:, 0:G], AX, ALU.add)
                        here.link(v.tensor_reduce(flags[:, 2 * G + 1:2 * G + 2], flags[:, G + 1:2 * G + 1], AX, ALU.max))
                        here.link(v.tensor_copy(last_bad[:, :], flags[:, 2 * G + 1:2 * G + 2]))
                        last = dve.value_load(last_bad[:, :], min_val=0, max_val=G - 1)
                        dve.reg_load(any_bad, flags[0:1, 2 * G + 2:].bitcast(u32))
                        exact(last)
                        with dve.If_ne(any_bad, ONE_BITS):
                            with dve.Fori(0, G) as t:
                                dve.reg_load(bad, flags[0:1, bass.ds(t, 1)].bitcast(u32))
                                with dve.If_ne(bad, 0):
                                    exact(t)
                                dve.nop()
                            dve.nop()
                        dve.nop()

                def maxima():
                    dve.wait_ge(S("C_take"), n * G + G)
                    v.tensor_scalar(nmax[:, s, :], rmax[:, s, :], -SCALE, None, ALU.mult).then_inc(S("C_nm"), 1)

                r, good = thr[:, 0, :], thr[:, 3, :]
                h3 = [hit[:, k, :].rearrange("p (j w) -> p j w", j=G) for k in range(3)]
                if cur:
                    take()
                    maxima()
                    counted = first_counts()
                if old:
                    keep_out(n - 3)
                if prev:
                    dve.wait_ge(S("C_c4"), n * G)
                    v.tensor_scalar(cand[:, :, 0], nthr[:, o, :], -1.0, None, ALU.mult)
                    ranked = me.mark(v.tensor_scalar(r, cnt[:, o, :], -0.5, TOPK - T / 2, ALU.mult, ALU.add))
                if cur:
                    me.need(counted)
                    update(1)
                if prev:
                    me.need(ranked)
                    for j in range(0, G, 2):
                        last = window(j)
                        if j == 0:
                            v.tensor_tensor(h3[0], places.unsqueeze(1).broadcast_to([P, G, WIN]), wide(r), ALU.is_equal)
                        if cur and j == 4:
                            update(2)
                    me.need(last)
                    v.tensor_tensor(h3[1], h3[0], cand[:, :, 0:WIN], ALU.mult)
                    me.link(v.tensor_tensor(h3[2], h3[0], cand[:, :, 1:], ALU.mult))
                    me.link(v.tensor_reduce(thr[:, 1:3, :].rearrange("p k j -> p (k j)"),
                                            hit[:, 1:3, :].rearrange("p k (j w) -> p (k j) w", j=G), AX, ALU.add))
                    v.scalar_tensor_tensor(good, thr[:, 2, :], 0.0, thr[:, 1, :], ALU.max,
                                           ALU.is_lt).then_inc(S("C_good"), 1)
                    for j in range(G):
                        dve.wait_ge(S("C_exp"), (n - 1) * G + j + 1)
                        if not (static and n < 2):
                            dve.wait_ge(S("C_pT"), (n - 2) * G + j + 1)
                        me.mark(v.scalar_tensor_tensor(sparse[:, j, :], score[o][:, j, :], thr[:, 1, j:j + 1],
                                                       prob[o][:, j, :], ALU.is_ge, ALU.mult,
                                                       accum_out=zz[:, o, G + j:G + j + 1]))
                        if cur and j == 2:
                            update(3)
                        if j == 5:
                            dve.wait_ge(S("C_flag"), n)
                            me.mark(v.tensor_reduce(flags[:, G:G + 1], bank[7][0:1, 0:G], AX, ALU.min))
                    me.need(me.k - 1)
                    fix()
                    me.need(me.k)
                    me.link(v.reciprocal(zz[:, o, :], zz[:, o, :]))
                    at = (n - 1) * 2 * G
                    gt = gates[:, at:at + 2 * G] if static else gates[:, bass.ds(at, 2 * G)]
                    v.tensor_tensor(cc[:, o, :], zz[:, o, :], gt, ALU.mult).then_inc(S("C_cc"), 1)
                else:
                    for k in (2, 3):
                        update(k)
            def keep_out(m):
                dve.wait_ge(S("C_pv"), m * G + G + 2 * G)
                w = G * DK
                dst = o_all[:, m * w:m * w + w] if isinstance(m, int) else o_all[:, bass.ds(m * w, w)]
                v.tensor_copy(dst, bank[4][:, 0:w]).then_inc(S("C_o"), 1)
            me.clear()
            step(0, 0, True, False, False)
            step(0, 1, True, True, False)
            me.clear()
            step(1, 0, True, True, False)
            step(1, 1, True, True, True)
            with dve.Fori(2, NI) as i:
                me.clear()
                step(i, 0, True, True, True)
                step(i, 1, True, True, True)
            me.clear()
            step(NI, 0, False, True, True)
            dve.wait_ge(S("C_cc"), NG)
            scaled = [me.mark(v.tensor_scalar(prob[1][:, j, :], prob[1][:, j, :], cc[:, 1, j:j + 1], None, ALU.mult))
                      for j in range(LAST_BY_DVE)]
            for j in range(LAST_BY_DVE):
                me.need(scaled[j])
                v.scalar_tensor_tensor(sparse[:, j, :], sparse[:, j, :], cc[:, 1, G + j:G + j + 1],
                                       prob[1][:, j, :], ALU.mult, ALU.add).then_inc(S("C_cc"), 1)
            keep_out(NG - 2)
            keep_out(NG - 1)
            dve.wait_ge(S("C_o"), NG + 1)
            for b in range(B):
                for q in range(QT):
                    src = o_all[:, :].rearrange("p (g b s q d) -> p g b s q d", g=HG, b=B, s=HG, q=QT)
                    v.tensor_copy(o_tok[:, b * QT + q, :].rearrange("p (g s d) -> p g s d", g=HG, s=HG),
                                  src[:, :, b, :, q, :]).then_inc(S("C_otok"), 1)

            def token_add(tag, out_sem):
                for c in range(B):
                    dve.wait_ge(S(tag), c + 1)
                    ins = v.scalar_tensor_tensor(tok(ytok, c), bank[4 + c][:, :], col("alpha"), tok(ytok, c),
                                                 ALU.mult, ALU.add)
                link(ins)
            token_add("C_aT", None)
            ln("ln5", ytok, htok_d, False)
            v.memset(cw_full[:, :, ED:], 1.0)
            v.tensor_copy(halfsel_bf, halfsel)
            link(v.memset(cw_parts, 0.0))
            token_add("C_mT", None)
            for c in range(B):
                v.tensor_tensor(tok(xres, c), tok(xres, c), tok(ytok, c), ALU.add).then_inc(S("C_out"), 1)
            dve.wait_ge(S("C_out"), B)

            ln("ln6", xres, htok_b, False)
            route("D", ED, False)

            def unit_d(i, u, first):
                for c in range(B):
                    k = i * (RING * B) + (B * u + c)
                    dve.wait_ge(S("D_u"), k + 1)
                    dve.wait_ge(S("D_sil"), k + 1)
                    v.tensor_tensor(temp(9, c % 2), temp(5, c % 2), bank[4 + (3 * c + 1) % 4][:, :],
                                    ALU.mult).then_inc(S("D_us"), 1)
                    dve.wait_ge(S("D_us"), k + 1)
                    if not (first and u == 0 and c < 2):
                        dve.wait_ge(S("D_down"), k - 1)
                    dve.wait_ge(S("D_bc"), k + 1)
                    v.tensor_tensor(temp(9, 2 + c % 2), temp(9, c % 2), bank[4 + (3 * c + 2) % 4][:, :],
                                    ALU.mult).then_inc(S("D_a"), 1)
            for u in range(RING):
                unit_d(0, u, True)
            with dve.Fori(1, UNITS // RING) as i:
                for u in range(RING):
                    unit_d(i, u, False)
            add_back("D")

        @block.tensor
        def _(pe):
            mm = nc.tensor.matmul

            def chunk(n, c):
                return flat(n)[:, c * T:(c + 1) * T]

            def ln(tag, src):
                for c in range(B):
                    pe.wait_ge(S("ln_norm" if c < BY_DVE else "ln_norm_gp"), norm_count(tag, c))
                    for t in range(QT):
                        ins = nc.tensor.transpose(bank[c][:, t * P:(t + 1) * P], src[:, QT * c + t, :], ident)
                    ins.then_inc(S("ln_T"), 1)

            def to_tokens(src, c, dst):
                for t in range(QT):
                    ins = nc.tensor.transpose(dst[:, t * P:(t + 1) * P], src[:, t * P:(t + 1) * P], ident)
                return ins

            pe.wait_ge(S("ld_const"), 48)
            ln("ln1", htok)
            pe.wait_ge(S("ld_wa"), 16)
            for c in range(B):
                pe.wait_ge(S("A_xxx"), c + 1)
                mm(bank[c][:, :], wk, chunk(13, c), start=True, stop=True)
                mm(bank[4 + c][:, :], wv, chunk(13, c), start=True, stop=True).then_inc(S("A_kv"), 1)
            for c in range(B):
                pe.wait_ge(S("A_kvs"), 2 * (c + 1))
                mm(bank[c][:, :], wr, chunk(13, c), start=True, stop=True).then_inc(S("A_r"), 1)
            for c in range(B):
                pe.wait_ge(S("A_z"), c + 1)
                to_tokens(chunk(8, c), c, bank[c]).then_inc(S("A_zT"), 1)
            ln("ln2", htok)
            for c in range(B):
                pe.wait_ge(S("A_xx2"), c + 1)
                mm(bank[c][:, :], wcr, chunk(13, c), start=True, stop=True).then_inc(S("A_rc"), 1)

            def up(s):
                if s >= 2:
                    pe.wait_ge(S("A_rl"), s - 1)
                mm(bank[4 + s % 2][:, :], wck[:, (s % 4) * P:(s % 4 + 1) * P], chunk(13, s // 4),
                   start=True, stop=True).then_inc(S("A_kc"), 1)
            up(0)
            up(1)
            for s in range(4 * B):
                if s + 2 < 4 * B:
                    up(s + 2)
                if s % 4 == 0 and s >= 8:
                    pe.wait_ge(S("A_vz"), s // 4 - 1)
                pe.wait_ge(S("A_sq"), s + 1)
                mm(bank[6 + s // 4 % 2][:, :], wcv[:, (s % 4) * P:(s % 4 + 1) * P], temp(5, s % 4),
                   start=(s % 4 == 0), stop=(s % 4 == 3)).then_inc(S("A_vv"), 1)
            for c in range(B):
                pe.wait_ge(S("A_vz"), c + 1)
                to_tokens(chunk(7, c), c, bank[c]).then_inc(S("A_vT"), 1)

            def route(tag, ne, w):
                pe.wait_ge(S("ln_F"), ln_count("ln3" if tag == "B" else "ln6", B - 1))
                for t in range(NT):
                    ins = mm(bank[4][:, t * ne:(t + 1) * ne], feat[:, t * P:(t + 1) * P], w, start=True, stop=True)
                ins.then_inc(S(f"{tag}_lg"), 1)
                pe.wait_ge(S(f"{tag}_cw"), 1)
                cw, rows_n = (cw_all, ne + 1) if tag == "B" else (cw_parts, SPLIT_ROWS)
                for c in range(B):
                    for t in range(QT):
                        ins = nc.tensor.transpose(bank[4 + c][0:rows_n, t * P:(t + 1) * P], cw[:, QT * c + t, :], ident)
                    ins.then_inc(S(f"{tag}_cwTp"), 1)
                pe.wait_ge(S(f"{tag}_cwT"), B)

            def moe(tag, ne, products, sel, tail):
                npr = len(products) + 1

                def step(i, u, c, first):
                    k = i * (RING * B) + (B * u + c)
                    if c == 0:
                        pe.wait_ge(S(f"{tag}_w{u}"), i * 16 + 16)
                    for n, (done, w, reader, lag) in enumerate(products):
                        if not (first and u == 0 and c < lag):
                            pe.wait_ge(S(reader), k - lag + 1)
                        mm(bank[4 + (npr * c + n) % 4][:, :], flat(u)[:, w * P:(w + 1) * P],
                           feat[:, c * T:(c + 1) * T], start=True, stop=True).then_inc(S(done), 1)
                    reader, lag = sel[1], sel[2]
                    if not (first and u == 0 and c < lag):
                        pe.wait_ge(S(reader), k - lag + 1)
                    pe.wait_ge(S(f"{tag}_msk"), k + 1)
                    mm(bank[4 + (npr * c + npr - 1) % 4][:, :], sel[0], cw_masked[c % 2],
                       start=True, stop=True).then_inc(S(f"{tag}_bc"), 1)

                def down(i, u, c, first):
                    k = i * (RING * B) + (B * u + c)
                    pe.wait_ge(S(f"{tag}_a"), k + 1)
                    mm(bank[c][:, :], flat(u)[:, len(products) * P:(len(products) + 1) * P], temp(9, 2 + c % 2),
                       start=(first and u == 0), stop=False, skip_group_check=True).then_inc(S(f"{tag}_down"), 1)

                def body(i, first):
                    for l in range(RING * B):
                        step(i, l // B, l % B, first)
                        if l:
                            down(i, (l - 1) // B, (l - 1) % B, first)
                    down(i, RING - 1, B - 1, first)
                body(0, True)
                with pe.Fori(1, UNITS // RING) as i:
                    body(i, False)
                tail()

            def finish(tag):
                for c in range(B):
                    pe.wait_ge(S(f"{tag}_accs"), c + 1)
                    to_tokens(chunk(8, c), c, bank[4 + c]).then_inc(S(f"{tag}_oT"), 1)

            pe.wait_ge(S("A_out"), B)
            ln("ln3", htok_b)
            pe.wait_ge(S("ld_b"), 32)
            route("B", EB, rt[:, 0:EB])

            def products_b(i, l, first):
                u, c, k = l // B, l % B, i * LOOP + l
                if c == 0:
                    pe.wait_ge(S(f"B_w{u}"), i * 16 + 16)
                for n, (done, w, reader, lag) in enumerate((("B_h1e", 0, "B_t2", 2), ("B_h3e", 2, "B_po", 2),
                                                            ("B_h1o", 1, "B_t1", 1), ("B_h3o", 3, "B_pe", 1))):
                    if not (first and 4 * l + n < 6):
                        pe.wait_ge(S(reader), k - lag + 1)
                    mm(up_bank(l, n)[:, :], flat(u)[:, w * P:(w + 1) * P], feat[:, c * T:(c + 1) * T],
                       start=True, stop=True).then_inc(S(done), 1)

            def down_b(i, l, first):
                u, c, k = l // B, l % B, i * LOOP + l
                pe.wait_ge(S("B_a"), k + 1)
                if not (first and l < 2):
                    pe.wait_ge(S("B_y"), k - 1)
                for t in range(QT):
                    ins = mm(bank[6 + l % 2][:, t * P:(t + 1) * P], temp(9, c)[:, t * P:(t + 1) * P],
                             flat(u)[:, 4 * P:5 * P], start=True, stop=True)
                ins.then_inc(S("B_down"), 1)

            def steps_b(i, first):
                for l in range(LOOP):
                    products_b(i, l, first)
                    if l >= 2:
                        down_b(i, l - 2, first)
                    elif not first:
                        down_b(i - 1, LOOP + l - 2, False)
            steps_b(0, True)
            with pe.Fori(1, UNITS // RING) as i:
                steps_b(i, False)
            for l in (LOOP - 2, LOOP - 1):
                down_b(UNITS // RING - 1, l, False)
            for c in range(B):
                for t in range(QT):
                    at = c * T + t * P
                    ins = mm(bank[c][:, t * P:(t + 1) * P], flat(3)[0:EB + 1, at:at + P], b2[:, :],
                             start=True, stop=True)
                ins.then_inc(S("B_bias"), 1)

            pe.wait_ge(S("B_out"), B)
            ln("ln4", htok_c)
            pe.wait_ge(S("ld_qkv"), 32)
            for c in range(B):
                pe.wait_ge(S("ln_F"), ln_count("ln4", c))
                mm(bank[c][:, :], wqkv[:, P:2 * P], feat[:, c * T:(c + 1) * T],
                   start=True, stop=True).then_inc(S("C_pk"), 1)
            for c in range(B):
                mm(bank[4 + c][:, :], wqkv[:, 0:P], feat[:, c * T:(c + 1) * T],
                   start=True, stop=True).then_inc(S("C_pq"), 1)
            for c in range(B):
                pe.wait_ge(S("C_kc"), c + 1)
                to_tokens(chunk(14, c), c, bank[c]).then_inc(S("C_kT"), 1)
            for c in range(B):
                pe.wait_ge(S("C_ktok"), c + 1)
                pe.wait_ge(S("C_q"), c + 1)
                for t in range(QT):
                    kt = chunk(0, c)[:, t * P:(t + 1) * P]
                    ins = mm(bank[4 + c][:, 0:P], kt, kt, start=(t == 0), stop=(t == QT - 1))
                ins.then_inc(S("C_gram"), 1)
            for c in range(B):
                pe.wait_ge(S("C_gm"), c + 1)
                mm(bank[c][:, :], temp(1, c)[:, 0:P], chunk(13, c), start=True, stop=True).then_inc(S("C_gq"), 1)
            for c in range(B):
                pe.wait_ge(S("C_qgq"), c + 1)
                for q in range(QT):
                    ins = mm(bank[6][:, (c * QT + q) * HEADS:(c * QT + q + 1) * HEADS],
                             chunk(2, c)[:, q * P:(q + 1) * P], headsel, start=True, stop=True)
            ins.then_inc(S("C_var"), 1)
            for t in range(NT):
                if t >= 2:
                    pe.wait_ge(S("C_vs"), t - 1)
                mm(bank[4 + t % 2][:, 0:P], feat[:, t * P:(t + 1) * P], wqkv[:, 2 * P:],
                   start=True, stop=True).then_inc(S("C_v"), 1)
            pe.wait_ge(S("C_vs"), NT)
            pe.wait_ge(S("C_sig"), 1)
            pe.sem_inc(S("C_pv"), 2 * G)

            def scores(i, s, j, wait_free):
                n = 2 * i + s if isinstance(i, int) else i * 2 + s
                h, q = j // QT, j % QT
                if wait_free:
                    pe.wait_ge(S("C_take"), n * G + j - 3)
                q_rows, k_rows = qk_rows[s]
                mm(bank[j % 4][:, :], q_rows[:, h, q * P:(q + 1) * P], k_rows[:, h, :],
                   start=True, stop=True).then_inc(S("C_s"), 1)

            def pv(n, i, s, j):
                pe.wait_ge(S("C_pTs"), n * G + j + 1 + 2)
                if j == 0:
                    pe.wait_ge(S("C_o"), n + 1)
                w = HG * DK
                for kc in range(QT):
                    at = i * P + kc * w + (2 * s + j // QT) * DK
                    vals = v_all[:, at:at + DK] if isinstance(i, int) else v_all[:, bass.ds(at, DK)]
                    ins = mm(bank[4][:, j * DK:(j + 1) * DK], pT[j % 4][:, kc, :], vals,
                             start=(kc == 0), stop=(kc == QT - 1))
                ins.then_inc(S("C_pv"), 1)

            def step(i, s, cur, ahead, prev, old):
                n = 2 * i + s if isinstance(i, int) else i * 2 + s
                if cur:
                    for j in range(4, G):
                        scores(i, s, j, True)
                if ahead:
                    pe.wait_ge(S(f"C_qk{1 - s}"), (i + s) * LOADED + LOADED)
                    for a in range(4):
                        scores(i + s, 1 - s, a, True)
                for j in range(G):
                    if old:
                        if not isinstance(n, int) or n - 2 < NG - 1:
                            pe.wait_ge(S("C_mix"), (n - 2) * G + j + 1)
                        elif j < LAST_BY_DVE:
                            pe.wait_ge(S("C_cc"), NG + j + 1)
                        else:
                            pe.wait_ge(S("C_mix"), (n - 2) * G + j - LAST_BY_DVE + 1)
                        pe.wait_ge(S("C_pTs"), (n - 2) * G + j + 1)
                        for kc in range(QT):
                            ins = nc.tensor.transpose(bank[5 + j % 2][:, kc * P:(kc + 1) * P],
                                                      sparse[:, j, kc * P:(kc + 1) * P], ident)
                        ins.then_inc(S("C_pT"), 1)
                    if j == 6 and prev:
                        pe.wait_ge(S("C_good"), n)
                        mm(bank[7][0:1, 0:G], onescol, thr[:, 3, :], start=True, stop=True).then_inc(S("C_flag"), 1)
                    if old and j:
                        pv(n - 2, i - 1, s, j - 1)
                if old:
                    pv(n - 2, i - 1, s, G - 1)

            LOADED = 16 * 2 * 2 * PARTS
            pe.wait_ge(S("C_qk0"), LOADED)
            for j in range(4):
                scores(0, 0, j, False)
            step(0, 0, True, True, False, False)
            step(0, 1, True, True, True, False)
            with pe.Fori(1, NI - 1) as i:
                step(i, 0, True, True, True, True)
                step(i, 1, True, True, True, True)
            step(NI - 1, 0, True, True, True, True)
            step(NI - 1, 1, True, False, True, True)
            step(NI, 0, False, False, True, True)
            step(NI, 1, False, False, False, True)
            pe.wait_ge(S("ld_wo"), 16)
            for c in range(B):
                for t in range(QT):
                    pe.wait_ge(S("C_otok"), QT * c + t + 1)
                    ins = nc.tensor.transpose(bank[4 + c][:, t * P:(t + 1) * P], o_tok[:, QT * c + t, :], ident)
                ins.then_inc(S("C_oT"), 1)
            for c in range(B):
                pe.wait_ge(S("C_oTs"), c + 1)
                mm(bank[c][:, :], flat(0)[:, 0:P], chunk(2, c), start=True, stop=True).then_inc(S("C_ao"), 1)
            for c in range(B):
                pe.wait_ge(S("C_aos"), c + 1)
                to_tokens(chunk(12, c), c, bank[4 + c]).then_inc(S("C_aT"), 1)
            ln("ln5", htok_d)
            pe.wait_ge(S("ld_mlp"), 32)
            pe.wait_ge(S("ln_F"), ln_count("ln5", B - 1))
            NH = HID // P

            def hidden(s):
                if s >= 2:
                    pe.wait_ge(S("C_gl"), s - 1)
                j, c = s % NH, s // NH
                mm(bank[4 + s % 2][:, :], flat(1)[:, j * P:(j + 1) * P], feat[:, c * T:(c + 1) * T],
                   start=True, stop=True).then_inc(S("C_h"), 1)
            hidden(0)
            hidden(1)
            for s in range(NH * B):
                if s + 2 < NH * B:
                    hidden(s + 2)
                j, c = s % NH, s // NH
                pe.wait_ge(S("C_gl"), s + 1)
                mm(bank[c][:, :], flat(1)[:, HID + j * P:HID + (j + 1) * P], temp(2, s % 4),
                   start=(j == 0), stop=(j == NH - 1)).then_inc(S("C_dn"), 1)
            for c in range(B):
                pe.wait_ge(S("C_mo"), c + 1)
                to_tokens(chunk(12, c), c, bank[4 + c]).then_inc(S("C_mT"), 1)

            pe.wait_ge(S("C_out"), B)
            ln("ln6", htok_b)
            route("D", ED, rt[:, EB:])

            def tail_d():
                pe.wait_ge(S("D_down"), UNITS * B)
                pe.sem_inc(S("D_acc"), 1)
            moe("D", ED, [("D_g", 0, "D_a", 2), ("D_u", 1, "D_sil", 1)], (halfsel_bf, "D_us", 1), tail_d)
            finish("D")


_COLS = ["L0_attn_ln1_w", "L0_attn_ln1_b", "L0_attn_ln2_w", "L0_attn_ln2_b", "L0_attn_time_shift",
         "L0_attn_time_first", "L1_attn_ln1_g", "L1_attn_ln1_b", "L1_attn_ln2_g", "L1_attn_ln2_b", "L1_attn_b2"]


def kernel(**inputs):
    import numpy as np
    import concourse.bacc as bacc
    from concourse import mybir as _mybir
    from concourse.bass_utils import run_bass_kernel_spmd as run

    x = {n: np.asarray(a) for n, a in inputs.items()}
    f = np.float32

    cols = [x[n].reshape(P, 1) for n in _COLS] + [np.broadcast_to(x["L1_attn_alpha"].reshape(1, 1), (P, 1))]
    cols.append(x["L1_attn_b1"].reshape(HID // P, P).T)
    cols = np.ascontiguousarray(np.concatenate(cols, axis=1))
    eb = np.concatenate([np.concatenate([x[f"L0_ffn_{n}"], x[f"L0_ffn_s{n}"][None]]).reshape(UNITS, P, 2)
                         for n in ("b1", "b3")], axis=2)
    heads = np.broadcast_to(x["L1_attn_alpha_head"].reshape(HG, 1, 2, 1, 2, 1), (HG, B, 2, 2, 2, QT)).reshape(-1)
    rows = np.concatenate([x["L0_ffn_gate_b"], x["L1_ffn_router_bias"], heads])
    rows = np.ascontiguousarray(np.broadcast_to(rows, (P, rows.size)))
    pairmask = np.zeros((UNITS, P, 1), f)
    cst = np.zeros((P, 2 * P + ED), f)
    cst[:, 0:P] = np.eye(P, dtype=f)
    for e in range(ED):
        cst[e:SPLIT_ROWS:32, P + 64 * (e % 2):P + 64 * (e % 2) + 64] = 1
        pairmask[e // 2, e:SPLIT_ROWS:32] = 1
    cst[ED:SPLIT_ROWS:32, P:2 * P] = 1
    pairmask[UNITS - 1, ED:SPLIT_ROWS:32] = 1
    cst[:, 2 * P:2 * P + ED] = np.arange(ED, 0, -1, dtype=f)
    wcv = x["L0_attn_Wcv"].T.reshape(4, P, P).transpose(1, 0, 2).reshape(P, 4 * P)
    wa = np.concatenate([x["L0_attn_Wk"].T, x["L0_attn_Wv"].T, x["L0_attn_Wr"].T, x["L0_attn_Wcr"].T,
                         x["L0_attn_Wck"].T, wcv], axis=1)

    def split(w):
        return np.concatenate([w[..., 0::2, :], w[..., 1::2, :]], axis=-2).swapaxes(-1, -2)
    routed = np.concatenate([split(x["L0_ffn_w1"]), split(x["L0_ffn_w3"]), x["L0_ffn_w2"].swapaxes(-1, -2)], axis=-1)
    shared = np.concatenate([split(x["L0_ffn_sw1"]), split(x["L0_ffn_sw3"]), x["L0_ffn_sw2"].T], axis=-1)
    wb = np.concatenate([np.concatenate([routed, shared[None]], axis=0), eb], axis=2)
    b2 = np.concatenate([x["L0_ffn_b2"], x["L0_ffn_sb2"][None]], axis=0)
    rt = np.concatenate([x["L0_ffn_gate_w"].T, x["L1_ffn_router_w"].T], axis=1)
    wqkv = x["L1_attn_w_qkv"]
    wo = x["L1_attn_w_out"]
    cstc = np.zeros((P, P + HEADS + WIN + 1), f)
    for h in range(HEADS):
        cstc[DK * h:DK * h + DK, DK * h:DK * h + DK] = 1 / T
        cstc[DK * h:DK * h + DK, P + h] = 1
    cstc[:, P + HEADS:P + HEADS + WIN] = np.arange(WIN, dtype=f)
    cstc[:, P + HEADS + WIN] = 1
    wm1 = x["L1_attn_w1"]
    wm2 = x["L1_attn_w2"].reshape(HID // P, P, P).transpose(1, 0, 2).reshape(P, HID)

    def pairs(w):
        return w.reshape(8, 2, P, 64).transpose(0, 2, 1, 3).reshape(8, P, P)
    routed = np.concatenate([pairs(x["L1_ffn_gate_proj"]), pairs(x["L1_ffn_up_proj"]),
                             x["L1_ffn_down_proj"].reshape(8, P, P)], axis=-1)
    shared = np.concatenate([x["L1_ffn_sh_gate"].T, x["L1_ffn_sh_up"].T, x["L1_ffn_sh_down"].T], axis=-1)
    wd = np.concatenate([np.concatenate([routed, shared[None]], axis=0), pairmask], axis=2)
    xt = x["L0_attn_x"].reshape(B, QT, P, P).transpose(0, 2, 1, 3)

    nc = bacc.Bacc("TRN2", target_bir_lowering=False, num_devices=1)
    arrays, args = {}, []
    for name, a in (("x", xt), ("cols", cols), ("rows", rows), ("cst", cst), ("cstc", cstc),
                    ("wa", wa), ("wb", wb), ("b2", b2),
                    ("rt", rt), ("wqkv", wqkv), ("wo", wo), ("wm1", wm1), ("wm2", wm2), ("wd", wd)):
        a = np.ascontiguousarray(a)
        arrays[f"{name}_dram"] = a
        args.append(nc.dram_tensor(f"{name}_dram", a.shape, _mybir.dt.from_np(a.dtype), kind="ExternalInput").ap())
    args.append(nc.dram_tensor("qk_scratch", (2, PARTS, P, N), BF16, kind="Internal").ap())
    args.append(nc.dram_tensor("out_dram", (B, P, QT, P), F32, kind="ExternalOutput").ap())
    build(nc, *args)
    r = run(nc, [arrays], core_ids=[0])
    got = r.results[0]["out_dram"]
    return np.ascontiguousarray(got.transpose(0, 2, 1, 3).reshape(B, T, P))
```
